# Optimizing a Trainium2 kernel written in Bass

```python
import numpy as np
import jax
import jax.numpy as jnp

def _softmax(x, axis=-1):
    return jax.nn.softmax(x, axis=axis)

def _gelu(x):
    return jax.nn.gelu(x, approximate=True)

def _silu(x):
    return jax.nn.silu(x)

def _sigmoid(x):
    return jax.nn.sigmoid(x)

def _layernorm(x, axis=-1, eps=1e-05):
    m = jnp.mean(x, axis=axis, keepdims=True)
    v = jnp.var(x, axis=axis, keepdims=True)
    return (x - m) / jnp.sqrt(v + eps)

def _scatter_add(tgt, idx, src, axis=0):
    return tgt.at[idx].add(src)

def _segment_sum(src, seg, n):
    return jax.ops.segment_sum(src, seg, n)
kernel_name = 'mk_vit_tower_cls_d1_tok_img1024_r4_6bd7bc'

def setup_inputs(seed: int=0):
    np.random.seed(seed)
    _w = jnp.asarray

    def _rec_inputs():
        import jax
        import jax.numpy as jnp
        _rk = jax.random.key(seed)
        x = -0.00011082 + 0.999858 * jax.random.normal(jax.random.fold_in(_rk, 1), (8, 5, 128, 128), jnp.float32)
        cls_tok = 0.02 * jax.random.normal(jax.random.fold_in(_rk, 5), (1, 1, 256), jnp.float32)
        return (x, cls_tok)
    x, cls_tok = _rec_inputs()

    def _L0_tok_setup():
        import jax, jax.numpy as jnp
        import numpy as np
        PATCH = 8
        EPS = 1e-05

        def _patchify(x):
            B, C, H, Wd = x.shape
            p = PATCH
            x = x.reshape(B, C, H // p, p, Wd // p, p)
            x = x.transpose(0, 2, 4, 1, 3, 5)
            return x.reshape(B, H // p * (Wd // p), C * p * p)
        key = jax.random.key(seed)
        k1, k2 = jax.random.split(key)
        B, C, H, W_ = (32, 5, 128, 128)
        in_feat, embed_dim = (C * PATCH * PATCH, 256)
        x = jax.random.normal(k1, (B, C, H, W_), dtype=jnp.float32)
        W = jax.random.normal(k2, (in_feat, embed_dim), dtype=jnp.float32) * (1.0 / np.sqrt(in_feat))
        gamma = jnp.ones((embed_dim,), dtype=jnp.float32)
        return {'x': x, 'W': W, 'gamma': gamma}
    _L0_tok_all = _L0_tok_setup()
    _L0_tok_in = {k: v for k, v in _L0_tok_all.items() if k in ('W', 'gamma')}
    del _L0_tok_all

    def _L0_attn_setup():
        import jax, jax.numpy as jnp
        import numpy as np
        import math
        NUM_HEADS = 16

        def rotate_half(x):
            x1 = x[..., ::2]
            x2 = x[..., 1::2]
            return jnp.concatenate((-x2, x1), axis=-1)

        def rotary_tables(seq_len, head_dim, dtype):
            inv_freq = 1.0 / 10000.0 ** (jnp.arange(0, head_dim, 2, dtype=jnp.float32) / head_dim)
            t = jnp.arange(seq_len, dtype=jnp.float32)
            freqs = t[:, None] * inv_freq[None, :]
            emb = jnp.concatenate((freqs, freqs), axis=-1)
            cos = jnp.cos(emb)[None, None, :, :].astype(dtype)
            sin = jnp.sin(emb)[None, None, :, :].astype(dtype)
            return (cos, sin)
        key = jax.random.key(seed)
        k1, k2, k3, k4 = jax.random.split(key, 4)
        B, T, D = (2, 512, 256)
        scale = 1.0 / math.sqrt(D)
        x = jax.random.normal(k1, (B, T, D), dtype=jnp.float32)
        w_qkv = jax.random.normal(k2, (3 * D, D), dtype=jnp.float32) * scale
        w_out = jax.random.normal(k3, (D, D), dtype=jnp.float32) * scale
        b_out = jax.random.normal(k4, (D,), dtype=jnp.float32) * scale
        return {'x': x, 'w_qkv': w_qkv, 'w_out': w_out, 'b_out': b_out}
    _L0_attn_all = _L0_attn_setup()
    _L0_attn_in = {k: v for k, v in _L0_attn_all.items() if k in ('w_qkv', 'w_out', 'b_out')}
    del _L0_attn_all

    def _L0_ffn_setup():
        import jax, jax.numpy as jnp
        import numpy as np
        E = 8
        K = 2
        D = 256
        H = 4 * D
        EPS = 1e-05
        TEMP = 1.5
        key = jax.random.key(seed)
        ks = jax.random.split(key, 6)
        B, T = (2, 512)
        x = jax.random.normal(ks[0], (B, T, D), dtype=jnp.float32)
        gamma = jnp.ones((D,), dtype=jnp.float32)
        beta = jnp.zeros((D,), dtype=jnp.float32)
        router_w = jax.random.normal(ks[1], (E, D), dtype=jnp.float32) * 0.02
        W1 = jax.random.normal(ks[2], (E, D, H), dtype=jnp.float32) * 0.02
        W2 = jax.random.normal(ks[3], (E, H, D), dtype=jnp.float32) * 0.02
        return {'x': x, 'gamma': gamma, 'beta': beta, 'router_w': router_w, 'W1': W1, 'W2': W2}
    _L0_ffn_all = _L0_ffn_setup()
    _L0_ffn_in = {k: v for k, v in _L0_ffn_all.items() if k in ('gamma', 'beta', 'router_w', 'W1', 'W2')}
    del _L0_ffn_all
    return {'x': x, 'cls_tok': cls_tok, 'L0_tok_W': _L0_tok_in['W'], 'L0_tok_gamma': _L0_tok_in['gamma'], 'L0_attn_w_qkv': _L0_attn_in['w_qkv'], 'L0_attn_w_out': _L0_attn_in['w_out'], 'L0_attn_b_out': _L0_attn_in['b_out'], 'L0_ffn_gamma': _L0_ffn_in['gamma'], 'L0_ffn_beta': _L0_ffn_in['beta'], 'L0_ffn_router_w': _L0_ffn_in['router_w'], 'L0_ffn_W1': _L0_ffn_in['W1'], 'L0_ffn_W2': _L0_ffn_in['W2']}

def reference(x, cls_tok, L0_tok_W, L0_tok_gamma, L0_attn_w_qkv, L0_attn_w_out, L0_attn_b_out, L0_ffn_gamma, L0_ffn_beta, L0_ffn_router_w, L0_ffn_W1, L0_ffn_W2):
    import jax
    import jax.numpy as jnp

    def _L0_tok_ref(x, W, gamma):
        import jax, jax.numpy as jnp
        import numpy as np
        PATCH = 8
        EPS = 1e-05

        def _patchify(x):
            B, C, H, Wd = x.shape
            p = PATCH
            x = x.reshape(B, C, H // p, p, Wd // p, p)
            x = x.transpose(0, 2, 4, 1, 3, 5)
            return x.reshape(B, H // p * (Wd // p), C * p * p)
        tokens = _patchify(x)
        h = jnp.einsum('bnf,fd->bnd', tokens, W)
        mu = jnp.mean(h, axis=-1, keepdims=True)
        var = jnp.mean(jnp.square(h - mu), axis=-1, keepdims=True)
        out = (h - mu) * jax.lax.rsqrt(var + EPS) * gamma
        return out

    def _L0_attn_ref(x, w_qkv, w_out, b_out):
        import jax, jax.numpy as jnp
        import numpy as np
        import math
        NUM_HEADS = 16

        def rotate_half(x):
            x1 = x[..., ::2]
            x2 = x[..., 1::2]
            return jnp.concatenate((-x2, x1), axis=-1)

        def rotary_tables(seq_len, head_dim, dtype):
            inv_freq = 1.0 / 10000.0 ** (jnp.arange(0, head_dim, 2, dtype=jnp.float32) / head_dim)
            t = jnp.arange(seq_len, dtype=jnp.float32)
            freqs = t[:, None] * inv_freq[None, :]
            emb = jnp.concatenate((freqs, freqs), axis=-1)
            cos = jnp.cos(emb)[None, None, :, :].astype(dtype)
            sin = jnp.sin(emb)[None, None, :, :].astype(dtype)
            return (cos, sin)
        B, T, D = x.shape
        H = NUM_HEADS
        hd = D // H
        qkv = x @ w_qkv.T
        q, k, v = jnp.split(qkv, 3, axis=-1)

        def to_heads(a):
            return a.reshape(B, T, H, hd).transpose(0, 2, 1, 3)
        q, k, v = (to_heads(q), to_heads(k), to_heads(v))
        cos, sin = rotary_tables(T, hd, x.dtype)
        q = q * cos + rotate_half(q) * sin
        k = k * cos + rotate_half(k) * sin
        attn = jnp.einsum('bhqd,bhkd->bhqk', q, k) / math.sqrt(hd)
        attn = jax.nn.softmax(attn, axis=-1)
        out = jnp.einsum('bhqk,bhkd->bhqd', attn, v)
        out = out.transpose(0, 2, 1, 3).reshape(B, T, D)
        return out @ w_out.T + b_out

    def _L0_ffn_ref(x, gamma, beta, router_w, W1, W2):
        import jax, jax.numpy as jnp
        import numpy as np
        E = 8
        K = 2
        D = 256
        H = 4 * D
        EPS = 1e-05
        TEMP = 1.5
        res = x
        mu = jnp.mean(x, axis=-1, keepdims=True)
        var = jnp.mean(jnp.square(x - mu), axis=-1, keepdims=True)
        xn = (x - mu) * jax.lax.rsqrt(var + EPS) * gamma + beta
        logits = jnp.einsum('btd,ed->bte', xn, router_w)
        probs = jax.nn.softmax(logits / TEMP, axis=-1)
        w, idx = jax.lax.top_k(probs, K)
        wdense = jnp.sum(jax.nn.one_hot(idx, E, dtype=w.dtype) * w[..., None], axis=-2)
        h = jax.nn.silu(jnp.einsum('btd,edf->betf', xn, W1))
        y = jnp.einsum('betf,efd->betd', h, W2)
        out = jnp.einsum('bte,betd->btd', wdense, y)
        return out + res
    h = _L0_tok_ref(x, L0_tok_W, L0_tok_gamma)
    h = jnp.concatenate([jnp.broadcast_to(cls_tok, (h.shape[0], 1, h.shape[2])), h], axis=1)
    h = h + _L0_attn_ref(_layernorm(h, axis=-1), L0_attn_w_qkv, L0_attn_w_out, L0_attn_b_out)
    h = h + _L0_ffn_ref(_layernorm(h, axis=-1), L0_ffn_gamma, L0_ffn_beta, L0_ffn_router_w, L0_ffn_W1, L0_ffn_W2)
    return h

_drawn_inputs = setup_inputs


def setup_inputs(seed=0):
    import zlib

    import numpy as np

    out = dict(_drawn_inputs(seed))
    spreads = {'L0_tok_gamma': (1.0, 0.2), 'L0_ffn_gamma': (1.0, 0.6), 'L0_ffn_beta': (0.0, 0.8)}
    factors = {'L0_ffn_router_w': 5.155, 'L0_ffn_W1': 4.355, 'L0_ffn_W2': 4.301}
    for name, (base, spread) in spreads.items():
        noise = np.random.default_rng([zlib.crc32(name.encode()), seed]).standard_normal(out[name].shape)
        drawn = base * np.exp(spread * noise) if base else spread * noise
        out[name] = jnp.asarray(drawn.astype(out[name].dtype))
    for name, factor in factors.items():
        out[name] = (out[name] * factor).astype(out[name].dtype)
    return out
```

```python
from contextlib import ExitStack

import concourse.bass as bass
import numpy as np
from concourse import mybir

F32 = mybir.dt.float32
BF16 = mybir.dt.bfloat16
I32 = mybir.dt.int32
ALU = mybir.AluOpType
ACT = mybir.ActivationFunctionType
AX = mybir.AxisListType

P = 128
B, C, IMG = 8, 5, 128
PATCH = 8
GRID = IMG // PATCH
D = 256
NTOK = GRID * GRID + 1
ROWS = B * NTOK
HEADS, HD = 16, 16
E, F = 8, 1024
KC = D // P
FT = 107
NFEAT = C * PATCH * PATCH
CUT = [0, FT, NFEAT - FT]
TT = NTOK + 1
KT = TT // 3
BANK = 512
TILES = GRID
GROUPS, GT = 4, 4
EPS = 1e-5
TEMP = 1.5
SLOTS = (2 * ROWS + E * (P - 1)) // P
QPART = [0, 0, 1, 1, 0, 2]
KPART = [0, 1, 0, 1, 2, 0]
SPLIT = HD * len(QPART)
MROWS = 3
LEAD = 8
INIT = 9
PRE = 2
LOADS = 2 * len(QPART)

T_VM, T_DUMMY, T_IDHI, T_IDLO, T_VALID, T_INV, T_DESC, T_J128, T_I128, T_I40, T_RESET = (
    0, 1, 2, 19, 36, 53, 70, 78, 95, 223, 263)
T_END = T_RESET + E * 17


def shape_tables():
    inv = (1.0 / 10000.0 ** (np.arange(0, HD, 2, dtype=np.float32) / np.float32(HD))).astype(np.float32)
    pos = np.minimum(np.arange(TT), NTOK - 1).astype(np.float32)
    ang = (inv[:, None] * pos[None, :]).astype(np.float32)
    lane = np.arange(P) % HD
    cos = np.cos(ang)[lane % (HD // 2)].astype(np.float32)
    sign = np.where(lane < HD // 2, -1.0, 1.0).astype(np.float32)
    sin = (np.sin(ang)[lane % (HD // 2)] * sign[:, None]).astype(np.float32)
    eye = np.eye(P, dtype=np.float32)
    tri = np.triu(np.ones((P, P), np.float32), 1)
    tab = np.zeros((P, T_END), np.float32)
    p = np.arange(P)
    tab[:, T_VM] = p != KT - 1
    tab[:, T_DUMMY] = ROWS + p
    tab[:, T_IDHI:T_IDHI + 17] = np.arange(17)
    tab[:, T_IDLO:T_IDLO + 17] = p[:, None]
    valid = np.ones((P, 17), np.float32)
    valid[B:, 16] = 0
    tab[:, T_VALID:T_VALID + 17] = valid
    tab[:, T_INV:T_INV + 17] = (1 - valid) * 8192
    tab[:, T_DESC:T_DESC + E] = E - np.arange(E)
    tab[:, T_J128:T_J128 + 17] = np.arange(17) * P
    tab[:, T_I128:T_I128 + P] = np.arange(P)
    tab[:, T_I40:T_I40 + SLOTS] = np.arange(SLOTS)
    tab[:, T_RESET:T_END] = np.tile(np.arange(17) != 0, E)
    return cos, sin, eye, tri, tab


class Steps:

    def __init__(self, eng, sem, apart=None):
        self.eng, self.sem, self.n, self.turn, self.apart = eng, sem, 0, 0, apart

    def done(self, ins, apart=None):
        ins.then_inc(self.sem, 1)
        self.n += 1
        wait(self.eng, self.sem, self.turn + self.n, apart or self.apart)

    def enter(self, turn, per):
        self.turn, self.start, self.per = turn * per, self.n, per

    def leave(self, turns):
        assert self.n - self.start == self.per, (self.n, self.start, self.per)
        self.n, self.turn = self.start + self.per * turns, 0


def wait(eng, sem, value, apart=None):
    if not isinstance(value, int) or value > 0:
        eng.wait_ge(sem, value)
        if apart is not None and not isinstance(value, int):
            eng.sem_inc(apart, 1)


def vit_block(nc, x, cls_tok, tok_w, tok_gamma, w_qkv, w_out, b_out, f_gamma, f_beta, router_w, w1, w2,
              cos_in, sin_in, eye_in, tri_in, tab_in, out):
    ctx = ExitStack()
    base = [(nc.sbuf_base + 63) // 64 * 64]

    def at(name, shape, dt, offset):
        return nc.alloc_sbuf_tensor_at(name, shape, dt, offset=offset)

    def size(shape, dt):
        n = 1
        for s in shape[1:]:
            n *= s
        return (n * (2 if dt == BF16 else 4) + 31) // 32 * 32

    class Region:

        def __init__(self, start):
            self.end = start

        def add(self, name, shape, dt=F32):
            t = at(name, shape, dt, self.end)
            self.end += size(shape, dt)
            return t

    with ctx:
        keep = Region(base[0])
        h_tok = keep.add("h_tok", [P, 17, D])
        eye = keep.add("eye", [P, P])
        eyeb = keep.add("eyeb", [P, P], BF16)
        trib = keep.add("trib", [P, P], BF16)
        onesb = keep.add("onesb", [P, P], BF16)
        tab = keep.add("tab", [P, T_END])
        gam_t = keep.add("gam_t", [P, D])
        bout = keep.add("bout", [P, D])
        gam_f = keep.add("gam_f", [P, D])
        bet_f = keep.add("bet_f", [P, D])
        r_t = keep.add("r_t", [P, KC, E])
        mv1 = keep.add("mv1", [P, 17, 2])
        mv2 = keep.add("mv2", [P, 17, 2])
        rs1 = keep.add("rs1", [P, 17])
        rs2 = keep.add("rs2", [P, 17])
        mhalf = keep.add("mhalf", [P, 17])
        bst = keep.add("bst", [P, 2, 6])
        bag = keep.add("bag", [P, 2, 2])
        wo_t = keep.add("wo_t", [P, 4, D])
        lwt = keep.add("lwt", [P, SLOTS])
        gid = keep.add("gid", [P, SLOTS], I32)
        sid = keep.add("sid", [P, SLOTS], I32)
        eid = keep.add("eid", [1, SLOTS], I32)
        lgt = keep.add("lgt", [P, 17, E])
        g_idx = keep.add("g_idx", [P, 2, 1], I32)
        s_idx = keep.add("s_idx", [P, 2, 1], I32)
        ph = Region(keep.end)
        pt = ph.add("pt", [P, 2, 3 * TT])
        wqkv_t = ph.add("wqkv_t", [P, KC, 3 * D])
        cos = ph.add("cos", [P, TT])
        sin = ph.add("sin", [P, TT])
        st = Region(keep.end)
        oa = st.add("oa", [P, 2, 4, P])
        xn = st.add("xn", [P, 2, D])
        xnt = st.add("xnt", [P, 2, KC, P])
        ut = st.add("ut", [P, 2, D])
        assert st.end <= ph.end
        at_start = ph.end
        ao = Region(at_start)
        attn_t = ao.add("attn_t", [P, 4, B * TT])
        su = Region(at_start)
        wq_raw = su.add("wq_raw", [P, 6, D])
        wo_in = su.add("wo_in", [P, KC, D])
        wo_raw = su.add("wo_raw", [P, KC, 4, 4, 32])
        r_raw = su.add("r_raw", [E, D])
        tri_f = su.add("tri_f", [P, P])
        wt = su.add("wt", [FT, 3, D])
        xs = su.add("xs", [P, 2, NFEAT])
        xt = su.add("xt", [FT, 2, 3, P])
        zs = su.add("zs", [P, 2, D])
        assert su.end <= ao.end
        ro = Region(at_start)
        sel = [ro.add(f"sel{k}", [P, 17, E]) for k in range(2)]
        prob = ro.add("prob", [P, 17, E])
        tmp8 = ro.add("tmp8", [P, 17, E])
        col = [ro.add(f"col{k}", [P, 17]) for k in range(3)]
        topw = ro.add("topw", [P, 2, 17])
        mask = ro.add("mask", [P, 17, E], BF16)
        tot = ro.add("tot", [P, E, 17])
        cum = ro.add("cum", [P, E, 17])
        posn = ro.add("posn", [P, 17, E])
        ntl = ro.add("ntl", [P, 3, E])
        big17 = ro.add("big17", [P, E, 17])
        pos2 = ro.add("pos2", [P, 2, 17])
        posi = ro.add("posi", [P, 2, 17], I32)
        poa = ro.add("poa", [P, 2, 17], I32)
        pop = ro.add("pop", [P, 2, 17], I32)
        poaf = ro.add("poaf", [P, 34])
        popf = ro.add("popf", [P, 34])
        wres = ro.add("wres", [P, 34])
        wpart = ro.add("wpart", [P, 3, 34], BF16)
        vals = ro.add("vals", [P, 34, 6, SLOTS], BF16)
        lst = ro.add("lst", [P, 6, SLOTS])
        ecmp = ro.add("ecmp", [1, SLOTS, E])
        esum = ro.add("esum", [1, SLOTS])
        assert ro.end <= ao.end, (ro.end, ao.end)
        ro2 = Region(keep.end)
        ohp = ro2.add("ohp", [P, 34, P], BF16)
        assert ro2.end <= ph.end
        fx = Region(at_start)
        xg = fx.add("xg", [P, 2, D])
        xgt = fx.add("xgt", [P, 2, KC, P])
        hb = fx.add("hb", [P, 2, F])
        ht = fx.add("ht", [P, 2, F // P, P])
        yb = fx.add("yb", [P, 2, D])
        assert fx.end <= ao.end
        E_EARLY = 6
        wr = Region(ao.end)
        w1_sb = wr.add("w1_sb", [P, E, KC, F])
        late = wr.end - (E - E_EARLY) * KC * F * 4
        w2_sb = wr.add("w2_sb", [P, E, F // P, D])
        assert wr.end <= nc.sbuf_usable_end, (wr.end, nc.sbuf_usable_end)
        ov = Region(late)
        zt = ov.add("zt", [P, KC, B * TT])
        x_at = ov.end
        qs = ov.add("qs", [P, 2, HEADS, TT], BF16)
        parts = ov.add("parts", [P, 3, 4, TT], BF16)
        xin = at("xin", [P, C * PATCH, GRID, PATCH], F32, x_at)
        assert x_at + size([P, C * PATCH, GRID, PATCH], F32) <= ov.end
        ks = ov.add("ks", [P, 2, HEADS, TT], BF16)
        vv = ov.add("vv", [KT, 2, 3, HEADS, 32])
        zb = ov.add("zb", [P, KC, TT])
        rot1 = ov.add("rot1", [P, 4, TT])
        rot2 = ov.add("rot2", [P, 4, TT])
        rec = ov.add("rec", [P, TT])
        shf = ov.add("shf", [P, TT])
        mx = ov.add("mx", [KT, 2, 3, 4])
        mneg = ov.add("mneg", [KT, 2, 3, 4])
        mres = ov.add("mres", [KT, 3, 4])
        mpt = ov.add("mpt", [KT, 2, 3, 3, 4], BF16)
        mtb = ov.add("mtb", [12, 2, TT], BF16)
        assert ov.end <= nc.sbuf_usable_end

        s_ps = ctx.enter_context(nc.psum_tensor("s_ps", [P, 2 * BANK], F32))
        st_ps = [ctx.enter_context(nc.psum_tensor(f"st_ps{i}", [P, 2 * BANK], F32)) for i in range(2)]
        o_ps = ctx.enter_context(nc.psum_tensor("o_ps", [P, BANK], F32))
        m_ps = ctx.enter_context(nc.psum_tensor("m_ps", [P, BANK], F32))
        bank = [s_ps[:, 0:BANK], s_ps[:, BANK:], st_ps[0][:, 0:BANK], st_ps[0][:, BANK:],
                st_ps[1][:, 0:BANK], st_ps[1][:, BANK:], o_ps[:, :], m_ps[:, :]]

        split_rows = nc.dram_tensor("split_rows", [3, 4, P, TT], BF16).ap()
        xn_rows = nc.dram_tensor("xn_rows", [ROWS, D], F32).ap()
        acc_rows = nc.dram_tensor("acc_rows", [ROWS + P, D], F32).ap()

        def sem(name):
            return ctx.enter_context(nc.semaphore(name))

        sp_passed, pool_passed, dve_passed = sem("sp_passed"), sem("pool_passed"), sem("dve_passed")
        tok_in = sem("tok_in")
        raw_in = sem("raw_in")
        small_in = sem("small_in")
        w_early_in = sem("w_early_in")
        w_late_in = sem("w_late_in")
        pool_step, dve_step, act_step = sem("pool_step"), sem("dve_step"), sem("act_step")
        setup_ready = sem("setup_ready")
        setup_read = sem("setup_read")
        raw_ready = sem("raw_ready")
        init_done = sem("init_done")
        xs_ready, tok_turned, xt_ready, tok_proj, h_raw = (
            sem("xs_ready"), sem("tok_turned"), sem("xt_ready"), sem("tok_proj"), sem("h_raw"))
        stats1, stats2, rstd1, rstd2 = sem("stats1"), sem("stats2"), sem("rstd1"), sem("rstd2")
        z_ready, z_turned, zt_written = sem("z_ready"), sem("z_turned"), sem("zt_written")
        zt_done = sem("zt_done")
        proj_ready, rot_in, x_ready, p1_ready, r_ready, p2_ready, rot_done = (
            sem("proj_ready"), sem("rot_in"), sem("x_ready"), sem("p1_ready"), sem("r_ready"),
            sem("p2_ready"), sem("rot_done"))
        split_out, stack_in = sem("split_out"), sem("stack_in")
        zb_ready, v_ready, v_written = sem("zb_ready"), sem("v_ready"), sem("v_written")
        s_ready, s_read, mp_ready, mt_ready, mt_copied = (
            sem("s_ready"), sem("s_read"), sem("mp_ready"), sem("mt_ready"), sem("mt_copied"))
        mrow_in = [sem(f"mrow_in{g}") for g in range(4)]
        st_ready, exp_done, pv_done, norm_done = sem("st_ready"), sem("exp_done"), sem("pv_done"), sem("norm_done")
        bias_added = sem("bias_added")
        oa_ready, op_ready, h1_ready, oa_used = sem("oa_ready"), sem("op_ready"), sem("h1_ready"), None
        stats3, stats4, rstd3, rstd4 = sem("stats3"), sem("stats4"), sem("rstd3"), sem("rstd4")
        base_ready, xn_ready, xn_turned, xnt_ready, lg_ready, lg_read = (
            sem("base_ready"), sem("xn_ready"), sem("xn_turned"), sem("xnt_ready"), sem("lg_ready"), sem("lg_read"))
        xn_out, acc_out = [sem("xn_out0"), sem("xn_out1")], sem("acc_out")
        ro_d, ex_ready, mask_ready, rank_ready, oh_ready, wp_ready, wv_ready, list_ready, route_done = (
            sem("ro_d"), sem("ex_ready"), sem("mask_ready"), sem("rank_ready"), sem("oh_ready"),
            sem("wp_ready"), sem("wv_ready"), sem("list_ready"), sem("route_done"))
        xg_in = [sem("xg_in0"), sem("xg_in1")]
        x_turned, xgt_ready, g1_ready, silu_done, t_ready, ht_ready, g2_ready, y_ready, y_added = (
            sem("x_turned"), sem("xgt_ready"), sem("g1_ready"), sem("silu_done"), sem("t_ready"),
            sem("ht_ready"), sem("g2_ready"), sem("y_ready"), sem("y_added"))
        out_done = sem("out_done")

        TOK_DMAS = 8 + 3 + 3
        RAW_DMAS = 4
        SMALL_DMAS = 6
        zt_b = zt[:, :, :].rearrange("p k (b t) -> p k b t", t=TT)
        zt_grid = zt_b[:, :, :, 1:NTOK].rearrange("p k b (h w) -> p k b h w", w=GRID)
        at_b = attn_t[:, :, :].rearrange("p g (b t) -> p g b t", t=TT)
        at_grid = at_b[:, :, :, 1:NTOK].rearrange("p g b (h w) -> p g b h w", w=GRID)

        def has_s_kind(kind, j):
            return kind != "first" if j < LEAD else kind != "last"

        def s_of(b, j):
            return (b, j + LEAD) if j < LEAD else (b + 1, j - LEAD)

        def misc_uses(b, kind):
            uses = []
            if kind != "first":
                uses += [(1, "mt", b, 1), (5, "mt", b, 2), (9, "mt", b, 3)]
            if kind in ("first", "loop"):
                uses += [(4, "p", b + 2, 0), (6, "p", b + 2, 1), (8, "p", b + 2, 2), (10, "p", b + 2, 3)]
            if kind != "last":
                uses += [(12, "v", b + 1, 0), (13, "mt", b + 1, 0), (13.5, "v", b + 1, 1), (14, "v", b + 1, 2)]
            return sorted(uses, key=lambda u: u[0])

        def read_of(use):
            _, what, b, n = use
            s, per = {"p": (rot_in, 4), "v": (v_written, 3), "mt": (mt_copied, 4)}[what]
            return s, b * per + n + 1

        def before(b, kind):
            if kind == "first":
                return (0, "p", 0, 3)
            return (14, "v", b, 2)

        TURNS = [(-1, "first"), (None, "loop"), (B - 2, "short"), (B - 1, "last")]

        def all_turns(eng, body):
            body(-1, 1, "first")
            with eng.Fori(0, (B - 2) // 2, 1) as i:
                for par in range(2):
                    body(2 * i + par, par, "loop")
            body(B - 2, 0, "short")
            body(B - 1, 1, "last")

        def tile_pairs(eng, t0, t1, body):
            if t0 < 2:
                body(t0, t0 % 2)
                body(t0 + 1, (t0 + 1) % 2)
                t0 += 2
            if t0 < t1:
                with eng.Fori(0, (t1 - t0) // 2, 1) as i:
                    body(2 * i + t0, t0 % 2)
                    body(2 * i + (t0 + 1), (t0 + 1) % 2)

        block = ctx.enter_context(nc.Block())

        @block.sync
        def _(sp):
            for b in range(B):
                sp.dma_start(xin[b * GRID:(b + 1) * GRID, :, :, :].rearrange("p (c r) w q -> p c (r w q)", c=C),
                             x[b].rearrange("c (h r) w -> h c (r w)", r=PATCH)).then_inc(tok_in, 16)
            sp.dma_start(wt[:, 0, :], tok_w[0:FT, :]).then_inc(tok_in, 16)
            sp.dma_start(wt[:, 1, :], tok_w[FT:2 * FT, :]).then_inc(tok_in, 16)
            sp.wait_ge(init_done, 1)
            sp.dma_start(wt[1:FT, 2, :], tok_w[2 * FT:NFEAT, :]).then_inc(tok_in, 16)
            w1_v = w1.rearrange("e (k p) f -> p e k f", p=P)
            w2_v = w2.rearrange("e (k p) d -> p e k d", p=P)
            for e in range(E_EARLY):
                sp.dma_start(w1_sb[:, e, :, :], w1_v[:, e, :, :]).then_inc(w_early_in, 16)

            def store_split(bb):
                wait(sp, rot_done, 4 * (bb + 1), apart=sp_passed)
                wait(sp, stack_in, 16 * LOADS * bb)
                sp.dma_start(split_rows.rearrange("r c p t -> p r c t"), parts[:, :, :, :]).then_inc(split_out, 16)

            def load_stack(bb, par, cold):
                wait(sp, split_out, 16 * (bb + 1), apart=sp_passed)
                if not cold:
                    wait(sp, st_ready, HEADS * (bb - 1) + 1)
                    wait(sp, s_ready, HEADS * (bb - 1) + 1)
                for dst, c0, pick in ((qs, 0, QPART), (ks, 2, KPART)):
                    src = split_rows[:, c0:c0 + 2, :, :].rearrange("r c (h i) t -> r i (c h) t", i=HD)
                    for r, part in enumerate(pick):
                        sp.dma_start(dst[r * HD:(r + 1) * HD, par, :, :], src[part]).then_inc(stack_in, 16)

            def max_rows(bb, par, g):
                wait(sp, mt_copied, 4 * bb + g + 1)
                for r in range(MROWS):
                    sp.dma_start(qs[SPLIT + r:SPLIT + r + 1, par, 4 * g:4 * g + 4, :],
                                 mtb[4 * r:4 * r + 4, g % 2, :]).then_inc(mrow_in[g], 16)

            def turn(b, par, kind):
                if kind != "first":
                    max_rows(b, par, 1)
                    if kind != "last":
                        load_stack(b + 1, 1 - par, False)
                    max_rows(b, par, 2)
                    max_rows(b, par, 3)
                if kind != "last":
                    max_rows(b + 1, 1 - par, 0)
                if kind in ("first", "loop"):
                    store_split(b + 2)

            store_split(0)
            load_stack(0, 0, True)
            all_turns(sp, turn)

            sp.wait_ge(norm_done, PRE + 4 * B)
            sp.wait_ge(proj_ready, 4 * B)
            for e in range(E_EARLY, E):
                sp.dma_start(w1_sb[:, e, :, :], w1_v[:, e, :, :]).then_inc(w_late_in, 16)
            for e in range(E):
                sp.dma_start(w2_sb[:, e, :, :], w2_v[:, e, :, :]).then_inc(w_late_in, 16)

            sp.wait_ge(y_added, 16 * SLOTS)
            acc_b = acc_rows[0:TILES * P].rearrange("(w b h) d -> b h w d", w=GRID, b=B)
            for b in range(B):
                sp.dma_start(out[b, 1:NTOK, :].rearrange("(h w) d -> h w d", w=GRID), acc_b[b]).then_inc(out_done, 16)
            sp.dma_start(out[:, 0, :], acc_rows[TILES * P:ROWS, :]).then_inc(out_done, 16)
            sp.wait_ge(out_done, 16 * (B + 1))

        @block.gpsimd
        def _(pool):
            step = Steps(pool, pool_step, apart=pool_passed)
            pool.memset(wt[:, 2, :], 0.0).then_inc(init_done, 1)
            for n, (ap, value) in enumerate(((mv1[:, :, :], 1.0), (mv2[:, :, :], 1.0), (mhalf[:, :], -0.5),
                                             (onesb[:, :], 1.0), (ks[SPLIT:SPLIT + MROWS, :, :, :], 1.0),
                                             (vv[:, :, :, :, HD:32], 1.0), (lgt[:, :, :], 0.0))):
                pool.wait_ge(init_done, n + 1)
                pool.memset(ap, value).then_inc(init_done, 1)
            pool.wait_ge(init_done, INIT - 1)
            pool.wait_ge(small_in, 16 * SMALL_DMAS)
            pool.tensor_scalar(vv[:, :, 2, :, HD:32], vv[:, :, 2, :, HD:32], tab[0:KT, T_VM:T_VM + 1], None,
                               ALU.mult).then_inc(init_done, 1)

            def rstd(mv, rs, t0, t1, p, ready):
                step.done(pool.tensor_scalar(rs[0:p, t0:t1], mv[0:p, t0:t1, 1], EPS, None, ALU.add))
                pool.tensor_tensor(out=rs[0:p, t0:t1], in0=rs[0:p, t0:t1], in1=mhalf[0:p, t0:t1],
                                   op=ALU.pow).then_inc(ready, 1)

            for g in range(GROUPS):
                pool.wait_ge(stats1, GT * (g + 1))
                rstd(mv1, rs1, GT * g, GT * (g + 1), P, rstd1)
                if g > 0:
                    pool.wait_ge(stats2, GT * g)
                    rstd(mv2, rs2, GT * (g - 1), GT * g, P, rstd2)
            pool.wait_ge(stats2, GT * GROUPS + 1)
            rstd(mv2, rs2, GT * (GROUPS - 1), GT * GROUPS + 1, P, rstd2)

            def turn_rot(bb, c):
                wait(pool, rot_in, 4 * bb + c + 1)
                s = c
                step.done(pool.tensor_tensor(out=rot2[:, s, :], in0=rot2[:, s, :], in1=sin[:, :], op=ALU.mult))
                pool.tensor_tensor(out=rot1[:, s, :], in0=rot1[:, s, :], in1=rot2[:, s, :],
                                   op=ALU.add).then_inc(x_ready, 1)

            def rest1(bb, c):
                wait(pool, p1_ready, 4 * bb + c + 1)
                wait(pool, x_ready, 4 * bb + c + 1)
                s = c
                pool.tensor_tensor(out=rot2[:, s, :], in0=rot1[:, s, :], in1=parts[:, 0, c, :],
                                   op=ALU.subtract).then_inc(r_ready, 1)

            def rest2(bb, c):
                wait(pool, p2_ready, 4 * bb + c + 1)
                s = c
                pool.tensor_tensor(out=parts[:, 2, c, :], in0=rot2[:, s, :], in1=parts[:, 1, c, :],
                                   op=ALU.subtract).then_inc(rot_done, 1)

            def max_parts(bb, g):
                s = g % 2
                wait(pool, s_read, HEADS * bb + 4 * g + 4, apart=pool_passed)
                wait(pool, mt_ready, 4 * bb + g - 1, apart=pool_passed)
                step.done(pool.tensor_scalar(mneg[:, s, :, :], mx[:, s, :, :], -1.0, None, ALU.mult))
                step.done(pool.tensor_copy(mpt[:, s, :, 0, :], mneg[:, s, :, :]))
                step.done(pool.tensor_tensor(out=mres[:, :, :], in0=mneg[:, s, :, :], in1=mpt[:, s, :, 0, :], op=ALU.subtract))
                step.done(pool.tensor_copy(mpt[:, s, :, 1, :], mres[:, :, :]))
                pool.tensor_tensor(out=mpt[:, s, :, 2, :], in0=mres[:, :, :], in1=mpt[:, s, :, 1, :],
                                   op=ALU.subtract).then_inc(mp_ready, 1)

            def copy_z(bb):
                wait(pool, v_ready, 3 * bb, apart=pool_passed)
                pool.tensor_copy(zb[:, :, :], zt_b[:, :, bb, :]).then_inc(zb_ready, 1)

            PER_TURN = 4 + 4 * 4

            def turn(b, par, kind):
                if kind != "first":
                    max_parts(b, 2)
                mids = kind in ("first", "loop")
                if mids:
                    turn_rot(b + 2, 0)
                    turn_rot(b + 2, 1)
                    rest1(b + 2, 0)
                if kind != "first":
                    max_parts(b, 3)
                if mids:
                    rest2(b + 2, 0)
                    turn_rot(b + 2, 2)
                    rest1(b + 2, 1)
                if kind != "last":
                    copy_z(b + 1)
                if mids:
                    rest2(b + 2, 1)
                    turn_rot(b + 2, 3)
                    rest1(b + 2, 2)
                if kind != "last":
                    max_parts(b + 1, 0)
                if mids:
                    rest2(b + 2, 2)
                    rest1(b + 2, 3)
                    rest2(b + 2, 3)
                if kind != "last":
                    max_parts(b + 1, 1)
                if kind == "first":
                    pool.tensor_tensor(out=h_tok[:, 0:TILES, :], in0=h_tok[:, 0:TILES, :],
                                       in1=bout[:, :].unsqueeze(1).to_broadcast([P, TILES, D]),
                                       op=ALU.add).then_inc(bias_added, 1)
                    pool.tensor_tensor(out=h_tok[0:B, 16, :], in0=h_tok[0:B, 16, :], in1=bout[0:B, :],
                                       op=ALU.add).then_inc(bias_added, 1)

            pool.wait_ge(zt_done, 1)
            turn_rot(0, 0)
            turn_rot(0, 1)
            rest1(0, 0)
            rest2(0, 0)
            turn_rot(0, 2)
            rest1(0, 1)
            rest2(0, 1)
            turn_rot(0, 3)
            rest1(0, 2)
            rest2(0, 2)
            rest1(0, 3)
            rest2(0, 3)
            turn(-1, 1, "first")
            with pool.Fori(0, (B - 2) // 2, 1) as i:
                step.enter(i, 2 * PER_TURN)
                for par in range(2):
                    turn(2 * i + par, par, "loop")
                step.leave((B - 2) // 2)
            turn(B - 2, 0, "short")
            turn(B - 1, 1, "last")

            for g in range(GROUPS):
                t1 = GT * (g + 1) + (g == GROUPS - 1)
                pool.wait_ge(stats3, t1)
                rstd(mv1, rs1, GT * g, t1, P, rstd3)
                if g > 0:
                    pool.wait_ge(stats4, GT * g)
                    rstd(mv2, rs2, GT * (g - 1), GT * g, P, rstd4)
            pool.wait_ge(stats4, TILES + 1)
            rstd(mv2, rs2, GT * (GROUPS - 1), TILES + 1, P, rstd4)

            pool.wait_ge(wp_ready, 1)
            for n in (1, 2):
                pool.tensor_tensor(out=vals[:, :, 3 + n, :], in0=vals[:, :, 2, :],
                                   in1=wpart[:, n, :].unsqueeze(2).to_broadcast([P, 34, SLOTS]),
                                   op=ALU.mult).then_inc(wv_ready, 1)

            pool.wait_ge(route_done, 1)
            pool.wait_ge(xn_out[0], 16 * 9)
            pool.wait_ge(xn_out[1], 16 * 8)
            pool.wait_ge(acc_out, 16 * 3)

            def gather(t, par):
                wait(pool, x_turned, t - 1)
                wait(pool, xg_in[par], 8 * (t - par), apart=pool_passed)
                step.done(pool.tensor_copy(g_idx[:, par, :], gid[:, bass.ds(t, 1)]))
                pool.indirect_dma_start(xg[:, par, :], None, xn_rows[:, :],
                                        bass.IndirectOffsetOnAxis(g_idx[:, par, :], 0)).then_inc(xg_in[par], 16)

            def scatter(t, par):
                wait(pool, y_added, 16 * t, apart=pool_passed)
                step.done(pool.tensor_copy(s_idx[:, par, :], sid[:, bass.ds(t, 1)]))
                wait(pool, y_ready, t + 1, apart=pool_passed)
                pool.indirect_dma_start(acc_rows[:, :], bass.IndirectOffsetOnAxis(s_idx[:, par, :], 0),
                                        yb[:, par, :], None, compute_op=ALU.add).then_inc(y_added, 16)

            gather(0, 0)
            gather(1, 1)
            for t in range(2):
                gather(t + 2, t)
                scatter(t, t)
            with pool.Fori(0, (SLOTS - 4) // 2, 1) as i:
                step.enter(i, 4)
                for par in range(2):
                    gather(2 * i + par + 4, par)
                    scatter(2 * i + par + 2, par)
                step.leave((SLOTS - 4) // 2)
            scatter(SLOTS - 2, 0)
            scatter(SLOTS - 1, 1)

        @block.scalar
        def _(act):
            act.dma_start(eye[:, :], eye_in).then_inc(tok_in, 16)
            act.dma_start(gam_t[:, :], tok_gamma.unsqueeze(0).to_broadcast([P, D])).then_inc(tok_in, 16)
            act.dma_start(h_tok[0:B, 16, :], cls_tok[0].to_broadcast([B, D])).then_inc(tok_in, 16)
            act.dma_start(wq_raw[:, :, :], w_qkv.rearrange("(o p) i -> p o i", p=P)).then_inc(raw_in, 16)
            act.dma_start(wo_in[:, :, :], w_out.rearrange("(o p) i -> p o i", p=P)).then_inc(raw_in, 16)
            act.dma_start(r_raw[:, :], router_w).then_inc(raw_in, 16)
            act.dma_start(tri_f[:, :], tri_in).then_inc(raw_in, 16)
            act.dma_start(tab[:, :], tab_in).then_inc(small_in, 16)
            act.dma_start(cos[:, :], cos_in).then_inc(small_in, 16)
            act.dma_start(sin[:, :], sin_in).then_inc(small_in, 16)
            for dst, src in ((bout, b_out), (gam_f, f_gamma), (bet_f, f_beta)):
                act.dma_start(dst[:, :], src.unsqueeze(0).to_broadcast([P, D])).then_inc(small_in, 16)

            def copy_x(w, par):
                wait(act, tok_turned, w - 1)
                act.activation(xs[:, par, :].rearrange("p (r q) -> p r q", q=PATCH), xin[:, :, w, :],
                               ACT.Copy).then_inc(xs_ready, 1)

            def copy_h(w, par):
                wait(act, tok_proj, w + 1)
                act.activation(h_tok[:, w, :], bank[2 + par][:, 0:D], ACT.Copy).then_inc(h_raw, 1)

            def copy_zt(w, par):
                wait(act, z_turned, w + 1)
                src = bank[4 + par][:, 0:D].rearrange("p (k b h) -> p k b h", k=KC, b=B)
                for k in range(KC):
                    last = act.activation(zt_grid[:, k, :, :, w], src[:, k, :, :], ACT.Copy)
                last.then_inc(zt_written, 1)

            act.wait_ge(tok_in, 16 * TOK_DMAS)
            copy_x(0, 0)
            copy_x(1, 1)
            for g in range(GROUPS):
                if g < GROUPS - 1:
                    tile_pairs(act, GT * g, GT * (g + 1), lambda w, par: (copy_h(w, par), copy_x(w + 2, par)))
                else:
                    for w in range(GT * g, GT * (g + 1)):
                        copy_h(w, w % 2)
                        if w + 2 < TILES:
                            copy_x(w + 2, w % 2)
                if g >= 2:
                    tile_pairs(act, GT * (g - 2), GT * (g - 1), copy_zt)
            tile_pairs(act, GT * 2, GT * 4, copy_zt)
            act.wait_ge(z_turned, TILES + 1)
            src = bank[4][:, 0:KC * B].rearrange("p (k b) -> p k b", k=KC)
            act.activation(zt_b[:, :, :, 0], src, ACT.Copy).then_inc(zt_written, 1)

            def part1(bb, c):
                wait(act, x_ready, 4 * bb + c + 1)
                if c == 0:
                    wait(act, split_out, 16 * bb)
                act.activation(parts[:, 0, c, :], rot1[:, c, :], ACT.Copy).then_inc(p1_ready, 1)

            def part2(bb, c):
                wait(act, r_ready, 4 * bb + c + 1)
                act.activation(parts[:, 1, c, :], rot2[:, c, :], ACT.Copy).then_inc(p2_ready, 1)

            def copy_v(bb, par, t):
                wait(act, v_ready, 3 * bb + t + 1)
                wait(act, pv_done, PRE + HEADS * (bb - 1))
                dst = vv[:, par, t, :, 0:HD]
                src = m_ps[0:KT, 0:D].rearrange("p (h i) -> p h i", i=HD)
                scale = tab[0:KT, T_VM:T_VM + 1] if t == 2 else 1.0
                act.activation(dst, src, ACT.Copy, scale=scale).then_inc(v_written, 1)

            def copy_mt(bb, g):
                wait(act, mt_ready, 4 * bb + g + 1)
                act.activation(mtb[:, g % 2, :], m_ps[0:12, :].bitcast(BF16)[:, 0:TT], ACT.Copy).then_inc(mt_copied, 1)

            def turn(b, par, kind):
                mids = kind in ("first", "loop")
                for j in range(HEADS):
                    if kind != "first":
                        n = HEADS * b + j
                        wait(act, st_ready, n + 1)
                        wait(act, pv_done, PRE + n - 1)
                        act.activation(pt[0:KT, j % 2, :], st_ps[j % 2][0:KT, 0:3 * TT], ACT.Exp,
                                       scale=1.0 / HD ** 0.5).then_inc(exp_done, 1)
                        if j in (1, 5, 9):
                            copy_mt(b, j // 4 + 1)
                    if mids:
                        if j in (6, 8, 10, 12):
                            part1(b + 2, (j - 6) // 2)
                        if j in (8, 10, 12, 14):
                            part2(b + 2, (j - 8) // 2)
                    if kind != "last":
                        if j == 12:
                            copy_v(b + 1, 1 - par, 0)
                        if j == 13:
                            copy_mt(b + 1, 0)
                            copy_v(b + 1, 1 - par, 1)
                        if j == 14:
                            copy_v(b + 1, 1 - par, 2)

            act.wait_ge(init_done, INIT)
            act.sem_inc(exp_done, PRE)
            for c in range(4):
                part1(0, c)
                part2(0, c)
            all_turns(act, turn)

            def copy_xnt(w, par, p=P):
                wait(act, xn_turned, w + 1)
                act.dma_start(xn_rows[bass.ds(w * P, p), :], xn[0:p, par, :]).then_inc(xn_out[par], 16)
                wait(act, lg_ready, w - 1)
                act.activation(xnt[:, par, :, 0:p], bank[2 + par][:, 0:KC * p].rearrange("p (k q) -> p k q", k=KC),
                               ACT.Copy).then_inc(xnt_ready, 1)

            tile_pairs(act, 0, TILES, copy_xnt)
            copy_xnt(TILES, 0, B)
            act.wait_ge(base_ready, TILES + 1)
            act.dma_start(acc_rows[0:TILES * P].rearrange("(w p) d -> p w d", p=P), h_tok[:, 0:TILES, :]).then_inc(acc_out, 16)
            act.dma_start(acc_rows[TILES * P:ROWS, :], h_tok[0:B, TILES, :]).then_inc(acc_out, 16)
            act.dma_start(acc_rows[ROWS:ROWS + P, :], h_tok[:, 0, :]).then_inc(acc_out, 16)

            act.wait_ge(ro_d, 1)
            act.activation(prob[:, :, :], tmp8[:, :, :], ACT.Exp, scale=1.0 / TEMP).then_inc(ex_ready, 1)

            def copy_xgt(t, par):
                wait(act, x_turned, t + 1)
                act.activation(xgt[:, par, :, :], bank[4][:, 0:D].rearrange("p (k q) -> p k q", k=KC),
                               ACT.Copy).then_inc(xgt_ready, 1)

            def silu(t, par):
                for half in range(2):
                    wait(act, g1_ready, 2 * t + half + 1)
                    wait(act, t_ready, 2 * t - 2)
                    act.activation(hb[:, par, half * BANK:(half + 1) * BANK], bank[half], ACT.Silu).then_inc(silu_done, 1)

            act.wait_ge(list_ready, 1)
            copy_xgt(0, 0)
            tile_pairs(act, 0, SLOTS - 2, lambda t, par: (silu(t, par), copy_xgt(t + 1, 1 - par)))
            silu(SLOTS - 2, 0)
            copy_xgt(SLOTS - 1, 1)
            silu(SLOTS - 1, 1)

        @block.vector
        def _(dve):
            step = Steps(dve, dve_step)
            step.done(dve.memset(wo_raw[:, :, :, :, :], 0.0))
            dve.wait_ge(raw_in, 16 * RAW_DMAS)
            step.done(dve.tensor_copy(trib[:, :], tri_f[:, :]))
            for o in range(KC):
                dve.tensor_copy(wo_raw[:, o, :, :, 0:HD],
                                wo_in[:, o, :].rearrange("p (g j i) -> p g j i", g=4, j=4)).then_inc(raw_ready, 1)
            dve.wait_ge(tok_in, 16 * TOK_DMAS)
            dve.tensor_copy(eyeb[:, :], eye[:, :]).then_inc(raw_ready, 1)
            n = 0
            for o in range(0, 6, 2):
                n += 1
                dve.wait_ge(setup_ready, n)
                dve.tensor_copy(wqkv_t[:, :, o * P:(o + 2) * P].rearrange("p k (o q) -> p o k q", o=2),
                                bank[6 + n % 2].rearrange("p (o k q) -> p o k q", o=2, k=KC)).then_inc(setup_read, 1)
            for g in range(0, 4, 2):
                n += 1
                dve.wait_ge(setup_ready, n)
                dve.tensor_copy(wo_t[:, g:g + 2, :].rearrange("p g d -> p (g d)"),
                                bank[6 + n % 2]).then_inc(setup_read, 1)
            n += 1
            dve.wait_ge(setup_ready, n)
            dve.tensor_copy(r_t[:, :, :], bank[6 + n % 2][:, 0:KC * E].rearrange("p (k e) -> p k e", k=KC)).then_inc(setup_read, 1)

            def copy_xt(w, par):
                wait(dve, tok_turned, w + 1)
                wait(dve, tok_proj, w - 1)
                dve.tensor_copy(xt[:, par, :, :], bank[par][0:FT, 0:3 * P].rearrange("p (c q) -> p c q", c=3)).then_inc(xt_ready, 1)

            def aggregate(w, par, mv, done, p):
                step.done(dve.bn_aggr(bag[0:p, par, :], bst[0:p, par, :]))
                dve.tensor_copy(mv[0:p, w, :], bag[0:p, par, :]).then_inc(done, 1)

            def stats(w, par, mv, done, p=P):
                step.done(dve.bn_stats(bst[0:p, par, :], h_tok[0:p, w, :]), apart=dve_passed)
                aggregate(w, par, mv, done, p)

            def norm(dst, src, w, mv, rs, p=P):
                return dve.tensor_scalar(dst, src, mv[0:p, w, 0:1], rs[0:p, w:w + 1] if isinstance(w, int)
                                         else rs[0:p, bass.ds(w, 1)], ALU.subtract, ALU.mult)

            def tok_stats(w, par):
                wait(dve, h_raw, w + 1, apart=dve_passed)
                stats(w, par, mv1, stats1)

            def tok_norm(w, par):
                step.done(norm(h_tok[:, w, :], h_tok[:, w, :], w, mv1, rs1))
                step.done(dve.tensor_tensor(out=h_tok[:, w, :], in0=h_tok[:, w, :], in1=gam_t[:, :], op=ALU.mult), apart=dve_passed)
                stats(w, par, mv2, stats2)

            def tok_z(w, par):
                wait(dve, z_turned, w - 1)
                norm(zs[:, par, :], h_tok[:, w, :], w, mv2, rs2).then_inc(z_ready, 1)

            def loop(g, body, per):
                if g == 0:
                    for w in range(GT):
                        body(w, w % 2)
                    return
                with dve.Fori(0, GT // 2, 1) as i:
                    step.enter(i, 2 * per)
                    for par in range(2):
                        body(2 * i + (GT * g + par), par)
                    step.leave(GT // 2)

            dve.wait_ge(init_done, 3)
            copy_xt(0, 0)
            for g in range(GROUPS + 2):
                if g < GROUPS - 1:
                    loop(g, lambda w, par: (copy_xt(w + 1, 1 - par), tok_stats(w, par)), 2)
                elif g == GROUPS - 1:
                    for w in range(GT * g, GT * (g + 1)):
                        if w + 1 < TILES:
                            copy_xt(w + 1, 1 - w % 2)
                        tok_stats(w, w % 2)
                if 1 <= g <= GROUPS:
                    dve.wait_ge(rstd1, g)
                    loop(g - 1, tok_norm, 4)
                    if g == GROUPS:
                        stats(16, 0, mv2, stats2, B)
                if g >= 2:
                    dve.wait_ge(rstd2, g - 1)
                    loop(g - 2, tok_z, 0)
            wait(dve, z_turned, TILES - 1)
            norm(zs[0:B, 0, :], h_tok[0:B, 16, :], 16, mv2, rs2, B).then_inc(z_ready, 1)
            dve.wait_ge(zt_written, TILES + 1)
            dve.tensor_copy(zt_b[:, :, :, NTOK], zt_b[:, :, :, NTOK - 1]).then_inc(zt_done, 1)

            ROTATE = [2 * i + 1 for i in range(8)] + [2 * i for i in range(8)]
            ROTATE = ROTATE + [HD + i for i in ROTATE]
            SUMS = [HD + i for i in range(HD)] * 2

            def rotate(bb, c):
                wait(dve, proj_ready, 4 * bb + c + 1)
                wait(dve, rot_done, 4 * (bb - 1) + c + 1, apart=dve_passed)
                dve.stream_shuffle(rot2[:, c, :], m_ps[:, 0:TT], ROTATE)
                dve.tensor_tensor(out=rot1[:, c, :], in0=m_ps[:, 0:TT], in1=cos[:, :], op=ALU.mult).then_inc(rot_in, 1)

            def maximum(bb, h):
                wait(dve, s_ready, HEADS * bb + h + 1)
                if h % 4 == 0:
                    wait(dve, mp_ready, 4 * bb + h // 4 - 1)
                dve.tensor_reduce(out=mx[:, (h // 4) % 2, :, h % 4],
                                  in_=s_ps[0:KT, 0:3 * TT].rearrange("p (q k) -> p q k", q=3),
                                  op=ALU.max, axis=AX.X).then_inc(s_read, 1)

            def normalize(bb, g):
                wait(dve, pv_done, PRE + HEADS * bb + 4 * g + 4)
                step.done(dve.reciprocal(rec[:, :], o_ps[:, 0:TT]), apart=dve_passed)
                step.done(dve.stream_shuffle(shf[:, :], rec[:, :], SUMS))
                dve.tensor_tensor(out=at_b[:, g, bb, :], in0=o_ps[:, 0:TT], in1=shf[:, :], op=ALU.mult).then_inc(norm_done, 1)

            def turn(b, par, kind):
                for j in range(HEADS):
                    if has_s_kind(kind, j):
                        maximum(*s_of(b, j))
                    if kind != "first" and j in (4, 8, 12):
                        normalize(b, j // 4 - 1)
                    if kind in ("first", "loop") and j in (4, 6, 8, 10):
                        rotate(b + 2, (j - 4) // 2)
                if kind != "first":
                    normalize(b, 3)

            dve.wait_ge(small_in, 16 * SMALL_DMAS)
            dve.sem_inc(norm_done, PRE)
            for c in range(4):
                rotate(0, c)
            turn(-1, 1, "first")
            with dve.Fori(0, (B - 2) // 2, 1) as i:
                step.enter(i, 2 * 8)
                for par in range(2):
                    turn(2 * i + par, par, "loop")
                step.leave((B - 2) // 2)
            turn(B - 2, 0, "short")
            turn(B - 1, 1, "last")

            def copy_oa(w, par):
                wait(dve, op_ready, w - 1)
                dve.tensor_copy(oa[:, par, :, :].rearrange("p g (b h) -> p g b h", b=B), at_grid[:, :, :, :, w]).then_inc(oa_ready, 1)

            def residual(w, par, p=P):
                wait(dve, op_ready, w + 1)
                step.done(dve.tensor_tensor(out=h_tok[0:p, w, :], in0=bank[par][0:p, 0:D], in1=h_tok[0:p, w, :], op=ALU.add), apart=dve_passed)
                step.done(dve.bn_stats(bst[0:p, par, :], h_tok[0:p, w, :]), apart=dve_passed)
                aggregate(w, par, mv1, stats3, p)

            def norm_u(w, par, p=P):
                step.done(norm(ut[0:p, par, :], h_tok[0:p, w, :], w, mv1, rs1, p), apart=dve_passed)
                step.done(dve.bn_stats(bst[0:p, par, :], ut[0:p, par, :]), apart=dve_passed)
                aggregate(w, par, mv2, stats4, p)

            def norm_x(w, par, p=P):
                wait(dve, xn_turned, w - 1)
                wait(dve, xn_out[par], 8 * (w - par))
                step.done(norm(ut[0:p, par, :], h_tok[0:p, w, :], w, mv1, rs1, p))
                step.done(norm(xn[0:p, par, :], ut[0:p, par, :], w, mv2, rs2, p))
                dve.tensor_tensor(out=h_tok[0:p, w, :], in0=h_tok[0:p, w, :], in1=ut[0:p, par, :], op=ALU.add).then_inc(base_ready, 1)
                step.done(dve.tensor_tensor(out=xn[0:p, par, :], in0=xn[0:p, par, :], in1=gam_f[0:p, :], op=ALU.mult))
                dve.tensor_tensor(out=xn[0:p, par, :], in0=xn[0:p, par, :], in1=bet_f[0:p, :], op=ALU.add).then_inc(xn_ready, 1)

            def copy_lg(w, par, p=P):
                wait(dve, lg_ready, w + 1)
                dve.tensor_copy(lgt[0:p, w, :], bank[4 + par][0:p, 0:E]).then_inc(lg_read, 1)

            def norm_xl(w, par):
                norm_x(w, par)
                copy_lg(w - 1, 1 - par)

            dve.wait_ge(norm_done, PRE + 4 * B)
            dve.wait_ge(bias_added, 2)
            copy_oa(0, 0)
            for g in range(GROUPS + 2):
                if g < GROUPS - 1:
                    loop(g, lambda w, par: (copy_oa(w + 1, 1 - par), residual(w, par)), 3)
                elif g == GROUPS - 1:
                    for w in range(GT * g, GT * (g + 1)):
                        if w + 1 < TILES:
                            copy_oa(w + 1, 1 - w % 2)
                        else:
                            wait(dve, op_ready, TILES - 1)
                            dve.tensor_copy(oa[:, 0, :, 0:B], at_b[:, :, :, 0]).then_inc(oa_ready, 1)
                        residual(w, w % 2)
                    residual(TILES, 0, B)
                if 1 <= g <= GROUPS:
                    dve.wait_ge(rstd3, g)
                    loop(g - 1, norm_u, 3)
                    if g == GROUPS:
                        norm_u(TILES, 0, B)
                if g >= 2:
                    dve.wait_ge(rstd4, g - 1)
                    if g == 2:
                        norm_x(0, 0)
                        norm_xl(1, 1)
                        norm_xl(2, 0)
                        norm_xl(3, 1)
                    else:
                        loop(g - 2, norm_xl, 3)
            norm_x(TILES, 0, B)
            copy_lg(TILES - 1, 1)
            copy_lg(TILES, 0, B)

            def b17(ap):
                return ap.unsqueeze(2).to_broadcast([P, 17, E])

            desc = tab[:, T_DESC:T_DESC + E].unsqueeze(1).to_broadcast([P, 17, E])
            dve.wait_ge(lg_read, TILES + 1)
            step.done(dve.tensor_reduce(out=col[0][:, :], in_=lgt[:, :, :], op=ALU.max, axis=AX.X))
            dve.tensor_tensor(out=tmp8[:, :, :], in0=lgt[:, :, :], in1=b17(col[0][:, :]), op=ALU.subtract).then_inc(ro_d, 1)
            dve.wait_ge(ex_ready, 1)
            step.done(dve.tensor_reduce(out=col[0][:, :], in_=prob[:, :, :], op=ALU.add, axis=AX.X))
            step.done(dve.reciprocal(col[1][:, :], col[0][:, :]))
            step.done(dve.tensor_tensor(out=prob[:, :, :], in0=prob[:, :, :], in1=b17(col[1][:, :]), op=ALU.mult))
            for k in range(2):
                step.done(dve.tensor_reduce(out=topw[:, k, :], in_=prob[:, :, :], op=ALU.max, axis=AX.X))
                step.done(dve.tensor_tensor(out=tmp8[:, :, :], in0=prob[:, :, :], in1=b17(topw[:, k, :]), op=ALU.is_equal))
                step.done(dve.tensor_tensor(out=tmp8[:, :, :], in0=tmp8[:, :, :], in1=desc, op=ALU.mult))
                step.done(dve.tensor_reduce(out=col[0][:, :], in_=tmp8[:, :, :], op=ALU.max, axis=AX.X))
                step.done(dve.tensor_tensor(out=sel[k][:, :, :], in0=desc, in1=b17(col[0][:, :]), op=ALU.is_equal))
                if k == 0:
                    step.done(dve.scalar_tensor_tensor(out=prob[:, :, :], in0=sel[0][:, :, :], scalar=-4.0,
                                                       in1=prob[:, :, :], op0=ALU.mult, op1=ALU.add))
            step.done(dve.tensor_tensor(out=tmp8[:, :, :], in0=sel[0][:, :, :], in1=sel[1][:, :, :], op=ALU.add))
            dve.tensor_tensor(out=mask[:, :, :], in0=tmp8[:, :, :], in1=b17(tab[:, T_VALID:T_VALID + 17]),
                              op=ALU.mult).then_inc(mask_ready, 1)
            tw = topw[:, :, :].rearrange("p k t -> p (k t)")
            step.done(dve.tensor_copy(wpart[:, 0, :], tw))
            step.done(dve.tensor_tensor(out=wres[:, :], in0=tw, in1=wpart[:, 0, :], op=ALU.subtract))
            step.done(dve.tensor_copy(wpart[:, 1, :], wres[:, :]))
            step.done(dve.tensor_tensor(out=wpart[:, 2, :], in0=wres[:, :], in1=wpart[:, 1, :], op=ALU.subtract))
            dve.wait_ge(rank_ready, 2)
            step.done(dve.tensor_copy(tot[:, :, :], bank[1][:, 0:17 * E].rearrange("p (t e) -> p e t", e=E)))
            step.done(dve.tensor_tensor_scan(cum[:, :, :].rearrange("p e t -> p (e t)"), tab[:, T_RESET:T_END],
                                             tot[:, :, :].rearrange("p e t -> p (e t)"), 0.0, ALU.mult, ALU.add))
            step.done(dve.tensor_tensor(out=tot[:, :, :], in0=cum[:, :, :], in1=tot[:, :, :], op=ALU.subtract))
            step.done(dve.tensor_tensor(out=big17[:, :, :], in0=cum[:, :, 16:17].to_broadcast([P, E, 17]),
                                        in1=tab[:, T_J128:T_J128 + 17].unsqueeze(1).to_broadcast([P, E, 17]), op=ALU.is_gt))
            step.done(dve.tensor_reduce(out=ntl[:, 0, :], in_=big17[:, :, :], op=ALU.add, axis=AX.X))
            step.done(dve.tensor_tensor_scan(ntl[:, 1, :], tab[:, T_VALID:T_VALID + E], ntl[:, 0, :], 0.0, ALU.mult, ALU.add))
            step.done(dve.tensor_tensor(out=ntl[:, 2, :], in0=ntl[:, 1, :], in1=ntl[:, 0, :], op=ALU.subtract))
            step.done(dve.tensor_scalar(ntl[:, 2, :], ntl[:, 2, :], float(P), None, ALU.mult))
            step.done(dve.tensor_tensor(out=posn[:, :, :], in0=bank[0][:, 0:17 * E].rearrange("p (t e) -> p t e", e=E),
                                        in1=tot[:, :, :].rearrange("p e t -> p t e"), op=ALU.add))
            step.done(dve.tensor_tensor(out=posn[:, :, :], in0=posn[:, :, :],
                                        in1=ntl[:, 2:3, :].to_broadcast([P, 17, E]), op=ALU.add))
            for k in range(2):
                step.done(dve.tensor_tensor(out=tmp8[:, :, :], in0=posn[:, :, :], in1=sel[k][:, :, :], op=ALU.mult))
                step.done(dve.tensor_reduce(out=col[2][:, :], in_=tmp8[:, :, :], op=ALU.add, axis=AX.X))
                step.done(dve.tensor_tensor(out=pos2[:, k, :], in0=col[2][:, :], in1=tab[:, T_INV:T_INV + 17], op=ALU.add))
            step.done(dve.tensor_copy(posi[:, :, :], pos2[:, :, :]))
            step.done(dve.tensor_scalar(poa[:, :, :], posi[:, :, :], 7, None, ALU.logical_shift_right))
            step.done(dve.tensor_scalar(pop[:, :, :], posi[:, :, :], P - 1, None, ALU.bitwise_and))
            step.done(dve.tensor_copy(poaf[:, :], poa[:, :, :].rearrange("p k t -> p (k t)")))
            step.done(dve.tensor_copy(popf[:, :], pop[:, :, :].rearrange("p k t -> p (k t)")))

            def b34(ap, n):
                return ap.unsqueeze(2).to_broadcast([P, 34, n])

            dve.tensor_tensor(out=vals[:, :, 2, :], in0=b34(poaf[:, :], SLOTS),
                              in1=tab[:, T_I40:T_I40 + SLOTS].unsqueeze(1).to_broadcast([P, 34, SLOTS]),
                              op=ALU.is_equal).then_inc(wp_ready, 1)
            dve.wait_ge(wp_ready, 1)
            for k in range(2):
                for n, t0 in ((0, T_IDHI), (1, T_IDLO)):
                    dve.tensor_tensor(out=vals[:, 17 * k:17 * k + 17, n, :], in0=vals[:, 17 * k:17 * k + 17, 2, :],
                                      in1=tab[:, t0:t0 + 17].unsqueeze(2).to_broadcast([P, 17, SLOTS]), op=ALU.mult)
            dve.tensor_tensor(out=vals[:, :, 3, :], in0=vals[:, :, 2, :], in1=b34(wpart[:, 0, :], SLOTS), op=ALU.mult)
            dve.wait_ge(xn_out[0], 16 * 9)
            dve.wait_ge(xn_out[1], 16 * 8)
            dve.tensor_tensor(out=ohp[:, :, :], in0=b34(popf[:, :], P),
                              in1=tab[:, T_I128:T_I128 + P].unsqueeze(1).to_broadcast([P, 34, P]),
                              op=ALU.is_equal).then_inc(oh_ready, 1)
            step.done(dve.tensor_tensor(out=ecmp[:, :, :], in0=ntl[0:1, 1:2, :].to_broadcast([1, SLOTS, E]),
                                        in1=tab[0:1, T_I40:T_I40 + SLOTS].unsqueeze(2).to_broadcast([1, SLOTS, E]), op=ALU.is_le))
            step.done(dve.tensor_reduce(out=esum[:, :], in_=ecmp[:, :, :], op=ALU.add, axis=AX.X))
            step.done(dve.tensor_scalar(eid[:, :], esum[:, :], float(E - 1), None, ALU.min))
            dve.wait_ge(list_ready, 1)
            step.done(dve.tensor_copy(lst[:, :, :], bank[2][:, 0:6 * SLOTS].rearrange("p (v s) -> p v s", v=6)))
            step.done(dve.scalar_tensor_tensor(out=lst[:, 0, :], in0=lst[:, 0, :], scalar=float(P), in1=lst[:, 1, :],
                                               op0=ALU.mult, op1=ALU.add))
            step.done(dve.tensor_tensor(out=lwt[:, :], in0=lst[:, 3, :], in1=lst[:, 4, :], op=ALU.add))
            step.done(dve.tensor_tensor(out=lwt[:, :], in0=lwt[:, :], in1=lst[:, 5, :], op=ALU.add))
            step.done(dve.tensor_copy(gid[:, :], lst[:, 0, :]))
            step.done(dve.tensor_scalar(lst[:, 2, :], lst[:, 2, :], -1.0, 1.0, ALU.mult, ALU.add))
            step.done(dve.scalar_tensor_tensor(out=lst[:, 0, :], in0=lst[:, 2, :], scalar=tab[:, T_DUMMY:T_DUMMY + 1],
                                               in1=lst[:, 0, :], op0=ALU.mult, op1=ALU.add))
            dve.tensor_copy(sid[:, :], lst[:, 0, :]).then_inc(route_done, 1)

            def copy_ht(t, par):
                for half in range(2):
                    wait(dve, t_ready, 2 * t + half + 1)
                    wait(dve, g2_ready, t - 1)
                    dve.tensor_copy(ht[:, par, half * 4:half * 4 + 4, :],
                                    bank[2 + half].rearrange("p (c q) -> p c q", c=4)).then_inc(ht_ready, 1)

            def scale_y(t, par):
                wait(dve, g2_ready, t + 1)
                wait(dve, y_added, 16 * (t - 1))
                dve.tensor_scalar(yb[:, par, :], bank[5 + par][:, 0:D], lwt[:, bass.ds(t, 1)], None, ALU.mult).then_inc(y_ready, 1)

            dve.wait_ge(route_done, 1)
            tile_pairs(dve, 0, SLOTS, lambda t, par: (copy_ht(t, par), scale_y(t, par)))

        @block.tensor
        def _(pe):
            def mm(out_, lhs, rhs, start, stop):
                return pe.matmul(out_, lhs, rhs, start=start, stop=stop)

            pe.wait_ge(raw_in, 16 * RAW_DMAS)
            pe.wait_ge(tok_in, 16 * TOK_DMAS)
            n = 0
            for o in range(0, 6, 2):
                n += 1
                wait(pe, setup_read, n - 2)
                for a in range(2):
                    for k in range(KC):
                        c0 = (2 * a + k) * P
                        last = pe.transpose(bank[6 + n % 2][:, c0:c0 + P], wq_raw[:, o + a, k * P:(k + 1) * P], eye[:, :])
                last.then_inc(setup_ready, 1)
            pe.wait_ge(raw_ready, 3)
            for g in range(0, 4, 2):
                n += 1
                wait(pe, setup_read, n - 2)
                for a in range(2):
                    for o in range(KC):
                        c0 = (2 * a + o) * P
                        last = pe.transpose(bank[6 + n % 2][:, c0:c0 + P],
                                            wo_raw[:, o, g + a, :, :].rearrange("p j i -> p (j i)"), eye[:, :])
                last.then_inc(setup_ready, 1)
            n += 1
            wait(pe, setup_read, n - 2)
            for k in range(KC):
                last = pe.transpose(bank[6 + n % 2][:, k * E:(k + 1) * E], r_raw[:, k * P:(k + 1) * P], eye[0:E, 0:E])
            last.then_inc(setup_ready, 1)

            def turn_x(w, par):
                wait(pe, xs_ready, w + 1)
                wait(pe, xt_ready, w - 1)
                for c in range(3):
                    last = pe.transpose(bank[par][0:FT, c * P:(c + 1) * P], xs[:, par, CUT[c]:CUT[c] + FT], eye[:, :])
                last.then_inc(tok_turned, 1)

            def project(w, par):
                wait(pe, xt_ready, w + 1)
                wait(pe, h_raw, w - 1)
                for c in range(3):
                    last = mm(bank[2 + par][:, 0:D], xt[:, par, c, :], wt[:, c, :], c == 0, c == 2)
                last.then_inc(tok_proj, 1)

            def turn_z(w, par, p=P):
                wait(pe, z_ready, w + 1)
                wait(pe, zt_written, w - 1)
                for k in range(KC):
                    last = pe.transpose(bank[4 + par][:, k * p:(k + 1) * p], zs[0:p, par, k * P:(k + 1) * P], eye[0:p, 0:p])
                last.then_inc(z_turned, 1)

            turn_x(0, 0)
            for g in range(GROUPS):
                if g < GROUPS - 1:
                    tile_pairs(pe, GT * g, GT * (g + 1), lambda w, par: (turn_x(w + 1, 1 - par), project(w, par)))
                else:
                    for w in range(GT * g, GT * (g + 1)):
                        if w + 1 < TILES:
                            turn_x(w + 1, 1 - w % 2)
                        project(w, w % 2)
                if g >= 2:
                    tile_pairs(pe, GT * (g - 2), GT * (g - 1), turn_z)
            tile_pairs(pe, GT * 2, GT * 4, turn_z)
            turn_z(TILES, 0, B)

            def wide(ps, lhs, rhs):
                for t in range(3):
                    l = lhs(t)
                    if t == 1:
                        a = BANK - TT
                        mm(ps[0:KT, TT:BANK], l, rhs[:, 0:a], True, True)
                        mm(ps[0:KT, BANK:2 * TT], l, rhs[:, a:TT], True, True)
                    else:
                        last = mm(ps[0:KT, t * TT:(t + 1) * TT], l, rhs, True, True)
                return last

            def scores(bb, par, h):
                if h == 0:
                    wait(pe, stack_in, 16 * LOADS * (bb + 1))
                wait(pe, s_read, HEADS * bb + h)
                wide(s_ps, lambda t: qs[0:SPLIT, par, h, t * KT:(t + 1) * KT], ks[0:SPLIT, par, h, :]).then_inc(s_ready, 1)

            def scores_t(bb, par, h):
                if h % 4 == 0:
                    wait(pe, mrow_in[h // 4], 16 * MROWS * (bb + 1))
                wait(pe, exp_done, PRE + HEADS * bb + h - 1)
                wide(st_ps[h % 2], lambda t: ks[0:SPLIT + MROWS, par, h, t * KT:(t + 1) * KT],
                     qs[0:SPLIT + MROWS, par, h, :]).then_inc(st_ready, 1)

            def weigh(bb, par, h):
                wait(pe, exp_done, PRE + HEADS * bb + h + 1)
                if h == 0:
                    wait(pe, v_written, 3 * (bb + 1))
                if h % 4 == 0:
                    wait(pe, norm_done, PRE + 4 * bb + h // 4)
                r0 = 32 * (h % 4)
                for t in range(3):
                    last = mm(o_ps[r0:r0 + 32, 0:TT], vv[:, par, t, h, :], pt[0:KT, h % 2, t * TT:(t + 1) * TT], t == 0, t == 2)
                last.then_inc(pv_done, 1)

            def misc(use, prev):
                _, what, bb, n_ = use
                s_, v_ = read_of(prev)
                wait(pe, s_, v_)
                if what == "p":
                    for k in range(KC):
                        last = mm(m_ps[:, 0:TT], wqkv_t[:, k, n_ * P:(n_ + 1) * P], zt_b[:, k, bb, :], k == 0, k == KC - 1)
                    last.then_inc(proj_ready, 1)
                elif what == "v":
                    wait(pe, zb_ready, bb + 1)
                    for k in range(KC):
                        last = mm(m_ps[0:KT, 0:D], zb[:, k, n_ * KT:(n_ + 1) * KT], wqkv_t[:, k, 2 * D:3 * D], k == 0, k == KC - 1)
                    last.then_inc(v_ready, 1)
                else:
                    wait(pe, mp_ready, 4 * bb + n_ + 1)
                    dst = m_ps[0:12, :].bitcast(BF16)
                    for t in range(3):
                        last = pe.transpose(dst[:, t * KT:(t + 1) * KT],
                                            mpt[:, n_ % 2, t, :, :].rearrange("p r h -> p (r h)"), eyeb[0:KT, 0:KT])
                    last.then_inc(mt_ready, 1)

            def turn(b, par, kind):
                uses = misc_uses(b, kind)
                prev = before(b, kind)
                for j in range(HEADS):
                    if has_s_kind(kind, j):
                        bb, h = s_of(b, j)
                        scores(bb, par if j < LEAD else 1 - par, h)
                    if kind != "first":
                        scores_t(b, par, j)
                        if j > 0:
                            weigh(b, par, j - 1)
                    for use in uses:
                        if int(use[0]) == j:
                            misc(use, prev)
                            prev = use
                if kind != "first":
                    weigh(b, par, HEADS - 1)

            pe.wait_ge(zt_done, 1)
            prev = None
            for c in range(4):
                use = (0, "p", 0, c)
                if prev is None:
                    pe.wait_ge(setup_read, n)
                    for k in range(KC):
                        last = mm(m_ps[:, 0:TT], wqkv_t[:, k, c * P:(c + 1) * P], zt_b[:, k, 0, :], k == 0, k == KC - 1)
                    last.then_inc(proj_ready, 1)
                else:
                    misc(use, prev)
                prev = use
            pe.wait_ge(init_done, INIT)
            pe.sem_inc(pv_done, PRE)
            all_turns(pe, turn)

            def out_project(w, par, p=P):
                wait(pe, oa_ready, w + 1)
                wait(pe, stats3, w - 1)
                for g2 in range(4):
                    last = mm(bank[par][0:p, 0:D], oa[:, par, g2, 0:p], wo_t[:, g2, :], g2 == 0, g2 == 3)
                last.then_inc(op_ready, 1)

            def turn_xn(w, par, p=P):
                wait(pe, xn_ready, w + 1)
                wait(pe, xnt_ready, w - 1)
                for k in range(KC):
                    last = pe.transpose(bank[2 + par][:, k * p:(k + 1) * p], xn[0:p, par, k * P:(k + 1) * P], eye[0:p, 0:p])
                last.then_inc(xn_turned, 1)

            def logits(w, par, p=P):
                wait(pe, xnt_ready, w + 1)
                wait(pe, lg_read, w - 1)
                for k in range(KC):
                    last = mm(bank[4 + par][0:p, 0:E], xnt[:, par, k, 0:p], r_t[:, k, :], k == 0, k == KC - 1)
                last.then_inc(lg_ready, 1)

            pe.wait_ge(norm_done, PRE + 4 * B)
            for g in range(GROUPS):
                tile_pairs(pe, GT * g, GT * (g + 1), out_project)
                if g == GROUPS - 1:
                    out_project(TILES, 0, B)
                if g >= 2:
                    tile_pairs(pe, GT * (g - 2), GT * (g - 1), lambda w, par: (turn_xn(w, par), logits(w, par)))
            tile_pairs(pe, GT * 2, GT * 4, lambda w, par: (turn_xn(w, par), logits(w, par)))
            turn_xn(TILES, 0, B)
            logits(TILES, 0, B)

            pe.wait_ge(mask_ready, 1)
            flat = mask[:, :, :].rearrange("p t e -> p (t e)")
            mm(bank[0][:, 0:17 * E], trib[:, :], flat, True, True).then_inc(rank_ready, 1)
            mm(bank[1][:, 0:17 * E], onesb[:, :], flat, True, True).then_inc(rank_ready, 1)
            pe.wait_ge(oh_ready, 1)
            pe.wait_ge(wv_ready, 2)
            for c in range(34):
                last = mm(bank[2][:, 0:6 * SLOTS], ohp[:, c, :], vals[:, c, :, :].rearrange("p v s -> p (v s)"), c == 0, c == 33)
            last.then_inc(list_ready, 1)

            def turn_g(t, par):
                wait(pe, xg_in[par], 8 * (t - par) + 16)
                wait(pe, xgt_ready, t)
                for k in range(KC):
                    last = pe.transpose(bank[4][:, k * P:(k + 1) * P], xg[:, par, k * P:(k + 1) * P], eye[:, :])
                last.then_inc(x_turned, 1)

            def gemm1(t, par, half, e):
                if half == 0:
                    wait(pe, xgt_ready, t + 1)
                wait(pe, silu_done, 2 * t - 1 + half)
                for k in range(KC):
                    last = mm(bank[half], xgt[:, par, k, :], w1_sb[:, e, k, half * BANK:(half + 1) * BANK], k == 0, k == KC - 1)
                last.then_inc(g1_ready, 1)

            def turn_h(t, par):
                for half in range(2):
                    wait(pe, silu_done, 2 * t + half + 1)
                    wait(pe, ht_ready, 2 * t - 1 + half)
                    for c in range(4):
                        cc = half * 4 + c
                        last = pe.transpose(bank[2 + half][:, c * P:(c + 1) * P], hb[:, par, cc * P:(cc + 1) * P], eye[:, :])
                    last.then_inc(t_ready, 1)

            def gemm2(t, par, e):
                wait(pe, y_ready, t - 1)
                for c in range(F // P):
                    if c % 4 == 0:
                        wait(pe, ht_ready, 2 * t + c // 4 + 1)
                    last = mm(bank[5 + par][:, 0:D], ht[:, par, c, :], w2_sb[:, e, c, :], c == 0, c == F // P - 1)
                last.then_inc(g2_ready, 1)

            def expert(t):
                return pe.value_load(eid[0:1, bass.ds(t, 1)], min_val=0, max_val=E - 1)

            pe.wait_ge(route_done, 1)
            pe.wait_ge(w_early_in, 16 * E_EARLY)
            pe.wait_ge(w_late_in, 16 * (2 * E - E_EARLY))
            turn_g(0, 0)
            e0 = expert(0)
            gemm1(0, 0, 0, e0)
            gemm1(0, 0, 1, e0)
            turn_g(1, 1)

            def tile(t, par, more):
                e_now, e_before = expert(t), expert(t - 1)
                gemm1(t, par, 0, e_now)
                turn_h(t - 1, 1 - par)
                gemm1(t, par, 1, e_now)
                gemm2(t - 1, 1 - par, e_before)
                if more:
                    turn_g(t + 1, 1 - par)

            tile_pairs(pe, 1, SLOTS - 1, lambda t, par: tile(t, par, True))
            tile(SLOTS - 1, 1, False)
            turn_h(SLOTS - 1, 1)
            gemm2(SLOTS - 1, 1, expert(SLOTS - 1))


def kernel(x, cls_tok, L0_tok_W, L0_tok_gamma, L0_attn_w_qkv, L0_attn_w_out, L0_attn_b_out, L0_ffn_gamma,
           L0_ffn_beta, L0_ffn_router_w, L0_ffn_W1, L0_ffn_W2):
    import concourse.bacc as _bacc
    from concourse.bass_utils import run_bass_kernel_spmd as _run

    data = dict(x=x, cls_tok=cls_tok, tok_w=L0_tok_W, tok_gamma=L0_tok_gamma, w_qkv=L0_attn_w_qkv,
                w_out=L0_attn_w_out, b_out=L0_attn_b_out, f_gamma=L0_ffn_gamma, f_beta=L0_ffn_beta,
                router_w=L0_ffn_router_w, w1=L0_ffn_W1, w2=L0_ffn_W2)
    data = {k: np.ascontiguousarray(v) for k, v in data.items()}
    data.update(zip(("cos_in", "sin_in", "eye_in", "tri_in", "tab_in"), shape_tables()))
    nc = _bacc.Bacc("TRN2", target_bir_lowering=False, num_devices=1)
    args = {k: nc.dram_tensor(k, v.shape, mybir.dt.from_np(v.dtype), kind="ExternalInput").ap() for k, v in data.items()}
    args["out"] = nc.dram_tensor("out", (B, NTOK, D), F32, kind="ExternalOutput").ap()
    vit_block(nc, **args)
    r = _run(nc, [data], core_ids=[0])
    return r.results[0]["out"]
```

```python
from contextlib import ExitStack

import concourse.bass as bass
import numpy as np
from concourse import mybir

F32 = mybir.dt.float32
BF16 = mybir.dt.bfloat16
I32 = mybir.dt.int32
ALU = mybir.AluOpType
ACT = mybir.ActivationFunctionType
AX = mybir.AxisListType

P = 128
B, C, IMG = 8, 5, 128
PATCH = 8
GRID = IMG // PATCH
D = 256
NTOK = GRID * GRID + 1
ROWS = B * NTOK
HEADS, HD = 16, 16
E, F = 8, 1024
KC = D // P
FT = 107
NFEAT = C * PATCH * PATCH
CUT = [0, FT, NFEAT - FT]
TT = NTOK + 1
OC = (TT + 31) // 32 * 32
KT = TT // 3
BANK = 512
TILES = GRID
EPS = 1e-5
TEMP = 1.5
SLOTS = (2 * ROWS + E * (P - 1)) // P
QPART = [0, 0, 1, 1, 0, 2]
KPART = [0, 1, 0, 1, 2, 0]
SPLIT = HD * len(QPART)
MROWS = 3
LEAD = 8
INIT = 8
PRE = 2
LOADS = 2 * len(QPART)

T_VM, T_DUMMY, T_IDHI, T_IDLO, T_VALID, T_INV, T_DESC, T_J128, T_I128, T_I40, T_RESET = (
    0, 1, 2, 19, 36, 53, 70, 78, 95, 223, 263)
T_END = T_RESET + E * 17


def shape_tables():
    inv = (1.0 / 10000.0 ** (np.arange(0, HD, 2, dtype=np.float32) / np.float32(HD))).astype(np.float32)
    pos = np.minimum(np.arange(TT), NTOK - 1).astype(np.float32)
    ang = (inv[:, None] * pos[None, :]).astype(np.float32)
    lane = np.arange(P) % HD
    cos = np.cos(ang)[lane % (HD // 2)].astype(np.float32)
    sign = np.where(lane < HD // 2, -1.0, 1.0).astype(np.float32)
    sin = (np.sin(ang)[lane % (HD // 2)] * sign[:, None]).astype(np.float32)
    eye = np.eye(P, dtype=np.float32)
    tri = np.triu(np.ones((P, P), np.float32), 1)
    tab = np.zeros((P, T_END), np.float32)
    p = np.arange(P)
    tab[:, T_VM] = p != KT - 1
    tab[:, T_DUMMY] = ROWS + p
    tab[:, T_IDHI:T_IDHI + 17] = np.arange(17)
    tab[:, T_IDLO:T_IDLO + 17] = p[:, None]
    valid = np.ones((P, 17), np.float32)
    valid[B:, 16] = 0
    tab[:, T_VALID:T_VALID + 17] = valid
    tab[:, T_INV:T_INV + 17] = (1 - valid) * 8192
    tab[:, T_DESC:T_DESC + E] = E - np.arange(E)
    tab[:, T_J128:T_J128 + 17] = np.arange(17) * P
    tab[:, T_I128:T_I128 + P] = np.arange(P)
    tab[:, T_I40:T_I40 + SLOTS] = np.arange(SLOTS)
    tab[:, T_RESET:T_END] = np.tile(np.arange(17) != 0, E)
    return cos, sin, eye, tri, tab


class Steps:

    def __init__(self, eng, sem, apart=None):
        self.eng, self.sem, self.n, self.turn, self.apart = eng, sem, 0, 0, apart

    def done(self, ins, apart=None):
        ins.then_inc(self.sem, 1)
        self.n += 1
        wait(self.eng, self.sem, self.turn + self.n, apart or self.apart)

    def enter(self, turn, per):
        self.turn, self.start, self.per = turn * per, self.n, per

    def leave(self, turns):
        assert self.n - self.start == self.per, (self.n, self.start, self.per)
        self.n, self.turn = self.start + self.per * turns, 0


def wait(eng, sem, value, apart=None):
    if not isinstance(value, int) or value > 0:
        eng.wait_ge(sem, value)
        if apart is not None and not isinstance(value, int):
            eng.sem_inc(apart, 1)


def vit_block(nc, x, cls_tok, tok_w, tok_gamma, w_qkv, w_out, b_out, f_gamma, f_beta, router_w, w1, w2,
              cos_in, sin_in, eye_in, tri_in, tab_in, out):
    ctx = ExitStack()
    base = [(nc.sbuf_base + 63) // 64 * 64]

    def at(name, shape, dt, offset):
        return nc.alloc_sbuf_tensor_at(name, shape, dt, offset=offset)

    def size(shape, dt):
        n = 1
        for s in shape[1:]:
            n *= s
        return (n * (2 if dt == BF16 else 4) + 31) // 32 * 32

    class Region:

        def __init__(self, start):
            self.end = start

        def add(self, name, shape, dt=F32):
            t = at(name, shape, dt, self.end)
            self.end += size(shape, dt)
            return t

    with ctx:
        keep = Region(base[0])
        h_tok = keep.add("h_tok", [P, 17, D])
        eye = keep.add("eye", [P, P])
        eyeb = keep.add("eyeb", [P, P], BF16)
        trib = keep.add("trib", [P, P], BF16)
        onesb = keep.add("onesb", [P, P], BF16)
        tab = keep.add("tab", [P, T_END])
        gam_t = keep.add("gam_t", [P, D])
        bout = keep.add("bout", [P, D])
        gam_f = keep.add("gam_f", [P, D])
        bet_f = keep.add("bet_f", [P, D])
        r_t = keep.add("r_t", [P, KC, E])
        bst = [keep.add(f"bst{n}", [P, 4, 6]) for n in range(2)]
        mv = [keep.add(f"mv{n}", [P, 4, 2]) for n in range(2)]
        rs = [keep.add(f"rs{n}", [P, 4]) for n in range(2)]
        nb = [keep.add(f"nb{n}", [P, 4]) for n in range(2)]
        mhalf = keep.add("mhalf", [P, 2])
        wo_t = keep.add("wo_t", [P, 4, D])
        lwt = keep.add("lwt", [P, SLOTS])
        gid = keep.add("gid", [P, SLOTS], I32)
        sid = keep.add("sid", [P, SLOTS], I32)
        eid = keep.add("eid", [1, SLOTS], I32)
        lgt = keep.add("lgt", [P, 17, E])
        g_idx = keep.add("g_idx", [P, 2, 1], I32)
        s_idx = keep.add("s_idx", [P, 2, 1], I32)
        ph = Region(keep.end)
        pt = ph.add("pt", [P, 8, 3 * TT])
        wqkv_t = ph.add("wqkv_t", [P, KC, 3 * D])
        cos = ph.add("cos", [P, TT])
        sin = ph.add("sin", [P, TT])
        st = Region(keep.end)
        oa = st.add("oa", [P, 2, 4, P])
        xnt = st.add("xnt", [P, 2, KC, P])
        xn = st.add("xn", [P, 4, D])
        ut = st.add("ut", [P, 4, D])
        assert st.end <= ph.end
        at_start = ph.end
        ao = Region(at_start)
        attn_t = ao.add("attn_t", [P, 4, B * TT])
        su = Region(at_start)
        wq_raw = su.add("wq_raw", [P, 6, D])
        wo_in = su.add("wo_in", [P, KC, D])
        wo_raw = su.add("wo_raw", [P, KC, 4, 4, 32])
        r_raw = su.add("r_raw", [E, D])
        tri_f = su.add("tri_f", [P, P])
        wt = su.add("wt", [FT, 3, D])
        xs = su.add("xs", [P, 2, NFEAT])
        xt = su.add("xt", [FT, 2, 3, P])
        zs = su.add("zs", [P, 2, D])
        assert su.end <= ao.end
        ro = Region(st.end)
        sel = [ro.add(f"sel{k}", [P, 17, E]) for k in range(2)]
        prob = ro.add("prob", [P, 17, E])
        tmp8 = ro.add("tmp8", [P, 17, E])
        col = [ro.add(f"col{k}", [P, 17]) for k in range(3)]
        topw = ro.add("topw", [P, 2, 17])
        mask = ro.add("mask", [P, 17, E], BF16)
        tot = ro.add("tot", [P, E, 17])
        cum = ro.add("cum", [P, E, 17])
        posn = ro.add("posn", [P, 17, E])
        ntl = ro.add("ntl", [P, 3, E])
        big17 = ro.add("big17", [P, E, 17])
        pos2 = ro.add("pos2", [P, 2, 17])
        posi = ro.add("posi", [P, 2, 17], I32)
        poa = ro.add("poa", [P, 2, 17], I32)
        pop = ro.add("pop", [P, 2, 17], I32)
        poaf = ro.add("poaf", [P, 34])
        popf = ro.add("popf", [P, 34])
        wres = ro.add("wres", [P, 34])
        wpart = ro.add("wpart", [P, 3, 34], BF16)
        vals = ro.add("vals", [P, 34, 6, SLOTS], BF16)
        lst = ro.add("lst", [P, 6, SLOTS])
        ecmp = ro.add("ecmp", [1, SLOTS, E])
        esum = ro.add("esum", [1, SLOTS])
        ro2 = Region(keep.end)
        ohp = ro2.add("ohp", [P, 34, P], BF16)
        assert ro2.end <= st.end
        fx = Region(keep.end)
        xg = fx.add("xg", [P, 2, D])
        xgt = fx.add("xgt", [P, 2, KC, P])
        w1c = fx.add("w1c", [P, 2, KC, F])
        ht = fx.add("ht", [P, 2, F // P, P])
        yb = fx.add("yb", [P, 2, D])
        W_EXPERT = KC * F * 4
        w_start = nc.sbuf_usable_end // 64 * 64 - 2 * E * W_EXPERT
        wr = Region(w_start)
        w1_sb = wr.add("w1_sb", [P, E, KC, F])
        w2_sb = wr.add("w2_sb", [P, E, F // P, D])
        assert wr.end <= nc.sbuf_usable_end and max(fx.end, ro.end) <= w_start
        first = -(-(ao.end - w_start) // W_EXPERT)
        EARLY = range(first, first + 3)
        OVER_AO = range(first)
        BEHIND = range(first + 3, E)
        ov = Region(w_start + (first + 3) * W_EXPERT)
        zt = ov.add("zt", [P, KC, B * TT])
        x_at = ov.end
        qs = ov.add("qs", [P, 2, HEADS, TT], BF16)
        parts = ov.add("parts", [P, 3, 4, TT], BF16)
        xin = at("xin", [P, C * PATCH, GRID, PATCH], F32, x_at)
        assert x_at + size([P, C * PATCH, GRID, PATCH], F32) <= ov.end
        ks = ov.add("ks", [P, 2, HEADS, TT], BF16)
        vv = ov.add("vv", [P, 2, 3, HEADS, 32])
        zb = ov.add("zb", [P, KC, TT])
        rot1 = ov.add("rot1", [P, 4, TT])
        rot2 = ov.add("rot2", [P, 4, TT])
        ot = ov.add("ot", [P, OC])
        oq = ov.add("oq", [P, OC])
        ob = ov.add("ob", [P, OC])
        rec = ov.add("rec", [P, OC // 32])
        mx = ov.add("mx", [KT, 2, 3, 4])
        mneg = ov.add("mneg", [KT, 2, 3, 4])
        mres = ov.add("mres", [KT, 3, 4])
        mpt = ov.add("mpt", [KT, 2, 3, 3, 4], BF16)
        mtb = ov.add("mtb", [12, 2, TT], BF16)
        assert ov.end <= nc.sbuf_usable_end

        s_ps = ctx.enter_context(nc.psum_tensor("s_ps", [P, 2 * BANK], F32))
        st_ps = [ctx.enter_context(nc.psum_tensor(f"st_ps{i}", [P, 2 * BANK], F32)) for i in range(2)]
        o_ps = ctx.enter_context(nc.psum_tensor("o_ps", [P, BANK], F32))
        m_ps = ctx.enter_context(nc.psum_tensor("m_ps", [P, BANK], F32))
        bank = [s_ps[:, 0:BANK], s_ps[:, BANK:], st_ps[0][:, 0:BANK], st_ps[0][:, BANK:],
                st_ps[1][:, 0:BANK], st_ps[1][:, BANK:], o_ps[:, :], m_ps[:, :]]

        split_rows = nc.dram_tensor("split_rows", [3, 4, P, TT], BF16).ap()
        xn_rows = nc.dram_tensor("xn_rows", [ROWS, D], F32).ap()
        acc_rows = nc.dram_tensor("acc_rows", [ROWS + P, D], F32).ap()

        def sem(name):
            return ctx.enter_context(nc.semaphore(name))

        sp_passed, pool_passed, dve_passed = sem("sp_passed"), sem("pool_passed"), sem("dve_passed")
        tok_in = sem("tok_in")
        raw_in = sem("raw_in")
        small_in = sem("small_in")
        w_early_in = sem("w_early_in")
        w_late_in = sem("w_late_in")
        pool_step, dve_step, act_step = sem("pool_step"), sem("dve_step"), sem("act_step")
        setup_ready = sem("setup_ready")
        setup_read = sem("setup_read")
        raw_ready = sem("raw_ready")
        init_done = sem("init_done")
        pt_cleared = sem("pt_cleared")
        xs_ready, tok_turned, xt_ready, tok_proj, h_raw = (
            sem("xs_ready"), sem("tok_turned"), sem("xt_ready"), sem("tok_proj"), sem("h_raw"))
        bn1_done, bn2_done, normed, gamma_done = sem("bn1_done"), sem("bn2_done"), sem("normed"), sem("gamma_done")
        stats1, stats2, rstd1, rstd2 = sem("stats1"), sem("stats2"), sem("rstd1"), sem("rstd2")
        z_ready, z_turned, zt_written = sem("z_ready"), sem("z_turned"), sem("zt_written")
        zt_done = sem("zt_done")
        proj_ready, rot_in, x_ready, p1_ready, r_ready, p2_ready, rot_done = (
            sem("proj_ready"), sem("rot_in"), sem("x_ready"), sem("p1_ready"), sem("r_ready"),
            sem("p2_ready"), sem("rot_done"))
        split_out, stack_in = sem("split_out"), sem("stack_in")
        zb_ready, v_ready, v_written = sem("zb_ready"), sem("v_ready"), sem("v_written")
        s_ready, s_read, mp_ready, mt_ready, mt_copied = (
            sem("s_ready"), sem("s_read"), sem("mp_ready"), sem("mt_ready"), sem("mt_copied"))
        mrow_in = [sem(f"mrow_in{g}") for g in range(4)]
        st_ready, exp_done, pv_done, o_read, ob_ready, norm_done = (
            sem("st_ready"), sem("exp_done"), sem("pv_done"), sem("o_read"), sem("ob_ready"), sem("norm_done"))
        bias_added = sem("bias_added")
        oa_ready, op_ready, h1_ready, u_ready, xa_ready, xg_done = (
            sem("oa_ready"), sem("op_ready"), sem("h1_ready"), sem("u_ready"), sem("xa_ready"), sem("xg_done"))
        bn3_done, bn4_done = sem("bn3_done"), sem("bn4_done")
        stats3, stats4, rstd3, rstd4 = sem("stats3"), sem("stats4"), sem("rstd3"), sem("rstd4")
        base_ready, xn_ready, xn_turned, xnt_ready, lg_ready, lg_read = (
            sem("base_ready"), sem("xn_ready"), sem("xn_turned"), sem("xnt_ready"), sem("lg_ready"), sem("lg_read"))
        xn_out, acc_out = [sem("xn_out0"), sem("xn_out1")], sem("acc_out")
        ro_d, ex_ready, mask_ready, rank_ready, oh_ready, wp_ready, wv_ready, list_ready, route_done = (
            sem("ro_d"), sem("ex_ready"), sem("mask_ready"), sem("rank_ready"), sem("oh_ready"),
            sem("wp_ready"), sem("wv_ready"), sem("list_ready"), sem("route_done"))
        xg_in = [sem("xg_in0"), sem("xg_in1")]
        x_turned, xgt_ready, w1_ready, g1_ready, silu_done, g2_ready, y_ready, y_added = (
            sem("x_turned"), sem("xgt_ready"), sem("w1_ready"), sem("g1_ready"), sem("silu_done"),
            sem("g2_ready"), sem("y_ready"), sem("y_added"))
        out_done = sem("out_done")

        TOK_DMAS = 8 + 3 + 3
        RAW_DMAS = 4
        SMALL_DMAS = 6
        zt_b = zt[:, :, :].rearrange("p k (b t) -> p k b t", t=TT)
        zt_grid = zt_b[:, :, :, 1:NTOK].rearrange("p k b (h w) -> p k b h w", w=GRID)
        at_b = attn_t[:, :, :].rearrange("p g (b t) -> p g b t", t=TT)
        at_grid = at_b[:, :, :, 1:NTOK].rearrange("p g b (h w) -> p g b h w", w=GRID)

        def has_s_kind(kind, j):
            return kind != "first" if j < LEAD else kind != "last"

        def s_of(b, j):
            return (b, j + LEAD) if j < LEAD else (b + 1, j - LEAD)

        def misc_uses(b, kind):
            uses = []
            if kind != "first":
                uses += [(1, "mt", b, 1), (5, "mt", b, 2), (9, "mt", b, 3)]
            if kind in ("first", "loop"):
                uses += [(0, "p", b + 2, 0), (4, "p", b + 2, 1), (8, "p", b + 2, 2), (12, "p", b + 2, 3)]
            if kind != "last":
                uses += [(6, "v", b + 1, 0), (10, "v", b + 1, 1), (13, "mt", b + 1, 0), (14, "v", b + 1, 2)]
            return sorted(uses, key=lambda u: u[0])

        def read_of(use):
            _, what, b, n = use
            s, per = {"p": (rot_in, 4), "v": (v_written, 3), "mt": (mt_copied, 4)}[what]
            return s, b * per + n + 1

        def before(b, kind):
            if kind == "first":
                return (0, "p", 0, 3)
            return (14, "v", b, 2)

        PASSES = (B - 4) // 2

        def all_turns(eng, body, step=None, per=0):
            body(-1, 1, "first")
            body(0, 0, "loop")
            with eng.Fori(0, PASSES, 1) as i:
                if step is not None:
                    step.enter(i, 2 * per)
                for par in (1, 0):
                    body(2 * i + (2 - par), par, "loop")
                if step is not None:
                    step.leave(PASSES)
            body(B - 3, 1, "loop")
            body(B - 2, 0, "short")
            body(B - 1, 1, "last")

        def has_before(b):
            return not isinstance(b, int) or b > 0

        STEP0, STEP_PASSES = 3, 2

        def all_steps(eng, body, step=None, per=0):
            for s in range(STEP0):
                body(s, s % 2)
            with eng.Fori(0, STEP_PASSES, 1) as i:
                if step is not None:
                    step.enter(i, 2 * per)
                body(2 * i + STEP0, STEP0 % 2)
                body(2 * i + (STEP0 + 1), (STEP0 + 1) % 2)
                if step is not None:
                    step.leave(STEP_PASSES)
            for s in range(STEP0 + 2 * STEP_PASSES, 12):
                body(s, s % 2)

        def some(w, count=TILES):
            return not isinstance(w, int) or 0 <= w < count

        def rows(w):
            return B if isinstance(w, int) and w == TILES else P

        def pair_end(pair):
            return min(2 * pair + 2, TILES + 1) if isinstance(pair, int) else 2 * pair + 2

        def tile_pairs(eng, t0, t1, body):
            if t0 < 2:
                body(t0, t0 % 2)
                body(t0 + 1, (t0 + 1) % 2)
                t0 += 2
            if t0 < t1:
                with eng.Fori(0, (t1 - t0) // 2, 1) as i:
                    body(2 * i + t0, t0 % 2)
                    body(2 * i + (t0 + 1), (t0 + 1) % 2)

        ot_b = ot[:, :].rearrange("p (c i) -> p c i", i=32)
        oq_b = oq[:, :].rearrange("p (c i) -> p c i", i=32)
        block = ctx.enter_context(nc.Block())

        @block.sync
        def _(sp):
            for b in range(B):
                sp.dma_start(xin[b * GRID:(b + 1) * GRID, :, :, :].rearrange("p (c r) w q -> p c (r w q)", c=C),
                             x[b].rearrange("c (h r) w -> h c (r w)", r=PATCH)).then_inc(tok_in, 16)
            sp.dma_start(wt[:, 0, :], tok_w[0:FT, :]).then_inc(tok_in, 16)
            sp.dma_start(wt[:, 1, :], tok_w[FT:2 * FT, :]).then_inc(tok_in, 16)
            sp.wait_ge(init_done, 1)
            sp.dma_start(wt[1:FT, 2, :], tok_w[2 * FT:NFEAT, :]).then_inc(tok_in, 16)
            w1_v = w1.rearrange("e (k p) f -> p e k f", p=P)
            w2_v = w2.rearrange("e (k p) d -> p e k d", p=P)
            for e in EARLY:
                sp.dma_start(w1_sb[:, e, :, :], w1_v[:, e, :, :]).then_inc(w_early_in, 16)

            def store_split(bb):
                wait(sp, rot_done, 4 * (bb + 1), apart=sp_passed)
                wait(sp, stack_in, 16 * LOADS * bb)
                sp.dma_start(split_rows.rearrange("r c p t -> p r c t"), parts[:, :, :, :]).then_inc(split_out, 16)

            def load_stack(bb, par, cold):
                wait(sp, split_out, 16 * (bb + 1), apart=sp_passed)
                if not cold:
                    wait(sp, st_ready, HEADS * (bb - 1) + 1)
                    wait(sp, s_ready, HEADS * (bb - 1) + 1)
                for dst, c0, pick in ((qs, 0, QPART), (ks, 2, KPART)):
                    src = split_rows[:, c0:c0 + 2, :, :].rearrange("r c (h i) t -> r i (c h) t", i=HD)
                    for r, part in enumerate(pick):
                        sp.dma_start(dst[r * HD:(r + 1) * HD, par, :, :], src[part]).then_inc(stack_in, 16)

            def max_rows(bb, par, g):
                wait(sp, mt_copied, 4 * bb + g + 1)
                for r in range(MROWS):
                    sp.dma_start(qs[SPLIT + r:SPLIT + r + 1, par, 4 * g:4 * g + 4, :],
                                 mtb[4 * r:4 * r + 4, g % 2, :]).then_inc(mrow_in[g], 16)

            def turn(b, par, kind):
                if kind != "first":
                    max_rows(b, par, 1)
                    if kind != "last":
                        load_stack(b + 1, 1 - par, False)
                    max_rows(b, par, 2)
                    max_rows(b, par, 3)
                if kind != "last":
                    max_rows(b + 1, 1 - par, 0)
                if kind in ("first", "loop"):
                    store_split(b + 2)

            store_split(0)
            load_stack(0, 0, True)
            all_turns(sp, turn)

            sp.wait_ge(norm_done, PRE + 4 * B)
            sp.wait_ge(proj_ready, 4 * B)
            for e in BEHIND:
                sp.dma_start(w1_sb[:, e, :, :], w1_v[:, e, :, :]).then_inc(w_late_in, 16)
            for e in range(E):
                sp.dma_start(w2_sb[:, e, :, :], w2_v[:, e, :, :]).then_inc(w_late_in, 16)
            sp.wait_ge(oa_ready, TILES + 1)
            for e in OVER_AO:
                sp.dma_start(w1_sb[:, e, :, :], w1_v[:, e, :, :]).then_inc(w_late_in, 16)

            sp.wait_ge(y_added, 16 * SLOTS)
            acc_b = acc_rows[0:TILES * P].rearrange("(w b h) d -> b h w d", w=GRID, b=B)
            for b in range(B):
                sp.dma_start(out[b, 1:NTOK, :].rearrange("(h w) d -> h w d", w=GRID), acc_b[b]).then_inc(out_done, 16)
            sp.dma_start(out[:, 0, :], acc_rows[TILES * P:ROWS, :]).then_inc(out_done, 16)
            sp.wait_ge(out_done, 16 * (B + 1))

        @block.gpsimd
        def _(pool):
            step = Steps(pool, pool_step, apart=pool_passed)
            pool.memset(wt[:, 2, :], 0.0).then_inc(init_done, 1)
            for n, (ap, value) in enumerate(((mhalf[:, :], -0.5), (onesb[:, :], 1.0), (ks[SPLIT:P, :, :, :], 1.0),
                                             (vv[:, :, :, :, :], 1.0), (lgt[:, :, :], 0.0))):
                pool.wait_ge(init_done, n + 1)
                pool.memset(ap, value).then_inc(init_done, 1)
            pool.wait_ge(init_done, INIT - 2)
            pool.wait_ge(small_in, 16 * SMALL_DMAS)
            pool.tensor_scalar(vv[0:KT, :, 2, :, HD:32], vv[0:KT, :, 2, :, HD:32], tab[0:KT, T_VM:T_VM + 1], None,
                               ALU.mult).then_inc(init_done, 1)

            def rstd(n, pair, q, ready, shift):
                p, m = (B, 1) if isinstance(pair, int) and pair == TILES // 2 else (P, 2)
                sl = slice(2 * q, 2 * q + m)
                step.done(pool.tensor_scalar(rs[n][0:p, sl], mv[n][0:p, sl, 1], EPS, None, ALU.add))
                last = pool.tensor_tensor(out=rs[n][0:p, sl], in0=rs[n][0:p, sl], in1=mhalf[0:p, 0:m], op=ALU.pow)
                if shift:
                    step.done(last)
                    step.done(pool.tensor_scalar(nb[n][0:p, sl], mv[n][0:p, sl, 0], -1.0, None, ALU.mult))
                    last = pool.tensor_tensor(out=nb[n][0:p, sl], in0=nb[n][0:p, sl], in1=rs[n][0:p, sl], op=ALU.mult)
                last.then_inc(ready, 1)
                wait(pool, ready, pair + 1, apart=pool_passed)

            def tokens_step(s, q):
                if some(s - 2, 9):
                    wait(pool, stats2, s - 1, apart=pool_passed)
                    if isinstance(s, int):
                        wait(pool, z_ready, 2 * (s - 2) - 2)
                    rstd(1, s - 2, q, rstd2, True)
                for k in range(2):
                    w = 2 * s + k - 2
                    if some(w):
                        wait(pool, normed, w + 1, apart=pool_passed)
                        pool.tensor_tensor(out=h_tok[:, w, :], in0=h_tok[:, w, :], in1=gam_t[:, :],
                                           op=ALU.mult).then_inc(gamma_done, 1)
                        wait(pool, gamma_done, w + 1, apart=pool_passed)
                if some(s, 8):
                    wait(pool, stats1, s + 1, apart=pool_passed)
                    rstd(0, s, q, rstd1, False)

            all_steps(pool, tokens_step, step, 4)

            def turn_rot(bb, c):
                wait(pool, rot_in, 4 * bb + c + 1)
                s = c
                step.done(pool.tensor_tensor(out=rot2[:, s, :], in0=rot2[:, s, :], in1=sin[:, :], op=ALU.mult))
                pool.tensor_tensor(out=rot1[:, s, :], in0=rot1[:, s, :], in1=rot2[:, s, :],
                                   op=ALU.add).then_inc(x_ready, 1)

            def rest1(bb, c):
                wait(pool, p1_ready, 4 * bb + c + 1)
                wait(pool, x_ready, 4 * bb + c + 1)
                s = c
                pool.tensor_tensor(out=rot2[:, s, :], in0=rot1[:, s, :], in1=parts[:, 0, c, :],
                                   op=ALU.subtract).then_inc(r_ready, 1)

            def rest2(bb, c):
                wait(pool, p2_ready, 4 * bb + c + 1)
                s = c
                pool.tensor_tensor(out=parts[:, 2, c, :], in0=rot2[:, s, :], in1=parts[:, 1, c, :],
                                   op=ALU.subtract).then_inc(rot_done, 1)

            def max_parts(bb, g):
                s = g % 2
                wait(pool, s_read, HEADS * bb + 4 * g + 4, apart=pool_passed)
                wait(pool, mt_ready, 4 * bb + g - 1, apart=pool_passed)
                step.done(pool.tensor_scalar(mneg[:, s, :, :], mx[:, s, :, :], -1.0, None, ALU.mult))
                step.done(pool.tensor_copy(mpt[:, s, :, 0, :], mneg[:, s, :, :]))
                step.done(pool.tensor_tensor(out=mres[:, :, :], in0=mneg[:, s, :, :], in1=mpt[:, s, :, 0, :], op=ALU.subtract))
                step.done(pool.tensor_copy(mpt[:, s, :, 1, :], mres[:, :, :]))
                pool.tensor_tensor(out=mpt[:, s, :, 2, :], in0=mres[:, :, :], in1=mpt[:, s, :, 1, :],
                                   op=ALU.subtract).then_inc(mp_ready, 1)

            PER_TURN = 4 + 4 * 4

            def turn(b, par, kind):
                mids = kind in ("first", "loop")
                for c in range(4):
                    if c > 0 and (kind != "first" if c < 3 else kind != "last"):
                        max_parts(*((b, c + 1) if c < 3 else (b + 1, 0)))
                    if mids:
                        turn_rot(b + 2, c)
                        rest1(b + 2, c)
                        if c < 3:
                            rest2(b + 2, c)
                if kind != "last":
                    max_parts(b + 1, 1)
                if mids:
                    rest2(b + 2, 3)
                if kind == "first":
                    pool.tensor_tensor(out=h_tok[:, 0:TILES, :], in0=h_tok[:, 0:TILES, :],
                                       in1=bout[:, :].unsqueeze(1).to_broadcast([P, TILES, D]),
                                       op=ALU.add).then_inc(bias_added, 1)
                    pool.tensor_tensor(out=h_tok[0:B, 16, :], in0=h_tok[0:B, 16, :], in1=bout[0:B, :],
                                       op=ALU.add).then_inc(bias_added, 1)

            pool.wait_ge(xs_ready, TILES)
            pool.memset(qs[SPLIT:P, :, :, :], 0.0).then_inc(init_done, 1)
            pool.wait_ge(init_done, INIT)
            pool.wait_ge(zt_done, 1)
            turn_rot(0, 0)
            turn_rot(0, 1)
            rest1(0, 0)
            rest2(0, 0)
            turn_rot(0, 2)
            rest1(0, 1)
            rest2(0, 1)
            turn_rot(0, 3)
            rest1(0, 2)
            rest2(0, 2)
            rest1(0, 3)
            rest2(0, 3)
            all_turns(pool, turn, step, PER_TURN)

            def norms_step(s, q):
                if some(s - 1, 9):
                    wait(pool, stats4, s, apart=pool_passed)
                    if isinstance(s, int):
                        wait(pool, xa_ready, 2 * (s - 1) - 2)
                    else:
                        wait(pool, xa_ready, 2 * (s - 1) - 2, apart=pool_passed)
                    rstd(1, s - 1, 1 - q, rstd4, True)
                for k in range(2):
                    w = 2 * s + k - 2
                    if some(w, TILES + 1):
                        p = rows(w)
                        wait(pool, u_ready, w + 1, apart=pool_passed)
                        pool.tensor_tensor(out=h_tok[0:p, w, :], in0=h_tok[0:p, w, :], in1=ut[0:p, 2 * (1 - q) + k, :],
                                           op=ALU.add).then_inc(base_ready, 1)
                        wait(pool, base_ready, w + 1, apart=pool_passed)
                if some(s, 9):
                    wait(pool, stats3, s + 1, apart=pool_passed)
                    rstd(0, s, q, rstd3, True)

            all_steps(pool, norms_step, step, 6)

            pool.wait_ge(wp_ready, 1)
            for n in (1, 2):
                pool.tensor_tensor(out=vals[:, :, 3 + n, :], in0=vals[:, :, 2, :],
                                   in1=wpart[:, n, :].unsqueeze(2).to_broadcast([P, 34, SLOTS]),
                                   op=ALU.mult).then_inc(wv_ready, 1)

            pool.wait_ge(route_done, 1)
            pool.wait_ge(xn_out[0], 16 * 10)
            pool.wait_ge(xn_out[1], 16 * 9)
            pool.wait_ge(acc_out, 16 * 3)

            def gather(t, par):
                wait(pool, x_turned, t - 1)
                wait(pool, xg_in[par], 8 * (t - par), apart=pool_passed)
                step.done(pool.tensor_copy(g_idx[:, par, :], gid[:, bass.ds(t, 1)]))
                pool.indirect_dma_start(xg[:, par, :], None, xn_rows[:, :],
                                        bass.IndirectOffsetOnAxis(g_idx[:, par, :], 0)).then_inc(xg_in[par], 16)

            def scatter(t, par):
                wait(pool, y_added, 16 * t, apart=pool_passed)
                step.done(pool.tensor_copy(s_idx[:, par, :], sid[:, bass.ds(t, 1)]))
                wait(pool, y_ready, t + 1, apart=pool_passed)
                pool.indirect_dma_start(acc_rows[:, :], bass.IndirectOffsetOnAxis(s_idx[:, par, :], 0),
                                        yb[:, par, :], None, compute_op=ALU.add).then_inc(y_added, 16)

            for t in range(4):
                gather(t, t % 2)
            for t in range(2):
                gather(t + 4, t)
                scatter(t, t)
            with pool.Fori(0, (SLOTS - 6) // 2, 1) as i:
                step.enter(i, 4)
                for par in range(2):
                    gather(2 * i + par + 6, par)
                    scatter(2 * i + par + 2, par)
                step.leave((SLOTS - 6) // 2)
            for t in range(SLOTS - 4, SLOTS):
                scatter(t, t % 2)

        @block.scalar
        def _(act):
            act.dma_start(eye[:, :], eye_in).then_inc(tok_in, 16)
            act.dma_start(gam_t[:, :], tok_gamma.unsqueeze(0).to_broadcast([P, D])).then_inc(tok_in, 16)
            act.dma_start(h_tok[0:B, 16, :], cls_tok[0].to_broadcast([B, D])).then_inc(tok_in, 16)
            act.dma_start(wq_raw[:, :, :], w_qkv.rearrange("(o p) i -> p o i", p=P)).then_inc(raw_in, 16)
            act.dma_start(wo_in[:, :, :], w_out.rearrange("(o p) i -> p o i", p=P)).then_inc(raw_in, 16)
            act.dma_start(r_raw[:, :], router_w).then_inc(raw_in, 16)
            act.dma_start(tri_f[:, :], tri_in).then_inc(raw_in, 16)
            act.dma_start(tab[:, :], tab_in).then_inc(small_in, 16)
            act.dma_start(cos[:, :], cos_in).then_inc(small_in, 16)
            act.dma_start(sin[:, :], sin_in).then_inc(small_in, 16)
            for dst, src in ((bout, b_out), (gam_f, f_gamma), (bet_f, f_beta)):
                act.dma_start(dst[:, :], src.unsqueeze(0).to_broadcast([P, D])).then_inc(small_in, 16)

            def copy_x(w, par):
                wait(act, tok_turned, w - 1)
                act.activation(xs[:, par, :].rearrange("p (r q) -> p r q", q=PATCH), xin[:, :, w, :],
                               ACT.Copy).then_inc(xs_ready, 1)

            def copy_h(w, par):
                wait(act, tok_proj, w + 1)
                act.activation(h_tok[:, w, :], bank[2 + par][:, 0:D], ACT.Copy).then_inc(h_raw, 1)

            def copy_zt(w, par):
                wait(act, z_turned, w + 1)
                if rows(w) == B:
                    src = bank[4 + par][:, 0:KC * B].rearrange("p (k b) -> p k b", k=KC)
                    act.activation(zt_b[:, :, :, 0], src, ACT.Copy).then_inc(zt_written, 1)
                    return
                src = bank[4 + par][:, 0:D].rearrange("p (k b h) -> p k b h", k=KC, b=B)
                for k in range(KC):
                    last = act.activation(zt_grid[:, k, :, :, w], src[:, k, :, :], ACT.Copy)
                last.then_inc(zt_written, 1)

            def make_z(w, k, q):
                p, slot = rows(w), 2 * q + k
                act.activation(zs[0:p, k, :], h_tok[0:p, w, :], ACT.Identity, bias=nb[1][0:p, slot:slot + 1],
                               scale=rs[1][0:p, slot:slot + 1]).then_inc(z_ready, 1)

            def tokens_step(s, q):
                if some(s - 3, 9):
                    wait(act, rstd2, s - 2)
                for k in range(2):
                    if some(2 * s + k - 6, TILES + 1):
                        make_z(2 * s + k - 6, k, 1 - q)
                for k in range(2):
                    w = 2 * s + k
                    if some(w + 2):
                        copy_x(w + 2, k)
                    if some(w):
                        copy_h(w, k)
                for k in range(2):
                    if some(2 * s + k - 6, TILES + 1):
                        copy_zt(2 * s + k - 6, k)

            act.wait_ge(tok_in, 16 * TOK_DMAS)
            copy_x(0, 0)
            copy_x(1, 1)
            all_steps(act, tokens_step)

            def part1(bb, c):
                wait(act, x_ready, 4 * bb + c + 1)
                if c == 0:
                    wait(act, split_out, 16 * bb)
                act.activation(parts[:, 0, c, :], rot1[:, c, :], ACT.Copy).then_inc(p1_ready, 1)

            def part2(bb, c):
                wait(act, r_ready, 4 * bb + c + 1)
                act.activation(parts[:, 1, c, :], rot2[:, c, :], ACT.Copy).then_inc(p2_ready, 1)

            def copy_z(bb):
                wait(act, v_ready, 3 * bb)
                act.activation(zb[:, :, :], zt_b[:, :, bb, :], ACT.Copy).then_inc(zb_ready, 1)

            def copy_v(bb, par, t):
                wait(act, v_ready, 3 * bb + t + 1)
                wait(act, pv_done, PRE + 4 * (bb - 1))
                dst = vv[0:KT, par, t, :, 0:HD]
                src = m_ps[0:KT, 0:D].rearrange("p (h i) -> p h i", i=HD)
                scale = tab[0:KT, T_VM:T_VM + 1] if t == 2 else 1.0
                act.activation(dst, src, ACT.Copy, scale=scale).then_inc(v_written, 1)

            def copy_mt(bb, g):
                wait(act, mt_ready, 4 * bb + g + 1)
                act.activation(mtb[:, g % 2, :], m_ps[0:12, :].bitcast(BF16)[:, 0:TT], ACT.Copy).then_inc(mt_copied, 1)

            def copy_ob(bb, g):
                wait(act, ob_ready, 4 * bb + g + 1)
                act.activation(at_b[:, g, bb, :], ob[:, 0:TT], ACT.Copy).then_inc(norm_done, 1)

            def turn(b, par, kind):
                mids = kind in ("first", "loop")
                for j in range(HEADS):
                    if kind != "first":
                        n = HEADS * b + j
                        wait(act, st_ready, n + 1)
                        if j % 4 == 0:
                            wait(act, pv_done, PRE + 4 * b + j // 4 - 1)
                        act.activation(pt[0:KT, j % 8, :], st_ps[j % 2][0:KT, 0:3 * TT], ACT.Exp,
                                       scale=1.0 / HD ** 0.5).then_inc(exp_done, 1)
                        if j in (1, 5, 9):
                            copy_mt(b, j // 4 + 1)
                        if j in (3, 7) and has_before(b):
                            copy_ob(b - 1, j // 4 + 2)
                        if j in (11, 15):
                            copy_ob(b, j // 4 - 2)
                    if mids:
                        if j % 4 == 2:
                            part1(b + 2, j // 4)
                        if j % 4 == 3:
                            part2(b + 2, j // 4)
                    if kind != "last":
                        if j in (6, 10, 14):
                            copy_v(b + 1, 1 - par, j // 4 - 1)
                        if j == 13:
                            copy_mt(b + 1, 0)
                    if mids and j == 15:
                        copy_z(b + 2)

            act.wait_ge(init_done, INIT)
            act.wait_ge(zt_done, 1)
            act.wait_ge(pt_cleared, 1)
            act.sem_inc(exp_done, PRE)
            copy_z(0)
            for c in range(4):
                part1(0, c)
                part2(0, c)
            all_turns(act, turn)
            copy_ob(B - 1, 2)
            copy_ob(B - 1, 3)

            def copy_oa(w, par):
                wait(act, op_ready, w - 1)
                if rows(w) == B:
                    act.activation(oa[:, par, :, 0:B], at_b[:, :, :, 0], ACT.Copy).then_inc(oa_ready, 1)
                else:
                    for g in range(4):
                        last = act.activation(oa[:, par, g, :].rearrange("p (b h) -> p b h", b=B),
                                              at_grid[:, g, :, :, w], ACT.Copy)
                    last.then_inc(oa_ready, 1)

            def norm(dst, src, n, slot, p):
                return act.activation(dst, src, ACT.Identity, bias=nb[n][0:p, slot:slot + 1],
                                      scale=rs[n][0:p, slot:slot + 1])

            def norms_step(s, q):
                for k in range(2):
                    w = 2 * s + k - 2
                    if some(w, TILES + 1):
                        p, slot = rows(w), 2 * (1 - q) + k
                        wait(act, rstd3, s)
                        norm(ut[0:p, slot, :], h_tok[0:p, w, :], 0, slot, p).then_inc(u_ready, 1)
                for k in range(2):
                    if some(2 * s + k + 1, TILES + 1):
                        copy_oa(2 * s + k + 1, 1 - k)
                    w = 2 * s + k - 4
                    if some(w, TILES + 1):
                        p, slot = rows(w), 2 * q + k
                        wait(act, rstd4, s - 1)
                        wait(act, xn_out[k], 8 * (w - k))
                        norm(xn[0:p, slot, :], ut[0:p, slot, :], 1, slot, p).then_inc(xa_ready, 1)
                for k in range(2):
                    w = 2 * s + k - 6
                    if some(w, TILES + 1):
                        p, slot = rows(w), 2 * (1 - q) + k
                        wait(act, xn_turned, w + 1)
                        act.dma_start(xn_rows[bass.ds(w * P, p), :], xn[0:p, slot, :]).then_inc(xn_out[k], 16)
                        act.activation(xnt[:, k, :, 0:p], bank[2 + k][:, 0:KC * p].rearrange("p (k q) -> p k q", k=KC),
                                       ACT.Copy).then_inc(xnt_ready, 1)

            act.wait_ge(norm_done, PRE + 4 * B)
            for k in range(2):
                act.sem_inc(xn_out[k], 16)
            copy_oa(0, 0)
            all_steps(act, norms_step)
            act.wait_ge(base_ready, TILES + 1)
            act.dma_start(acc_rows[0:TILES * P].rearrange("(w p) d -> p w d", p=P), h_tok[:, 0:TILES, :]).then_inc(acc_out, 16)
            act.dma_start(acc_rows[TILES * P:ROWS, :], h_tok[0:B, TILES, :]).then_inc(acc_out, 16)
            act.dma_start(acc_rows[ROWS:ROWS + P, :], h_tok[:, 0, :]).then_inc(acc_out, 16)

            act.wait_ge(ro_d, 1)
            act.activation(prob[:, :, :], tmp8[:, :, :], ACT.Exp, scale=1.0 / TEMP).then_inc(ex_ready, 1)

            def copy_xgt(t, par):
                wait(act, x_turned, t + 1)
                act.activation(xgt[:, par, :, :], bank[4][:, 0:D].rearrange("p (k q) -> p k q", k=KC),
                               ACT.Copy).then_inc(xgt_ready, 1)

            def silu(t, par):
                wait(act, g2_ready, t - 1)
                for half in range(2):
                    wait(act, g1_ready, 2 * t + half + 1)
                    act.activation(ht[:, par, half * 4:half * 4 + 4, :],
                                   bank[2 * par + half].rearrange("p (c q) -> p c q", c=4), ACT.Silu).then_inc(silu_done, 1)

            act.wait_ge(list_ready, 1)
            copy_xgt(0, 0)
            tile_pairs(act, 0, SLOTS - 2, lambda t, par: (silu(t, par), copy_xgt(t + 1, 1 - par)))
            silu(SLOTS - 2, 0)
            copy_xgt(SLOTS - 1, 1)
            silu(SLOTS - 1, 1)

        @block.vector
        def _(dve):
            step = Steps(dve, dve_step)
            dve.memset(pt[64:P, :, :], 0.0).then_inc(pt_cleared, 1)
            step.done(dve.memset(wo_raw[:, :, :, :, :], 0.0))
            dve.wait_ge(raw_in, 16 * RAW_DMAS)
            step.done(dve.tensor_copy(trib[:, :], tri_f[:, :]))
            for o in range(KC):
                dve.tensor_copy(wo_raw[:, o, :, :, 0:HD],
                                wo_in[:, o, :].rearrange("p (g j i) -> p g j i", g=4, j=4)).then_inc(raw_ready, 1)
            dve.wait_ge(tok_in, 16 * TOK_DMAS)
            dve.tensor_copy(eyeb[:, :], eye[:, :]).then_inc(raw_ready, 1)
            n = 0
            for o in range(0, 6, 2):
                n += 1
                dve.wait_ge(setup_ready, n)
                dve.tensor_copy(wqkv_t[:, :, o * P:(o + 2) * P].rearrange("p k (o q) -> p o k q", o=2),
                                bank[6 + n % 2].rearrange("p (o k q) -> p o k q", o=2, k=KC)).then_inc(setup_read, 1)
            for g in range(0, 4, 2):
                n += 1
                dve.wait_ge(setup_ready, n)
                dve.tensor_copy(wo_t[:, g:g + 2, :].rearrange("p g d -> p (g d)"),
                                bank[6 + n % 2]).then_inc(setup_read, 1)
            n += 1
            dve.wait_ge(setup_ready, n)
            dve.tensor_copy(r_t[:, :, :], bank[6 + n % 2][:, 0:KC * E].rearrange("p (k e) -> p k e", k=KC)).then_inc(setup_read, 1)

            def copy_xt(w, par):
                wait(dve, tok_turned, w + 1)
                wait(dve, tok_proj, w - 1)
                dve.tensor_copy(xt[:, par, :, :], bank[par][0:FT, 0:3 * P].rearrange("p (c q) -> p c q", c=3)).then_inc(xt_ready, 1)

            def moments(n, pair, q, bn_done, ready):
                wait(dve, bn_done, pair_end(pair), apart=dve_passed)
                for k in range(2):
                    if some(2 * pair + k, TILES + 1):
                        p = rows(2 * pair + k)
                        last = dve.bn_aggr(mv[n][0:p, 2 * q + k, :], bst[n][0:p, 2 * q + k, :])
                last.then_inc(ready, 1)

            def tokens_step(s, q):
                if some(2 * s + 1):
                    copy_xt(2 * s + 1, 1)
                for k in range(2):
                    w = 2 * s + k - 4
                    if some(w, TILES + 1):
                        p = rows(w)
                        wait(dve, gamma_done, w + 1 if p == P else TILES, apart=dve_passed)
                        if p == B:
                            wait(dve, rstd2, s - 3)
                        dve.bn_stats(bst[1][0:p, 2 * q + k, :], h_tok[0:p, w, :]).then_inc(bn2_done, 1)
                if some(s - 2, 9):
                    moments(1, s - 2, q, bn2_done, stats2)
                for k in range(2):
                    w, slot = 2 * s + k - 2, 2 * (1 - q) + k
                    if some(w):
                        wait(dve, rstd1, s)
                        dve.tensor_scalar(h_tok[:, w, :], h_tok[:, w, :], mv[0][:, slot, 0:1], rs[0][:, slot:slot + 1],
                                          ALU.subtract, ALU.mult).then_inc(normed, 1)
                for k in range(2):
                    w = 2 * s + k
                    if some(w):
                        wait(dve, h_raw, w + 1, apart=dve_passed)
                        dve.bn_stats(bst[0][:, 2 * q + k, :], h_tok[:, w, :]).then_inc(bn1_done, 1)
                        if k == 0 and some(w + 2):
                            copy_xt(w + 2, 0)
                if some(s, 8):
                    moments(0, s, q, bn1_done, stats1)

            copy_xt(0, 0)
            all_steps(dve, tokens_step)
            dve.wait_ge(zt_written, TILES + 1)
            dve.tensor_copy(zt_b[:, :, :, NTOK], zt_b[:, :, :, NTOK - 1]).then_inc(zt_done, 1)

            ROTATE = [2 * i + 1 for i in range(8)] + [2 * i for i in range(8)]
            ROTATE = ROTATE + [HD + i for i in ROTATE]

            def rotate(bb, c):
                wait(dve, proj_ready, 4 * bb + c + 1)
                wait(dve, rot_done, 4 * (bb - 1) + c + 1, apart=dve_passed)
                dve.stream_shuffle(rot2[:, c, :], m_ps[:, 0:TT], ROTATE)
                dve.tensor_tensor(out=rot1[:, c, :], in0=m_ps[:, 0:TT], in1=cos[:, :], op=ALU.mult).then_inc(rot_in, 1)

            def maximum(bb, h):
                wait(dve, s_ready, HEADS * bb + h + 1)
                if h % 4 == 0:
                    wait(dve, mp_ready, 4 * bb + h // 4 - 1)
                dve.tensor_reduce(out=mx[:, (h // 4) % 2, :, h % 4],
                                  in_=s_ps[0:KT, 0:3 * TT].rearrange("p (q k) -> p q k", q=3),
                                  op=ALU.max, axis=AX.X).then_inc(s_read, 1)

            def normal(bb, g, stage):
                if stage == 0:
                    wait(dve, pv_done, PRE + 4 * bb + g + 1)
                    dve.transpose(ot[:, :], o_ps[:, 0:OC]).then_inc(o_read, 1)
                elif stage == 1:
                    wait(dve, o_read, PRE + 4 * bb + g + 1)
                    step.done(dve.reciprocal(rec[:, :], ot_b[:, :, HD]))
                elif stage == 2:
                    step.done(dve.tensor_tensor(out=oq_b[:, :, 0:HD], in0=ot_b[:, :, 0:HD],
                                                in1=rec[:, :].unsqueeze(2).to_broadcast([P, OC // 32, HD]),
                                                op=ALU.mult))
                else:
                    wait(dve, norm_done, PRE + 4 * bb + g)
                    dve.transpose(ob[:, :], oq[:, :]).then_inc(ob_ready, 1)

            def turn(b, par, kind):
                for j in range(HEADS):
                    g, stage = (j - 8) // 4, j % 4
                    now = kind != "first" and (g >= 0 or has_before(b))
                    bb = b if g >= 0 else b - 1
                    if now and stage == 0:
                        normal(bb, g % 4, 0)
                    if has_s_kind(kind, j):
                        maximum(*s_of(b, j))
                    if now and stage == 0:
                        normal(bb, g % 4, 1)
                    elif now and stage == 1:
                        normal(bb, g % 4, 2)
                    elif now and stage == 2:
                        normal(bb, g % 4, 3)
                    if kind in ("first", "loop") and j % 4 == 0:
                        rotate(b + 2, j // 4)

            step.done(dve.memset(oq[:, :], 0.0))
            dve.wait_ge(setup_ready, 6)
            step.done(dve.memset(o_ps[:, D:OC], 1.0))
            dve.wait_ge(small_in, 16 * SMALL_DMAS)
            dve.sem_inc(o_read, PRE)
            dve.sem_inc(norm_done, PRE)
            for c in range(4):
                rotate(0, c)
            all_turns(dve, turn, step, 8)
            for g in (2, 3):
                for stage in range(4):
                    normal(B - 1, g, stage)

            def norms_step(s, q):
                for k in range(2):
                    w, slot = 2 * s + k - 2, 2 * (1 - q) + k
                    if some(w, TILES + 1):
                        p = rows(w)
                        wait(dve, u_ready, w + 1, apart=dve_passed)
                        dve.bn_stats(bst[1][0:p, slot, :], ut[0:p, slot, :]).then_inc(bn4_done, 1)
                if some(s - 1, 9):
                    moments(1, s - 1, 1 - q, bn4_done, stats4)
                for k in range(2):
                    w = 2 * s + k
                    if some(w, TILES + 1):
                        p = rows(w)
                        wait(dve, op_ready, w + 1)
                        dve.tensor_tensor(out=h_tok[0:p, w, :], in0=bank[k][0:p, 0:D], in1=h_tok[0:p, w, :],
                                          op=ALU.add).then_inc(h1_ready, 1)
                    w, slot = 2 * s + k - 4, 2 * q + k
                    if some(w, TILES + 1):
                        p = rows(w)
                        wait(dve, xa_ready, w + 1)
                        dve.tensor_tensor(out=xn[0:p, slot, :], in0=xn[0:p, slot, :], in1=gam_f[0:p, :],
                                          op=ALU.mult).then_inc(xg_done, 1)
                    w = 2 * s + k
                    if some(w, TILES + 1):
                        p = rows(w)
                        wait(dve, h1_ready, w + 1, apart=dve_passed)
                        dve.bn_stats(bst[0][0:p, 2 * q + k, :], h_tok[0:p, w, :]).then_inc(bn3_done, 1)
                    w, slot = 2 * s + k - 4, 2 * q + k
                    if some(w, TILES + 1):
                        p = rows(w)
                        wait(dve, xg_done, w + 1)
                        dve.tensor_tensor(out=xn[0:p, slot, :], in0=xn[0:p, slot, :], in1=bet_f[0:p, :],
                                          op=ALU.add).then_inc(xn_ready, 1)
                if some(s, 9):
                    moments(0, s, q, bn3_done, stats3)
                for k in range(2):
                    w = 2 * s + k - 6
                    if some(w, TILES + 1):
                        p = rows(w)
                        wait(dve, lg_ready, w + 1)
                        dve.tensor_copy(lgt[0:p, w, :], bank[4 + k][0:p, 0:E]).then_inc(lg_read, 1)

            dve.sem_inc(lg_read, PRE)
            dve.wait_ge(bias_added, 2)
            all_steps(dve, norms_step)

            def b17(ap):
                return ap.unsqueeze(2).to_broadcast([P, 17, E])

            desc = tab[:, T_DESC:T_DESC + E].unsqueeze(1).to_broadcast([P, 17, E])
            dve.wait_ge(lg_read, PRE + TILES + 1)
            step.done(dve.tensor_reduce(out=col[0][:, :], in_=lgt[:, :, :], op=ALU.max, axis=AX.X))
            dve.tensor_tensor(out=tmp8[:, :, :], in0=lgt[:, :, :], in1=b17(col[0][:, :]), op=ALU.subtract).then_inc(ro_d, 1)
            dve.wait_ge(ex_ready, 1)
            step.done(dve.tensor_reduce(out=col[0][:, :], in_=prob[:, :, :], op=ALU.add, axis=AX.X))
            step.done(dve.reciprocal(col[1][:, :], col[0][:, :]))
            step.done(dve.tensor_tensor(out=prob[:, :, :], in0=prob[:, :, :], in1=b17(col[1][:, :]), op=ALU.mult))
            for k in range(2):
                step.done(dve.tensor_reduce(out=topw[:, k, :], in_=prob[:, :, :], op=ALU.max, axis=AX.X))
                step.done(dve.tensor_tensor(out=tmp8[:, :, :], in0=prob[:, :, :], in1=b17(topw[:, k, :]), op=ALU.is_equal))
                step.done(dve.tensor_tensor(out=tmp8[:, :, :], in0=tmp8[:, :, :], in1=desc, op=ALU.mult))
                step.done(dve.tensor_reduce(out=col[0][:, :], in_=tmp8[:, :, :], op=ALU.max, axis=AX.X))
                step.done(dve.tensor_tensor(out=sel[k][:, :, :], in0=desc, in1=b17(col[0][:, :]), op=ALU.is_equal))
                if k == 0:
                    step.done(dve.scalar_tensor_tensor(out=prob[:, :, :], in0=sel[0][:, :, :], scalar=-4.0,
                                                       in1=prob[:, :, :], op0=ALU.mult, op1=ALU.add))
            step.done(dve.tensor_tensor(out=tmp8[:, :, :], in0=sel[0][:, :, :], in1=sel[1][:, :, :], op=ALU.add))
            dve.tensor_tensor(out=mask[:, :, :], in0=tmp8[:, :, :], in1=b17(tab[:, T_VALID:T_VALID + 17]),
                              op=ALU.mult).then_inc(mask_ready, 1)
            tw = topw[:, :, :].rearrange("p k t -> p (k t)")
            step.done(dve.tensor_copy(wpart[:, 0, :], tw))
            step.done(dve.tensor_tensor(out=wres[:, :], in0=tw, in1=wpart[:, 0, :], op=ALU.subtract))
            step.done(dve.tensor_copy(wpart[:, 1, :], wres[:, :]))
            step.done(dve.tensor_tensor(out=wpart[:, 2, :], in0=wres[:, :], in1=wpart[:, 1, :], op=ALU.subtract))
            dve.wait_ge(rank_ready, 2)
            step.done(dve.tensor_copy(tot[:, :, :], bank[1][:, 0:17 * E].rearrange("p (t e) -> p e t", e=E)))
            step.done(dve.tensor_tensor_scan(cum[:, :, :].rearrange("p e t -> p (e t)"), tab[:, T_RESET:T_END],
                                             tot[:, :, :].rearrange("p e t -> p (e t)"), 0.0, ALU.mult, ALU.add))
            step.done(dve.tensor_tensor(out=tot[:, :, :], in0=cum[:, :, :], in1=tot[:, :, :], op=ALU.subtract))
            step.done(dve.tensor_tensor(out=big17[:, :, :], in0=cum[:, :, 16:17].to_broadcast([P, E, 17]),
                                        in1=tab[:, T_J128:T_J128 + 17].unsqueeze(1).to_broadcast([P, E, 17]), op=ALU.is_gt))
            step.done(dve.tensor_reduce(out=ntl[:, 0, :], in_=big17[:, :, :], op=ALU.add, axis=AX.X))
            step.done(dve.tensor_tensor_scan(ntl[:, 1, :], tab[:, T_VALID:T_VALID + E], ntl[:, 0, :], 0.0, ALU.mult, ALU.add))
            step.done(dve.tensor_tensor(out=ntl[:, 2, :], in0=ntl[:, 1, :], in1=ntl[:, 0, :], op=ALU.subtract))
            step.done(dve.tensor_scalar(ntl[:, 2, :], ntl[:, 2, :], float(P), None, ALU.mult))
            step.done(dve.tensor_tensor(out=posn[:, :, :], in0=bank[0][:, 0:17 * E].rearrange("p (t e) -> p t e", e=E),
                                        in1=tot[:, :, :].rearrange("p e t -> p t e"), op=ALU.add))
            step.done(dve.tensor_tensor(out=posn[:, :, :], in0=posn[:, :, :],
                                        in1=ntl[:, 2:3, :].to_broadcast([P, 17, E]), op=ALU.add))
            for k in range(2):
                step.done(dve.tensor_tensor(out=tmp8[:, :, :], in0=posn[:, :, :], in1=sel[k][:, :, :], op=ALU.mult))
                step.done(dve.tensor_reduce(out=col[2][:, :], in_=tmp8[:, :, :], op=ALU.add, axis=AX.X))
                step.done(dve.tensor_tensor(out=pos2[:, k, :], in0=col[2][:, :], in1=tab[:, T_INV:T_INV + 17], op=ALU.add))
            step.done(dve.tensor_copy(posi[:, :, :], pos2[:, :, :]))
            step.done(dve.tensor_scalar(poa[:, :, :], posi[:, :, :], 7, None, ALU.logical_shift_right))
            step.done(dve.tensor_scalar(pop[:, :, :], posi[:, :, :], P - 1, None, ALU.bitwise_and))
            step.done(dve.tensor_copy(poaf[:, :], poa[:, :, :].rearrange("p k t -> p (k t)")))
            step.done(dve.tensor_copy(popf[:, :], pop[:, :, :].rearrange("p k t -> p (k t)")))

            def b34(ap, n):
                return ap.unsqueeze(2).to_broadcast([P, 34, n])

            dve.tensor_tensor(out=vals[:, :, 2, :], in0=b34(poaf[:, :], SLOTS),
                              in1=tab[:, T_I40:T_I40 + SLOTS].unsqueeze(1).to_broadcast([P, 34, SLOTS]),
                              op=ALU.is_equal).then_inc(wp_ready, 1)
            dve.wait_ge(wp_ready, 1)
            for k in range(2):
                for n, t0 in ((0, T_IDHI), (1, T_IDLO)):
                    dve.tensor_tensor(out=vals[:, 17 * k:17 * k + 17, n, :], in0=vals[:, 17 * k:17 * k + 17, 2, :],
                                      in1=tab[:, t0:t0 + 17].unsqueeze(2).to_broadcast([P, 17, SLOTS]), op=ALU.mult)
            dve.tensor_tensor(out=vals[:, :, 3, :], in0=vals[:, :, 2, :], in1=b34(wpart[:, 0, :], SLOTS), op=ALU.mult)
            dve.wait_ge(xn_out[0], 16 * 10)
            dve.wait_ge(xn_out[1], 16 * 9)
            dve.tensor_tensor(out=ohp[:, :, :], in0=b34(popf[:, :], P),
                              in1=tab[:, T_I128:T_I128 + P].unsqueeze(1).to_broadcast([P, 34, P]),
                              op=ALU.is_equal).then_inc(oh_ready, 1)
            step.done(dve.tensor_tensor(out=ecmp[:, :, :], in0=ntl[0:1, 1:2, :].to_broadcast([1, SLOTS, E]),
                                        in1=tab[0:1, T_I40:T_I40 + SLOTS].unsqueeze(2).to_broadcast([1, SLOTS, E]), op=ALU.is_le))
            step.done(dve.tensor_reduce(out=esum[:, :], in_=ecmp[:, :, :], op=ALU.add, axis=AX.X))
            step.done(dve.tensor_scalar(eid[:, :], esum[:, :], float(E - 1), None, ALU.min))
            dve.wait_ge(list_ready, 1)
            step.done(dve.tensor_copy(lst[:, :, :], bank[2][:, 0:6 * SLOTS].rearrange("p (v s) -> p v s", v=6)))
            step.done(dve.scalar_tensor_tensor(out=lst[:, 0, :], in0=lst[:, 0, :], scalar=float(P), in1=lst[:, 1, :],
                                               op0=ALU.mult, op1=ALU.add))
            step.done(dve.tensor_tensor(out=lwt[:, :], in0=lst[:, 3, :], in1=lst[:, 4, :], op=ALU.add))
            step.done(dve.tensor_tensor(out=lwt[:, :], in0=lwt[:, :], in1=lst[:, 5, :], op=ALU.add))
            step.done(dve.tensor_copy(gid[:, :], lst[:, 0, :]))
            step.done(dve.tensor_scalar(lst[:, 2, :], lst[:, 2, :], -1.0, 1.0, ALU.mult, ALU.add))
            step.done(dve.scalar_tensor_tensor(out=lst[:, 0, :], in0=lst[:, 2, :], scalar=tab[:, T_DUMMY:T_DUMMY + 1],
                                               in1=lst[:, 0, :], op0=ALU.mult, op1=ALU.add))
            dve.tensor_copy(sid[:, :], lst[:, 0, :]).then_inc(route_done, 1)

            def copy_w1(t, par):
                wait(dve, g1_ready, 2 * t - 2)
                e = dve.value_load(eid[0:1, bass.ds(t, 1)], min_val=0, max_val=E - 1)
                for k in range(KC):
                    dve.tensor_copy(w1c[:, par, k, :], w1_sb[:, e, k, :]).then_inc(w1_ready, 1)

            def scale_y(t, par):
                wait(dve, g2_ready, t + 1)
                wait(dve, y_added, 16 * (t - 1))
                dve.tensor_scalar(yb[:, par, :], bank[5 + par][:, 0:D], lwt[:, bass.ds(t, 1)], None, ALU.mult).then_inc(y_ready, 1)

            dve.wait_ge(route_done, 1)
            dve.wait_ge(w_early_in, 16 * len(EARLY))
            dve.wait_ge(w_late_in, 16 * (2 * E - len(EARLY)))
            copy_w1(0, 0)
            copy_w1(1, 1)
            tile_pairs(dve, 0, SLOTS - 2, lambda t, par: (copy_w1(t + 2, par), scale_y(t, par)))
            scale_y(SLOTS - 2, 0)
            scale_y(SLOTS - 1, 1)

        @block.tensor
        def _(pe):
            def mm(out_, lhs, rhs, start, stop):
                return pe.matmul(out_, lhs, rhs, start=start, stop=stop)

            pe.wait_ge(raw_in, 16 * RAW_DMAS)
            pe.wait_ge(tok_in, 16 * TOK_DMAS)
            n = 0
            for o in range(0, 6, 2):
                n += 1
                wait(pe, setup_read, n - 2)
                for a in range(2):
                    for k in range(KC):
                        c0 = (2 * a + k) * P
                        last = pe.transpose(bank[6 + n % 2][:, c0:c0 + P], wq_raw[:, o + a, k * P:(k + 1) * P], eye[:, :])
                last.then_inc(setup_ready, 1)
            pe.wait_ge(raw_ready, 3)
            for g in range(0, 4, 2):
                n += 1
                wait(pe, setup_read, n - 2)
                for a in range(2):
                    for o in range(KC):
                        c0 = (2 * a + o) * P
                        last = pe.transpose(bank[6 + n % 2][:, c0:c0 + P],
                                            wo_raw[:, o, g + a, :, :].rearrange("p j i -> p (j i)"), eye[:, :])
                last.then_inc(setup_ready, 1)
            n += 1
            wait(pe, setup_read, n - 2)
            for k in range(KC):
                last = pe.transpose(bank[6 + n % 2][:, k * E:(k + 1) * E], r_raw[:, k * P:(k + 1) * P], eye[0:E, 0:E])
            last.then_inc(setup_ready, 1)

            def turn_x(w, par):
                wait(pe, xs_ready, w + 1)
                wait(pe, xt_ready, w - 1)
                for c in range(3):
                    last = pe.transpose(bank[par][0:FT, c * P:(c + 1) * P], xs[:, par, CUT[c]:CUT[c] + FT], eye[:, :])
                last.then_inc(tok_turned, 1)

            def project(w, par):
                wait(pe, xt_ready, w + 1)
                wait(pe, h_raw, w - 1)
                for c in range(3):
                    last = mm(bank[2 + par][:, 0:D], xt[:, par, c, :], wt[:, c, :], c == 0, c == 2)
                last.then_inc(tok_proj, 1)

            def turn_z(w, par, p=P):
                wait(pe, z_ready, w + 1)
                for k in range(KC):
                    last = pe.transpose(bank[4 + par][:, k * p:(k + 1) * p], zs[0:p, par, k * P:(k + 1) * P], eye[0:p, 0:p])
                last.then_inc(z_turned, 1)

            def tokens_step(s, q):
                for k in range(2):
                    w = 2 * s + k
                    if some(w + 1):
                        turn_x(w + 1, 1 - k)
                    if some(w):
                        project(w, k)
                    if some(w - 6, TILES + 1):
                        turn_z(w - 6, k, rows(w - 6))

            turn_x(0, 0)
            all_steps(pe, tokens_step)

            def wide(ps, lhs, rhs):
                for t in range(3):
                    l = lhs(t)
                    if t == 1:
                        a = BANK - TT
                        mm(ps[0:KT, TT:BANK], l, rhs[:, 0:a], True, True)
                        mm(ps[0:KT, BANK:2 * TT], l, rhs[:, a:TT], True, True)
                    else:
                        last = mm(ps[0:KT, t * TT:(t + 1) * TT], l, rhs, True, True)
                return last

            def scores(bb, par, h):
                if h == 0:
                    wait(pe, stack_in, 16 * LOADS * (bb + 1))
                wait(pe, s_read, HEADS * bb + h)
                wide(s_ps, lambda t: qs[0:SPLIT, par, h, t * KT:(t + 1) * KT], ks[0:SPLIT, par, h, :]).then_inc(s_ready, 1)

            def scores_t(bb, par, h):
                if h % 4 == 0:
                    wait(pe, mrow_in[h // 4], 16 * MROWS * (bb + 1))
                wait(pe, exp_done, PRE + HEADS * bb + h - 1)
                wide(st_ps[h % 2], lambda t: ks[:, par, h, t * KT:(t + 1) * KT], qs[:, par, h, :]).then_inc(st_ready, 1)

            def weigh(bb, par, g, t):
                if t == 0:
                    wait(pe, exp_done, PRE + HEADS * bb + 4 * g + 4)
                    if g == 0:
                        wait(pe, v_written, 3 * (bb + 1))
                    wait(pe, o_read, PRE + 4 * bb + g)
                for j in range(4):
                    h = 4 * g + j
                    last = mm(o_ps[32 * j:32 * j + 32, 0:TT], vv[:, par, t, h, :],
                              pt[:, h % 8, t * TT:(t + 1) * TT], t == 0, t == 2)
                if t == 2:
                    last.then_inc(pv_done, 1)

            def misc(use, prev):
                _, what, bb, n_ = use
                s_, v_ = read_of(prev)
                wait(pe, s_, v_)
                if what == "p":
                    for k in range(KC):
                        last = mm(m_ps[:, 0:TT], wqkv_t[:, k, n_ * P:(n_ + 1) * P], zt_b[:, k, bb, :], k == 0, k == KC - 1)
                    last.then_inc(proj_ready, 1)
                elif what == "v":
                    wait(pe, zb_ready, bb + 1)
                    for k in range(KC):
                        last = mm(m_ps[0:KT, 0:D], zb[:, k, n_ * KT:(n_ + 1) * KT], wqkv_t[:, k, 2 * D:3 * D], k == 0, k == KC - 1)
                    last.then_inc(v_ready, 1)
                else:
                    wait(pe, mp_ready, 4 * bb + n_ + 1)
                    dst = m_ps[0:12, :].bitcast(BF16)
                    for t in range(3):
                        last = pe.transpose(dst[:, t * KT:(t + 1) * KT],
                                            mpt[:, n_ % 2, t, :, :].rearrange("p r h -> p (r h)"), eyeb[0:KT, 0:KT])
                    last.then_inc(mt_ready, 1)

            def turn(b, par, kind):
                uses = misc_uses(b, kind)
                prev = before(b, kind)
                for j in range(HEADS):
                    if has_s_kind(kind, j):
                        bb, h = s_of(b, j)
                        scores(bb, par if j < LEAD else 1 - par, h)
                    if kind != "first":
                        scores_t(b, par, j)
                        if j % 4 > 0 and j > 4:
                            weigh(b, par, j // 4 - 1, j % 4 - 1)
                        elif j % 4 > 0 and has_before(b):
                            weigh(b - 1, 1 - par, 3, j % 4 - 1)
                    for use in uses:
                        if use[0] == j:
                            misc(use, prev)
                            prev = use

            pe.wait_ge(zt_done, 1)
            prev = None
            for c in range(4):
                use = (0, "p", 0, c)
                if prev is None:
                    pe.wait_ge(setup_read, n)
                    for k in range(KC):
                        last = mm(m_ps[:, 0:TT], wqkv_t[:, k, c * P:(c + 1) * P], zt_b[:, k, 0, :], k == 0, k == KC - 1)
                    last.then_inc(proj_ready, 1)
                else:
                    misc(use, prev)
                prev = use
            pe.wait_ge(init_done, INIT)
            pe.sem_inc(pv_done, PRE)
            all_turns(pe, turn)
            for t in range(3):
                weigh(B - 1, 1, 3, t)

            def out_project(w, par, p=P):
                wait(pe, oa_ready, w + 1)
                wait(pe, h1_ready, w - 1)
                for g2 in range(4):
                    last = mm(bank[par][0:p, 0:D], oa[:, par, g2, 0:p], wo_t[:, g2, :], g2 == 0, g2 == 3)
                last.then_inc(op_ready, 1)

            def turn_xn(w, par, slot, p):
                wait(pe, xn_ready, w + 1)
                for k in range(KC):
                    last = pe.transpose(bank[2 + par][:, k * p:(k + 1) * p], xn[0:p, slot, k * P:(k + 1) * P], eye[0:p, 0:p])
                last.then_inc(xn_turned, 1)

            def logits(w, par, p=P):
                wait(pe, xnt_ready, w + 1)
                wait(pe, lg_read, PRE + w - 1)
                for k in range(KC):
                    last = mm(bank[4 + par][0:p, 0:E], xnt[:, par, k, 0:p], r_t[:, k, :], k == 0, k == KC - 1)
                last.then_inc(lg_ready, 1)

            def norms_step(s, q):
                for k in range(2):
                    w = 2 * s + k
                    if some(w - 6, TILES + 1):
                        turn_xn(w - 6, k, 2 * (1 - q) + k, rows(w - 6))
                    if some(w, TILES + 1):
                        out_project(w, k, rows(w))
                for k in range(2):
                    if some(2 * s + k - 6, TILES + 1):
                        logits(2 * s + k - 6, k, rows(2 * s + k - 6))

            pe.wait_ge(norm_done, PRE + 4 * B)
            all_steps(pe, norms_step)

            pe.wait_ge(mask_ready, 1)
            flat = mask[:, :, :].rearrange("p t e -> p (t e)")
            mm(bank[0][:, 0:17 * E], trib[:, :], flat, True, True).then_inc(rank_ready, 1)
            mm(bank[1][:, 0:17 * E], onesb[:, :], flat, True, True).then_inc(rank_ready, 1)
            pe.wait_ge(oh_ready, 1)
            pe.wait_ge(wv_ready, 2)
            for c in range(34):
                last = mm(bank[2][:, 0:6 * SLOTS], ohp[:, c, :], vals[:, c, :, :].rearrange("p v s -> p (v s)"), c == 0, c == 33)
            last.then_inc(list_ready, 1)

            def turn_g(t, par):
                wait(pe, xg_in[par], 8 * (t - par) + 16)
                wait(pe, xgt_ready, t)
                for k in range(KC):
                    last = pe.transpose(bank[4][:, k * P:(k + 1) * P], xg[:, par, k * P:(k + 1) * P], eye[:, :])
                last.then_inc(x_turned, 1)

            def gemm1(t, par):
                wait(pe, xgt_ready, t + 1)
                wait(pe, w1_ready, KC * (t + 1))
                for half in range(2):
                    wait(pe, silu_done, 2 * t - 3 + half)
                    for c in range(4):
                        for k in range(KC):
                            f0 = (half * 4 + c) * P
                            last = mm(bank[2 * par + half][:, c * P:(c + 1) * P], w1c[:, par, k, f0:f0 + P],
                                      xgt[:, par, k, :], k == 0, k == KC - 1)
                    last.then_inc(g1_ready, 1)

            def gemm2(t, par, e):
                wait(pe, y_ready, t - 1)
                for c in range(F // P):
                    if c % 4 == 0:
                        wait(pe, silu_done, 2 * t + c // 4 + 1)
                    last = mm(bank[5 + par][:, 0:D], ht[:, par, c, :], w2_sb[:, e, c, :], c == 0, c == F // P - 1)
                last.then_inc(g2_ready, 1)

            def expert(t):
                return pe.value_load(eid[0:1, bass.ds(t, 1)], min_val=0, max_val=E - 1)

            pe.wait_ge(route_done, 1)
            pe.wait_ge(w_early_in, 16 * len(EARLY))
            pe.wait_ge(w_late_in, 16 * (2 * E - len(EARLY)))
            turn_g(0, 0)
            gemm1(0, 0)
            turn_g(1, 1)

            def tile(t, par, more):
                e_before = expert(t - 1)
                gemm1(t, par)
                if more:
                    turn_g(t + 1, 1 - par)
                gemm2(t - 1, 1 - par, e_before)

            tile_pairs(pe, 1, SLOTS - 1, lambda t, par: tile(t, par, True))
            tile(SLOTS - 1, 1, False)
            gemm2(SLOTS - 1, 1, expert(SLOTS - 1))


def kernel(x, cls_tok, L0_tok_W, L0_tok_gamma, L0_attn_w_qkv, L0_attn_w_out, L0_attn_b_out, L0_ffn_gamma,
           L0_ffn_beta, L0_ffn_router_w, L0_ffn_W1, L0_ffn_W2):
    import concourse.bacc as _bacc
    from concourse.bass_utils import run_bass_kernel_spmd as _run

    data = dict(x=x, cls_tok=cls_tok, tok_w=L0_tok_W, tok_gamma=L0_tok_gamma, w_qkv=L0_attn_w_qkv,
                w_out=L0_attn_w_out, b_out=L0_attn_b_out, f_gamma=L0_ffn_gamma, f_beta=L0_ffn_beta,
                router_w=L0_ffn_router_w, w1=L0_ffn_W1, w2=L0_ffn_W2)
    data = {k: np.ascontiguousarray(v) for k, v in data.items()}
    data.update(zip(("cos_in", "sin_in", "eye_in", "tri_in", "tab_in"), shape_tables()))
    nc = _bacc.Bacc("TRN2", target_bir_lowering=False, num_devices=1)
    args = {k: nc.dram_tensor(k, v.shape, mybir.dt.from_np(v.dtype), kind="ExternalInput").ap() for k, v in data.items()}
    args["out"] = nc.dram_tensor("out", (B, NTOK, D), F32, kind="ExternalOutput").ap()
    vit_block(nc, **args)
    r = _run(nc, [data], core_ids=[0])
    return r.results[0]["out"]
```

```python
from contextlib import ExitStack

import concourse.bass as bass
import numpy as np
from concourse import mybir

F32 = mybir.dt.float32
BF16 = mybir.dt.bfloat16
I32 = mybir.dt.int32
ALU = mybir.AluOpType
ACT = mybir.ActivationFunctionType
AX = mybir.AxisListType

P = 128
B, C, IMG = 8, 5, 128
PATCH = 8
GRID = IMG // PATCH
D = 256
NTOK = GRID * GRID + 1
ROWS = B * NTOK
HEADS, HD = 16, 16
E, F = 8, 1024
KC = D // P
FT = 107
NFEAT = C * PATCH * PATCH
CUT = [0, FT, NFEAT - FT]
TT = NTOK + 1
OC = (TT + 31) // 32 * 32
KT = TT // 3
BANK = 512
TILES = GRID
EPS = 1e-5
TEMP = 1.5
SLOTS = (2 * ROWS + E * (P - 1)) // P
QPART = [0, 0, 1, 1, 0, 2]
KPART = [0, 1, 0, 1, 2, 0]
SPLIT = HD * len(QPART)
MROWS = 3
LEAD = 8
INIT = 7
PRE = 2
LOADS = 2 * len(QPART)

T_VM, T_DUMMY, T_IDHI, T_IDLO, T_VALID, T_INV, T_DESC, T_J128, T_I128, T_I40, T_RESET = (
    0, 1, 2, 19, 36, 53, 70, 78, 95, 223, 263)
T_END = T_RESET + E * 17


def shape_tables():
    inv = (1.0 / 10000.0 ** (np.arange(0, HD, 2, dtype=np.float32) / np.float32(HD))).astype(np.float32)
    pos = np.minimum(np.arange(TT), NTOK - 1).astype(np.float32)
    ang = (inv[:, None] * pos[None, :]).astype(np.float32)
    lane = np.arange(P) % HD
    cos = np.cos(ang)[lane % (HD // 2)].astype(np.float32)
    sign = np.where(lane < HD // 2, -1.0, 1.0).astype(np.float32)
    sin = (np.sin(ang)[lane % (HD // 2)] * sign[:, None]).astype(np.float32)
    eye = np.eye(P, dtype=np.float32)
    tri = np.triu(np.ones((P, P), np.float32), 1)
    tab = np.zeros((P, T_END), np.float32)
    p = np.arange(P)
    tab[:, T_VM] = p != KT - 1
    tab[:, T_DUMMY] = ROWS + p - 1
    tab[:, T_IDHI:T_IDHI + TILES] = (p // GRID)[:, None]
    tab[:, T_IDLO:T_IDLO + TILES] = (p % GRID * GRID)[:, None] + np.arange(TILES)
    tab[:, T_IDHI + TILES] = B
    tab[:, T_IDLO + TILES] = p
    valid = np.ones((P, 17), np.float32)
    valid[B:, 16] = 0
    tab[:, T_VALID:T_VALID + 17] = valid
    tab[:, T_INV:T_INV + 17] = (1 - valid) * 8192
    tab[:, T_DESC:T_DESC + E] = E - np.arange(E)
    tab[:, T_J128:T_J128 + 17] = np.arange(17) * P
    tab[:, T_I128:T_I128 + P] = np.arange(P)
    tab[:, T_I40:T_I40 + SLOTS] = np.arange(SLOTS)
    tab[:, T_RESET:T_END] = np.tile(np.arange(17) != 0, E)
    return cos, sin, eye, tri, tab


class Steps:

    def __init__(self, eng, sem, apart=None):
        self.eng, self.sem, self.n, self.turn, self.apart = eng, sem, 0, 0, apart

    def done(self, ins, apart=None):
        ins.then_inc(self.sem, 1)
        self.n += 1
        wait(self.eng, self.sem, self.turn + self.n, apart or self.apart)

    def enter(self, turn, per):
        self.turn, self.start, self.per = turn * per, self.n, per

    def leave(self, turns):
        assert self.n - self.start == self.per, (self.n, self.start, self.per)
        self.n, self.turn = self.start + self.per * turns, 0


def wait(eng, sem, value, apart=None):
    if not isinstance(value, int) or value > 0:
        eng.wait_ge(sem, value)
        if apart is not None and not isinstance(value, int):
            eng.sem_inc(apart, 1)


def vit_block(nc, x, cls_tok, tok_w, tok_gamma, w_qkv, w_out, b_out, f_gamma, f_beta, router_w, w1, w2,
              cos_in, sin_in, eye_in, tri_in, tab_in, out):
    ctx = ExitStack()
    base = [(nc.sbuf_base + 63) // 64 * 64]

    def at(name, shape, dt, offset):
        return nc.alloc_sbuf_tensor_at(name, shape, dt, offset=offset)

    def size(shape, dt):
        n = 1
        for s in shape[1:]:
            n *= s
        return (n * (2 if dt == BF16 else 4) + 31) // 32 * 32

    class Region:

        def __init__(self, start):
            self.end = start

        def add(self, name, shape, dt=F32):
            t = at(name, shape, dt, self.end)
            self.end += size(shape, dt)
            return t

    with ctx:
        keep = Region(base[0])
        h_tok = keep.add("h_tok", [P, 17, D])
        eye = keep.add("eye", [P, P])
        eyeb = keep.add("eyeb", [P, P], BF16)
        trib = keep.add("trib", [P, P], BF16)
        onesb = keep.add("onesb", [P, P], BF16)
        tab = keep.add("tab", [P, T_END])
        gam_t = keep.add("gam_t", [P, D])
        bout = keep.add("bout", [P, D])
        gam_f = keep.add("gam_f", [P, D])
        bet_f = keep.add("bet_f", [P, D])
        r_t = keep.add("r_t", [P, KC, E])
        bst = [keep.add(f"bst{n}", [P, 4, 6]) for n in range(2)]
        mv = [keep.add(f"mv{n}", [P, 4, 2]) for n in range(2)]
        rs = [keep.add(f"rs{n}", [P, 4]) for n in range(2)]
        nb = [keep.add(f"nb{n}", [P, 4]) for n in range(2)]
        mhalf = keep.add("mhalf", [P, 2])
        wo_t = keep.add("wo_t", [P, 4, D])
        lwt = keep.add("lwt", [P, SLOTS])
        gid = keep.add("gid", [P, SLOTS], I32)
        sid = keep.add("sid", [P, SLOTS], I32)
        eid = keep.add("eid", [1, SLOTS], I32)
        lgt = keep.add("lgt", [P, 17, E])
        unused = keep.add("unused", [P, 1])
        g_idx = keep.add("g_idx", [P, 2, 1], I32)
        s_idx = keep.add("s_idx", [P, 2, 1], I32)
        ph = Region(keep.end)
        pt = ph.add("pt", [P, 8, 3 * TT])
        wqkv_t = ph.add("wqkv_t", [P, KC, 3 * D])
        cos = ph.add("cos", [P, TT])
        sin = ph.add("sin", [P, TT])
        st = Region(keep.end)
        oa = st.add("oa", [P, 4, 4, P])
        xnt = st.add("xnt", [P, 2, KC, P])
        xn = st.add("xn", [P, 4, D])
        ut = st.add("ut", [P, 4, D])
        assert st.end <= ph.end
        at_start = ph.end
        ao = Region(at_start)
        attn_t = ao.add("attn_t", [P, 4, B * TT])
        su = Region(at_start)
        wq_raw = su.add("wq_raw", [P, 6, D])
        wo_in = su.add("wo_in", [P, KC, D])
        wo_raw = su.add("wo_raw", [P, KC, 4, 4, 32])
        r_raw = su.add("r_raw", [E, D])
        tri_f = su.add("tri_f", [P, P])
        wt = su.add("wt", [FT, 3, D])
        xs = su.add("xs", [P, 2, NFEAT])
        xt = su.add("xt", [FT, 2, 3, P])
        zs = su.add("zs", [P, 2, D])
        assert su.end <= ao.end
        ro = Region(st.end)
        sel = [ro.add(f"sel{k}", [P, 17, E]) for k in range(2)]
        prob = ro.add("prob", [P, 17, E])
        tmp8 = ro.add("tmp8", [P, 17, E])
        col = [ro.add(f"col{k}", [P, 17]) for k in range(3)]
        topw = ro.add("topw", [P, 2, 17])
        mask = ro.add("mask", [P, 17, E], BF16)
        tot = ro.add("tot", [P, E, 17])
        cum = ro.add("cum", [P, E, 17])
        posn = ro.add("posn", [P, 17, E])
        ntl = ro.add("ntl", [P, 3, E])
        big17 = ro.add("big17", [P, E, 17])
        pos2 = ro.add("pos2", [P, 2, 17])
        posi = ro.add("posi", [P, 2, 17], I32)
        poa = ro.add("poa", [P, 2, 17], I32)
        pop = ro.add("pop", [P, 2, 17], I32)
        poaf = ro.add("poaf", [P, 34])
        popf = ro.add("popf", [P, 34])
        wres = ro.add("wres", [P, 34])
        wpart = ro.add("wpart", [P, 3, 34], BF16)
        vals = ro.add("vals", [P, 34, 6, SLOTS], BF16)
        lst = ro.add("lst", [P, 7, SLOTS])
        ecmp = ro.add("ecmp", [1, SLOTS, E])
        esum = ro.add("esum", [1, SLOTS])
        ro2 = Region(keep.end)
        ohp = ro2.add("ohp", [P, 34, P], BF16)
        assert ro2.end <= st.end
        fx = Region(keep.end)
        xg = fx.add("xg", [P, 2, D])
        xgt = fx.add("xgt", [P, 2, KC, P])
        w1c = fx.add("w1c", [P, 2, KC, F])
        ht = fx.add("ht", [P, 2, F // P, P])
        yb = fx.add("yb", [P, 2, D])
        W_EXPERT = KC * F * 4
        w_start = nc.sbuf_usable_end // 64 * 64 - 2 * E * W_EXPERT
        wr = Region(w_start)
        w1_sb = wr.add("w1_sb", [P, E, KC, F])
        w2_sb = wr.add("w2_sb", [P, E, F // P, D])
        assert wr.end <= nc.sbuf_usable_end and max(fx.end, ro.end) <= w_start
        first = -(-(ao.end - w_start) // W_EXPERT)
        EARLY = range(first, first + 3)
        OVER_AO = range(first)
        BEHIND = range(first + 3, E)
        ov = Region(w_start + (first + 3) * W_EXPERT)
        zt = ov.add("zt", [P, KC, B * TT])
        x_at = ov.end
        qs = ov.add("qs", [P, 2, HEADS, TT], BF16)
        parts = ov.add("parts", [P, 3, 4, TT], BF16)
        xin = at("xin", [P, C * PATCH, GRID, PATCH], F32, x_at)
        assert x_at + size([P, C * PATCH, GRID, PATCH], F32) <= ov.end
        ks = ov.add("ks", [P, 2, HEADS, TT], BF16)
        vv = ov.add("vv", [P, 2, 3, HEADS, 32])
        zb = ov.add("zb", [P, KC, TT])
        rot1 = ov.add("rot1", [P, 4, TT])
        rot2 = ov.add("rot2", [P, 4, TT])
        ot = ov.add("ot", [P, OC])
        oq = ov.add("oq", [P, OC])
        ob = ov.add("ob", [P, OC])
        rec = ov.add("rec", [P, OC // 32])
        mx = ov.add("mx", [KT, 2, 3, 4])
        mneg = ov.add("mneg", [KT, 2, 3, 4])
        mres = ov.add("mres", [KT, 3, 4])
        mpt = ov.add("mpt", [KT, 2, 3, 3, 4], BF16)
        mtb = ov.add("mtb", [12, 2, TT], BF16)
        assert ov.end <= nc.sbuf_usable_end

        s_ps = ctx.enter_context(nc.psum_tensor("s_ps", [P, 2 * BANK], F32))
        st_ps = [ctx.enter_context(nc.psum_tensor(f"st_ps{i}", [P, 2 * BANK], F32)) for i in range(2)]
        o_ps = ctx.enter_context(nc.psum_tensor("o_ps", [P, BANK], F32))
        m_ps = ctx.enter_context(nc.psum_tensor("m_ps", [P, BANK], F32))
        bank = [s_ps[:, 0:BANK], s_ps[:, BANK:], st_ps[0][:, 0:BANK], st_ps[0][:, BANK:],
                st_ps[1][:, 0:BANK], st_ps[1][:, BANK:], o_ps[:, :], m_ps[:, :]]

        split_rows = nc.dram_tensor("split_rows", [3, 4, P, TT], BF16).ap()
        xn_rows = nc.dram_tensor("xn_rows", [ROWS, D], F32).ap()
        xn_tiles = xn_rows[0:TILES * P].rearrange("(p w) d -> p w d", w=TILES)

        def sem(name):
            return ctx.enter_context(nc.semaphore(name))

        sp_passed, pool_passed, dve_passed = sem("sp_passed"), sem("pool_passed"), sem("dve_passed")
        tok_in = sem("tok_in")
        raw_in = sem("raw_in")
        small_in = sem("small_in")
        w_early_in = sem("w_early_in")
        w_late_in = sem("w_late_in")
        pool_step, dve_step, act_step = sem("pool_step"), sem("dve_step"), sem("act_step")
        setup_ready = sem("setup_ready")
        setup_read = sem("setup_read")
        raw_ready = sem("raw_ready")
        init_done = sem("init_done")
        pt_cleared, qs_cleared = sem("pt_cleared"), sem("qs_cleared")
        xs_ready, tok_turned, xt_ready, tok_proj, h_raw = (
            sem("xs_ready"), sem("tok_turned"), sem("xt_ready"), sem("tok_proj"), sem("h_raw"))
        bn1_done, bn2_done, normed, gamma_done = sem("bn1_done"), sem("bn2_done"), sem("normed"), sem("gamma_done")
        stats1, stats2, rstd1, rstd2 = sem("stats1"), sem("stats2"), sem("rstd1"), sem("rstd2")
        z_ready, z_turned, zt_written = sem("z_ready"), sem("z_turned"), sem("zt_written")
        zt_done = sem("zt_done")
        proj_ready, rot_in, x_ready, p1_ready, r_ready, p2_ready, rot_done = (
            sem("proj_ready"), sem("rot_in"), sem("x_ready"), sem("p1_ready"), sem("r_ready"),
            sem("p2_ready"), sem("rot_done"))
        o_cleared = sem("o_cleared")
        turned0, sined0 = sem("turned0"), sem("sined0")
        split_out, stack_in = sem("split_out"), sem("stack_in")
        zb_ready, v_ready, v_written = sem("zb_ready"), sem("v_ready"), sem("v_written")
        s_ready, s_read, mp_ready, mt_ready, mt_copied = (
            sem("s_ready"), sem("s_read"), sem("mp_ready"), sem("mt_ready"), sem("mt_copied"))
        mrow_in = [sem(f"mrow_in{g}") for g in range(4)]
        st_ready, exp_done, pv_done, o_read, ob_ready, norm_done = (
            sem("st_ready"), sem("exp_done"), sem("pv_done"), sem("o_read"), sem("ob_ready"), sem("norm_done"))
        bias_added = sem("bias_added")
        oa_ready, op_ready, h1_ready, u_ready, xg_done = (
            sem("oa_ready"), sem("op_ready"), sem("h1_ready"), sem("u_ready"), sem("xg_done"))
        bn3_done, bn4_done = sem("bn3_done"), sem("bn4_done")
        stats3, stats4, rstd3, rstd4 = sem("stats3"), sem("stats4"), sem("rstd3"), sem("rstd4")
        base_ready, xn_ready, xn_turned, xnt_ready, lg_ready, lg_read = (
            sem("base_ready"), sem("xn_ready"), sem("xn_turned"), sem("xnt_ready"), sem("lg_ready"), sem("lg_read"))
        xn_out, res_out = [sem("xn_out0"), sem("xn_out1")], sem("res_out")
        ro_d, ex_ready, mask_ready, rank_ready, oh_ready, wp_ready, wv_ready, list_ready, route_done = (
            sem("ro_d"), sem("ex_ready"), sem("mask_ready"), sem("rank_ready"), sem("oh_ready"),
            sem("wp_ready"), sem("wv_ready"), sem("list_ready"), sem("route_done"))
        xg_in = [sem("xg_in0"), sem("xg_in1")]
        x_turned, xgt_ready, w1_ready, g1_ready, silu_done, g2_ready, y_ready, y_added = (
            sem("x_turned"), sem("xgt_ready"), sem("w1_ready"), sem("g1_ready"), sem("silu_done"),
            sem("g2_ready"), sem("y_ready"), sem("y_added"))
        gid_ready = sem("gid_ready")

        TOK_DMAS = 8 + 3 + 3
        RAW_DMAS = 4
        SMALL_DMAS = 6
        zt_b = zt[:, :, :].rearrange("p k (b t) -> p k b t", t=TT)
        zt_grid = zt_b[:, :, :, 1:NTOK].rearrange("p k b (h w) -> p k b h w", w=GRID)
        at_b = attn_t[:, :, :].rearrange("p g (b t) -> p g b t", t=TT)
        at_grid = at_b[:, :, :, 1:NTOK].rearrange("p g b (h w) -> p g b h w", w=GRID)

        def has_s_kind(kind, j):
            return kind != "first" if j < LEAD else kind != "last"

        def s_of(b, j):
            return (b, j + LEAD) if j < LEAD else (b + 1, j - LEAD)

        def misc_uses(b, kind):
            uses = []
            if kind != "first":
                uses += [(1, "mt", b, 1), (5, "mt", b, 2), (9, "mt", b, 3)]
            if kind == "loop":
                uses += [(0, "p", b + 2, 0), (4, "p", b + 2, 1), (8, "p", b + 2, 2), (12, "p", b + 2, 3)]
            if kind != "last":
                uses += [(13, "mt", b + 1, 0)]
            if kind in ("loop", "short"):
                uses += [(6, "v", b + 1, 0), (10, "v", b + 1, 1), (14, "v", b + 1, 2)]
            return sorted(uses, key=lambda u: u[0])

        def read_of(use):
            _, what, b, n = use
            s, per = {"p": (rot_in, 4), "v": (v_written, 3), "mt": (mt_copied, 4)}[what]
            return s, b * per + n + 1

        def before(b, kind):
            if kind == "first":
                return (0, "v", 0, 2)
            if isinstance(b, int) and b == 0:
                return (13, "mt", 0, 0)
            return (14, "v", b, 2)

        FIRST_BANKS = [[2, 3, 4, 5], [0, 1, 6, 7]]
        PASSES = (B - 4) // 2

        def all_turns(eng, body, step=None, per=0):
            body(-1, 1, "first")
            body(0, 0, "loop")
            with eng.Fori(0, PASSES, 1) as i:
                if step is not None:
                    step.enter(i, 2 * per)
                for par in (1, 0):
                    body(2 * i + (2 - par), par, "loop")
                if step is not None:
                    step.leave(PASSES)
            body(B - 3, 1, "loop")
            body(B - 2, 0, "short")
            body(B - 1, 1, "last")

        def has_before(b):
            return not isinstance(b, int) or b > 0

        STEP0, STEP_PASSES = 3, 2
        W2_AHEAD = 1
        OH_CUTS = ((0, 9), (9, 17), (17, 26), (26, 34))

        def all_steps(eng, body, step=None, per=0):
            for s in range(STEP0):
                body(s, s % 2)
            with eng.Fori(0, STEP_PASSES, 1) as i:
                if step is not None:
                    step.enter(i, 2 * per)
                body(2 * i + STEP0, STEP0 % 2)
                body(2 * i + (STEP0 + 1), (STEP0 + 1) % 2)
                if step is not None:
                    step.leave(STEP_PASSES)
            for s in range(STEP0 + 2 * STEP_PASSES, 12):
                body(s, s % 2)

        def some(w, count=TILES):
            return not isinstance(w, int) or 0 <= w < count

        def rows(w):
            return B if isinstance(w, int) and w == TILES else P

        def pair_end(pair):
            return min(2 * pair + 2, TILES + 1) if isinstance(pair, int) else 2 * pair + 2

        def tile_pairs(eng, t0, t1, body):
            if t0 < 2:
                body(t0, t0 % 2)
                body(t0 + 1, (t0 + 1) % 2)
                t0 += 2
            if t0 < t1:
                with eng.Fori(0, (t1 - t0) // 2, 1) as i:
                    body(2 * i + t0, t0 % 2)
                    body(2 * i + (t0 + 1), (t0 + 1) % 2)

        ot_b = ot[:, :].rearrange("p (c i) -> p c i", i=32)
        oq_b = oq[:, :].rearrange("p (c i) -> p c i", i=32)
        block = ctx.enter_context(nc.Block())

        @block.sync
        def _(sp):
            for b in range(B):
                sp.dma_start(xin[b * GRID:(b + 1) * GRID, :, :, :].rearrange("p (c r) w q -> p c (r w q)", c=C),
                             x[b].rearrange("c (h r) w -> h c (r w)", r=PATCH)).then_inc(tok_in, 16)
            sp.dma_start(wt[:, 0, :], tok_w[0:FT, :]).then_inc(tok_in, 16)
            sp.dma_start(wt[:, 1, :], tok_w[FT:2 * FT, :]).then_inc(tok_in, 16)
            sp.wait_ge(init_done, 1)
            sp.dma_start(wt[1:FT, 2, :], tok_w[2 * FT:NFEAT, :]).then_inc(tok_in, 16)
            w1_v = w1.rearrange("e (k p) f -> p e k f", p=P)
            w2_v = w2.rearrange("e (k p) d -> p e k d", p=P)
            for e in EARLY:
                sp.dma_start(w1_sb[:, e, :, :], w1_v[:, e, :, :]).then_inc(w_early_in, 16)

            def store_split(bb):
                wait(sp, rot_done, 4 * (bb + 1), apart=sp_passed)
                wait(sp, stack_in, 16 * LOADS * bb)
                sp.dma_start(split_rows.rearrange("r c p t -> p r c t"), parts[:, :, :, :]).then_inc(split_out, 16)

            def load_stack(bb, par, cold):
                wait(sp, split_out, 16 * (bb + 1), apart=sp_passed)
                if not cold:
                    wait(sp, st_ready, HEADS * (bb - 1) + 1)
                    wait(sp, s_ready, HEADS * (bb - 1) + 1)
                for dst, c0, pick in ((qs, 0, QPART), (ks, 2, KPART)):
                    src = split_rows[:, c0:c0 + 2, :, :].rearrange("r c (h i) t -> r i (c h) t", i=HD)
                    for r, part in enumerate(pick):
                        sp.dma_start(dst[r * HD:(r + 1) * HD, par, :, :], src[part]).then_inc(stack_in, 16)

            def max_rows(bb, par, g):
                wait(sp, mt_copied, 4 * bb + g + 1)
                for r in range(MROWS):
                    sp.dma_start(qs[SPLIT + r:SPLIT + r + 1, par, 4 * g:4 * g + 4, :],
                                 mtb[4 * r:4 * r + 4, g % 2, :]).then_inc(mrow_in[g], 16)

            def turn(b, par, kind):
                if kind != "first":
                    max_rows(b, par, 1)
                    if kind != "last":
                        load_stack(b + 1, 1 - par, False)
                    max_rows(b, par, 2)
                    max_rows(b, par, 3)
                if kind != "last":
                    max_rows(b + 1, 1 - par, 0)
                if kind == "loop":
                    store_split(b + 2)

            store_split(0)
            load_stack(0, 0, True)
            store_split(1)
            all_turns(sp, turn)

            sp.wait_ge(norm_done, PRE + 4 * B)
            sp.wait_ge(proj_ready, 4 * B)
            for e in BEHIND:
                sp.dma_start(w1_sb[:, e, :, :], w1_v[:, e, :, :]).then_inc(w_late_in, 16)
            for e in range(E):
                if e >= W2_AHEAD:
                    sp.wait_ge(op_ready, 2 * (e - W2_AHEAD) + 2)
                sp.dma_start(w2_sb[:, e, :, :], w2_v[:, e, :, :]).then_inc(w_late_in, 16)
            sp.wait_ge(oa_ready, TILES + 1)
            for e in OVER_AO:
                sp.dma_start(w1_sb[:, e, :, :], w1_v[:, e, :, :]).then_inc(w_late_in, 16)

            sp.wait_ge(base_ready, TILES + 1)
            for b in range(B):
                sp.dma_start(out[b * NTOK + 1:(b + 1) * NTOK, :].rearrange("(h w) d -> h w d", w=GRID),
                             h_tok[b * GRID:(b + 1) * GRID, 0:TILES, :]).then_inc(res_out, 16)
            sp.dma_start(out[0:ROWS, :].rearrange("(b n) d -> b n d", n=NTOK)[:, 0, :],
                         h_tok[0:B, TILES, :]).then_inc(res_out, 16)
            sp.dma_start(out[ROWS:ROWS + P, :], h_tok[:, 0, :]).then_inc(res_out, 16)
            sp.wait_ge(res_out, 16 * (B + 2))
            sp.wait_ge(y_added, 16 * SLOTS)

        @block.gpsimd
        def _(pool):
            step = Steps(pool, pool_step, apart=pool_passed)
            pool.memset(wt[:, 2, :], 0.0).then_inc(init_done, 1)
            for n, (ap, value) in enumerate(((mhalf[:, :], -0.5), (onesb[:, :], 1.0), (ks[SPLIT:P, :, :, :], 1.0),
                                             (vv[:, :, :, :, :], 1.0), (lgt[:, :, :], 0.0))):
                pool.wait_ge(init_done, n + 1)
                pool.memset(ap, value).then_inc(init_done, 1)

            def rstd(n, pair, q, ready, shift):
                p, m = (B, 1) if isinstance(pair, int) and pair == TILES // 2 else (P, 2)
                sl = slice(2 * q, 2 * q + m)
                step.done(pool.tensor_scalar(rs[n][0:p, sl], mv[n][0:p, sl, 1], EPS, None, ALU.add))
                last = pool.tensor_tensor(out=rs[n][0:p, sl], in0=rs[n][0:p, sl], in1=mhalf[0:p, 0:m], op=ALU.pow)
                if shift:
                    step.done(last)
                    step.done(pool.tensor_scalar(nb[n][0:p, sl], mv[n][0:p, sl, 0], -1.0, None, ALU.mult))
                    last = pool.tensor_tensor(out=nb[n][0:p, sl], in0=nb[n][0:p, sl], in1=rs[n][0:p, sl], op=ALU.mult)
                last.then_inc(ready, 1)
                wait(pool, ready, pair + 1, apart=pool_passed)

            def tokens_step(s, q):
                if some(s - 2, 9):
                    wait(pool, stats2, s - 1, apart=pool_passed)
                    if isinstance(s, int):
                        wait(pool, z_ready, 2 * (s - 2) - 2)
                    rstd(1, s - 2, q, rstd2, True)
                for k in range(2):
                    w = 2 * s + k - 2
                    if some(w):
                        wait(pool, normed, w + 1, apart=pool_passed)
                        pool.tensor_tensor(out=h_tok[:, w, :], in0=h_tok[:, w, :], in1=gam_t[:, :],
                                           op=ALU.mult).then_inc(gamma_done, 1)
                        wait(pool, gamma_done, w + 1, apart=pool_passed)
                if some(s, 8):
                    wait(pool, stats1, s + 1, apart=pool_passed)
                    rstd(0, s, q, rstd1, False)

            all_steps(pool, tokens_step, step, 4)

            def turn_rot(bb, c):
                wait(pool, rot_in, 4 * bb + c + 1)
                s = c
                step.done(pool.tensor_tensor(out=rot2[:, s, :], in0=rot2[:, s, :], in1=sin[:, :], op=ALU.mult))
                pool.tensor_tensor(out=rot1[:, s, :], in0=rot1[:, s, :], in1=rot2[:, s, :],
                                   op=ALU.add).then_inc(x_ready, 1)

            def rest1(bb, c):
                wait(pool, p1_ready, 4 * bb + c + 1)
                wait(pool, x_ready, 4 * bb + c + 1)
                s = c
                pool.tensor_tensor(out=rot2[:, s, :], in0=rot1[:, s, :], in1=parts[:, 0, c, :],
                                   op=ALU.subtract).then_inc(r_ready, 1)

            def rest2(bb, c):
                wait(pool, p2_ready, 4 * bb + c + 1)
                s = c
                pool.tensor_tensor(out=parts[:, 2, c, :], in0=rot2[:, s, :], in1=parts[:, 1, c, :],
                                   op=ALU.subtract).then_inc(rot_done, 1)

            def max_parts(bb, g):
                s = g % 2
                wait(pool, s_read, HEADS * bb + 4 * g + 4, apart=pool_passed)
                wait(pool, mt_ready, 4 * bb + g - 1, apart=pool_passed)
                step.done(pool.tensor_scalar(mneg[:, s, :, :], mx[:, s, :, :], -1.0, None, ALU.mult))
                step.done(pool.tensor_copy(mpt[:, s, :, 0, :], mneg[:, s, :, :]))
                step.done(pool.tensor_tensor(out=mres[:, :, :], in0=mneg[:, s, :, :], in1=mpt[:, s, :, 0, :], op=ALU.subtract))
                step.done(pool.tensor_copy(mpt[:, s, :, 1, :], mres[:, :, :]))
                pool.tensor_tensor(out=mpt[:, s, :, 2, :], in0=mres[:, :, :], in1=mpt[:, s, :, 1, :],
                                   op=ALU.subtract).then_inc(mp_ready, 1)

            PER_TURN = 4 + 4 * 4

            def turn(b, par, kind):
                mids = kind == "loop"
                for c in range(4):
                    if c > 0 and (kind != "first" if c < 3 else kind != "last"):
                        max_parts(*((b, c + 1) if c < 3 else (b + 1, 0)))
                    if mids:
                        turn_rot(b + 2, c)
                        rest1(b + 2, c)
                        if c < 3:
                            rest2(b + 2, c)
                if kind != "last":
                    max_parts(b + 1, 1)
                if mids:
                    rest2(b + 2, 3)

            pool.wait_ge(xs_ready, TILES)
            pool.memset(qs[SPLIT:P, 0, :, :].bitcast(F32), 0.0).then_inc(qs_cleared, 1)
            pool.wait_ge(qs_cleared, 1)
            pool.wait_ge(small_in, 16 * SMALL_DMAS)
            pool.tensor_scalar(vv[0:KT, :, 2, :, HD:32], vv[0:KT, :, 2, :, HD:32], tab[0:KT, T_VM:T_VM + 1], None,
                               ALU.mult).then_inc(init_done, 1)
            for bb in range(2):
                for c in range(4):
                    rest1(bb, c)
                    rest2(bb, c)
            all_turns(pool, turn, step, PER_TURN)

            def norms_step(s, q):
                for k in range(2):
                    w = 2 * s + k - 2
                    if some(w, TILES + 1):
                        p = rows(w)
                        wait(pool, u_ready, w + 1, apart=pool_passed)
                        pool.tensor_tensor(out=h_tok[0:p, w, :], in0=h_tok[0:p, w, :], in1=ut[0:p, 2 * (1 - q) + k, :],
                                           op=ALU.add).then_inc(base_ready, 1)
                        wait(pool, base_ready, w + 1, apart=pool_passed)
                if some(s, 9):
                    wait(pool, stats3, s + 1, apart=pool_passed)
                    rstd(0, s, q, rstd3, True)
                if some(s - 1, 9):
                    wait(pool, stats4, s, apart=pool_passed)
                    rstd(1, s - 1, 1 - q, rstd4, False)

            all_steps(pool, norms_step, step, 4)

            for k in range(2):
                half = slice(17 * k, 17 * k + 17)
                pool.wait_ge(wp_ready, k + 1)
                for n in range(3):
                    pool.tensor_tensor(out=vals[:, half, 3 + n, :], in0=vals[:, half, 2, :],
                                       in1=wpart[:, n, half].unsqueeze(2).to_broadcast([P, 17, SLOTS]),
                                       op=ALU.mult).then_inc(wv_ready, 1)

            pool.wait_ge(gid_ready, 1)
            pool.wait_ge(xn_out[0], 16 * 10)
            pool.wait_ge(xn_out[1], 16 * 9)
            pool.wait_ge(res_out, 16 * (B + 2))

            def gather(t, par):
                wait(pool, x_turned, t - 1)
                wait(pool, xg_in[par], 8 * (t - par), apart=pool_passed)
                step.done(pool.tensor_copy(g_idx[:, par, :], gid[:, bass.ds(t, 1)]))
                pool.indirect_dma_start(xg[:, par, :], None, xn_rows[:, :],
                                        bass.IndirectOffsetOnAxis(g_idx[:, par, :], 0)).then_inc(xg_in[par], 16)

            def scatter(t, par):
                wait(pool, y_added, 16 * t, apart=pool_passed)
                step.done(pool.tensor_copy(s_idx[:, par, :], sid[:, bass.ds(t, 1)]))
                wait(pool, y_ready, t + 1, apart=pool_passed)
                pool.indirect_dma_start(out[:, :], bass.IndirectOffsetOnAxis(s_idx[:, par, :], 0),
                                        yb[:, par, :], None, compute_op=ALU.add).then_inc(y_added, 16)

            for t in range(4):
                gather(t, t % 2)
            pool.wait_ge(route_done, 1)
            for t in range(2):
                gather(t + 4, t)
                scatter(t, t)
            with pool.Fori(0, (SLOTS - 6) // 2, 1) as i:
                step.enter(i, 4)
                for par in range(2):
                    gather(2 * i + par + 6, par)
                    scatter(2 * i + par + 2, par)
                step.leave((SLOTS - 6) // 2)
            for t in range(SLOTS - 4, SLOTS):
                scatter(t, t % 2)

        @block.scalar
        def _(act):
            act.dma_start(eye[:, :], eye_in).then_inc(tok_in, 16)
            act.dma_start(gam_t[:, :], tok_gamma.unsqueeze(0).to_broadcast([P, D])).then_inc(tok_in, 16)
            act.dma_start(h_tok[0:B, 16, :], cls_tok[0].to_broadcast([B, D])).then_inc(tok_in, 16)
            act.wait_ge(tok_in, 16 * TOK_DMAS)
            act.dma_start(wq_raw[:, :, :], w_qkv.rearrange("(o p) i -> p o i", p=P)).then_inc(raw_in, 16)
            act.dma_start(tab[:, :], tab_in).then_inc(small_in, 16)
            act.dma_start(cos[:, :], cos_in).then_inc(small_in, 16)
            act.dma_start(sin[:, :], sin_in).then_inc(small_in, 16)
            act.dma_start(wo_in[:, :, :], w_out.rearrange("(o p) i -> p o i", p=P)).then_inc(raw_in, 16)
            act.dma_start(r_raw[:, :], router_w).then_inc(raw_in, 16)
            act.dma_start(tri_f[:, :], tri_in).then_inc(raw_in, 16)
            for dst, src in ((bout, b_out), (gam_f, f_gamma), (bet_f, f_beta)):
                act.dma_start(dst[:, :], src.unsqueeze(0).to_broadcast([P, D])).then_inc(small_in, 16)

            def copy_x(w, par):
                wait(act, tok_turned, w - 1)
                act.activation(xs[:, par, :].rearrange("p (r q) -> p r q", q=PATCH), xin[:, :, w, :],
                               ACT.Copy).then_inc(xs_ready, 1)

            def copy_h(w, par):
                wait(act, tok_proj, w + 1)
                act.activation(h_tok[:, w, :], bank[2 + par][:, 0:D], ACT.Copy).then_inc(h_raw, 1)

            def copy_zt(w, par):
                wait(act, z_turned, w + 1)
                if rows(w) == B:
                    src = bank[4 + par][:, 0:KC * B].rearrange("p (k b) -> p k b", k=KC)
                    act.activation(zt_b[:, :, :, 0], src, ACT.Copy).then_inc(zt_written, 1)
                    return
                src = bank[4 + par][:, 0:D].rearrange("p (k b h) -> p k b h", k=KC, b=B)
                for k in range(KC):
                    last = act.activation(zt_grid[:, k, :, :, w], src[:, k, :, :], ACT.Copy)
                last.then_inc(zt_written, 1)

            def make_z(w, k, q):
                p, slot = rows(w), 2 * q + k
                act.activation(zs[0:p, k, :], h_tok[0:p, w, :], ACT.Identity, bias=nb[1][0:p, slot:slot + 1],
                               scale=rs[1][0:p, slot:slot + 1]).then_inc(z_ready, 1)

            def tokens_step(s, q):
                if some(s - 3, 9):
                    wait(act, rstd2, s - 2)
                for k in range(2):
                    if some(2 * s + k - 6, TILES + 1):
                        make_z(2 * s + k - 6, k, 1 - q)
                for k in range(2):
                    w = 2 * s + k
                    if some(w + 2):
                        copy_x(w + 2, k)
                    if some(w):
                        copy_h(w, k)
                for k in range(2):
                    if some(2 * s + k - 6, TILES + 1):
                        copy_zt(2 * s + k - 6, k)

            copy_x(0, 0)
            copy_x(1, 1)
            all_steps(act, tokens_step)

            def part1(bb, c):
                wait(act, x_ready, 4 * bb + c + 1)
                if c == 0:
                    wait(act, split_out, 16 * bb)
                act.activation(parts[:, 0, c, :], rot1[:, c, :], ACT.Copy).then_inc(p1_ready, 1)

            def part2(bb, c):
                wait(act, r_ready, 4 * bb + c + 1)
                act.activation(parts[:, 1, c, :], rot2[:, c, :], ACT.Copy).then_inc(p2_ready, 1)

            def copy_z(bb):
                wait(act, v_ready, 3 * bb)
                act.activation(zb[:, :, :], zt_b[:, :, bb, :], ACT.Copy).then_inc(zb_ready, 1)

            def copy_v(bb, par, t):
                wait(act, v_ready, 3 * bb + t + 1)
                wait(act, pv_done, PRE + 4 * (bb - 1))
                dst = vv[0:KT, par, t, :, 0:HD]
                src = m_ps[0:KT, 0:D].rearrange("p (h i) -> p h i", i=HD)
                scale = tab[0:KT, T_VM:T_VM + 1] if t == 2 else 1.0
                act.activation(dst, src, ACT.Copy, scale=scale).then_inc(v_written, 1)

            def copy_mt(bb, g):
                wait(act, mt_ready, 4 * bb + g + 1)
                act.activation(mtb[:, g % 2, :], m_ps[0:12, :].bitcast(BF16)[:, 0:TT], ACT.Copy).then_inc(mt_copied, 1)

            def copy_ob(bb, g):
                wait(act, ob_ready, 4 * bb + g + 1)
                act.activation(at_b[:, g, bb, :], ob[:, 0:TT], ACT.Copy).then_inc(norm_done, 1)

            def turn(b, par, kind):
                mids = kind == "loop"
                for j in range(HEADS):
                    if kind != "first":
                        n = HEADS * b + j
                        wait(act, st_ready, n + 1)
                        if j % 4 == 0:
                            wait(act, pv_done, PRE + 4 * b + j // 4 - 1)
                        act.activation(pt[0:KT, j % 8, :], st_ps[j % 2][0:KT, 0:3 * TT], ACT.Exp,
                                       scale=1.0 / HD ** 0.5).then_inc(exp_done, 1)
                        if j in (1, 5, 9):
                            copy_mt(b, j // 4 + 1)
                        if j in (3, 7) and has_before(b):
                            copy_ob(b - 1, j // 4 + 2)
                        if j in (11, 15):
                            copy_ob(b, j // 4 - 2)
                    if mids:
                        if j % 4 == 2:
                            part1(b + 2, j // 4)
                        if j % 4 == 3:
                            part2(b + 2, j // 4)
                    if kind != "last":
                        if j in (6, 10, 14) and kind != "first":
                            copy_v(b + 1, 1 - par, j // 4 - 1)
                        if j == 13:
                            copy_mt(b + 1, 0)
                    if kind in ("first", "loop") and j == 15:
                        copy_z(b + 2)

            act.wait_ge(init_done, INIT)
            act.wait_ge(zt_done, 1)
            act.wait_ge(pt_cleared, 1)
            act.sem_inc(exp_done, PRE)
            copy_z(0)
            for bb in range(2):
                for c in range(4):
                    part1(bb, c)
                    part2(bb, c)
                if bb == 0:
                    for t in range(3):
                        copy_v(0, 0, t)
            all_turns(act, turn)
            copy_ob(B - 1, 2)
            copy_ob(B - 1, 3)

            def copy_oa(w, slot):
                wait(act, op_ready, w - 3)
                if rows(w) == B:
                    act.activation(oa[:, slot, :, 0:B], at_b[:, :, :, 0], ACT.Copy).then_inc(oa_ready, 1)
                else:
                    for g in range(4):
                        last = act.activation(oa[:, slot, g, :].rearrange("p (b h) -> p b h", b=B),
                                              at_grid[:, g, :, :, w], ACT.Copy)
                    last.then_inc(oa_ready, 1)

            def norm(dst, src, n, slot, p):
                return act.activation(dst, src, ACT.Identity, bias=nb[n][0:p, slot:slot + 1],
                                      scale=rs[n][0:p, slot:slot + 1])

            def norms_step(s, q):
                for k in range(2):
                    w = 2 * s + k - 6
                    if some(w, TILES + 1):
                        p, slot = rows(w), 2 * (1 - q) + k
                        wait(act, xn_turned, w + 1)
                        wait(act, xn_out[k], 8 * (w - k) + 16)
                        rows_w = (xn_rows[TILES * P:ROWS, :] if p == B else
                                  xn_tiles[:, bass.ds(w, 1), :].rearrange("p o d -> p (o d)"))
                        act.dma_start(rows_w, xn[0:p, slot, :]).then_inc(xn_out[k], 16)
                        act.activation(xnt[:, k, :, 0:p], bank[2 + k][:, 0:KC * p].rearrange("p (k q) -> p k q", k=KC),
                                       ACT.Copy).then_inc(xnt_ready, 1)
                for k in range(2):
                    w = 2 * s + k - 2
                    if some(w, TILES + 1):
                        p, slot = rows(w), 2 * (1 - q) + k
                        wait(act, rstd3, s)
                        norm(ut[0:p, slot, :], h_tok[0:p, w, :], 0, slot, p).then_inc(u_ready, 1)
                for k in range(2):
                    if some(2 * s + k + 2, TILES + 1):
                        copy_oa(2 * s + k + 2, 2 * (1 - q) + k)

            act.wait_ge(norm_done, PRE + 4 * B)
            for k in range(2):
                act.sem_inc(xn_out[k], 16)
            copy_oa(0, 0)
            copy_oa(1, 1)
            all_steps(act, norms_step)
            act.wait_ge(ro_d, 1)
            act.activation(prob[:, :, :], tmp8[:, :, :], ACT.Exp, scale=1.0 / TEMP).then_inc(ex_ready, 1)
            act.activation(unused[:, :], tab[:, 0:1], ACT.Silu)

            def copy_xgt(t, par):
                wait(act, x_turned, t + 1)
                act.activation(xgt[:, par, :, :], bank[4][:, 0:D].rearrange("p (k q) -> p k q", k=KC),
                               ACT.Copy).then_inc(xgt_ready, 1)

            def silu(t, par):
                wait(act, g2_ready, t - 1)
                for half in range(2):
                    wait(act, g1_ready, 2 * t + half + 1)
                    act.activation(ht[:, par, half * 4:half * 4 + 4, :],
                                   bank[2 * par + half].rearrange("p (c q) -> p c q", c=4), ACT.Silu).then_inc(silu_done, 1)

            act.wait_ge(list_ready, 1)
            copy_xgt(0, 0)
            tile_pairs(act, 0, SLOTS - 2, lambda t, par: (silu(t, par), copy_xgt(t + 1, 1 - par)))
            silu(SLOTS - 2, 0)
            copy_xgt(SLOTS - 1, 1)
            silu(SLOTS - 1, 1)

        @block.vector
        def _(dve):
            step = Steps(dve, dve_step)
            dve.memset(pt[64:P, :, :], 0.0).then_inc(pt_cleared, 1)
            step.done(dve.memset(wo_raw[:, :, :, :, :], 0.0))

            def setup_qkv():
                dve.wait_ge(raw_in, 16 * RAW_DMAS)
                for n in range(3):
                    dve.wait_ge(setup_ready, n + 1)
                    dve.tensor_copy(wqkv_t[:, :, 2 * n * P:(2 * n + 2) * P].rearrange("p k (o q) -> p o k q", o=2),
                                    bank[6 + n % 2].rearrange("p (o k q) -> p o k q", o=2, k=KC)).then_inc(setup_read, 1)

            def setup_out():
                for o in range(KC):
                    dve.tensor_copy(wo_raw[:, o, :, :, 0:HD],
                                    wo_in[:, o, :].rearrange("p (g j i) -> p g j i", g=4, j=4)).then_inc(raw_ready, 1)
                dve.tensor_copy(trib[:, :], tri_f[:, :])
                for n in range(2):
                    dve.wait_ge(setup_ready, n + 4)
                    dve.tensor_copy(wo_t[:, 2 * n:2 * n + 2, :].rearrange("p g d -> p (g d)"),
                                    bank[n]).then_inc(setup_read, 1)
                dve.wait_ge(setup_ready, 6)
                dve.tensor_copy(r_t[:, :, :], bank[0][:, 0:KC * E].rearrange("p (k e) -> p k e", k=KC)).then_inc(setup_read, 1)

            dve.wait_ge(tok_in, 16 * TOK_DMAS)
            dve.tensor_copy(eyeb[:, :], eye[:, :]).then_inc(raw_ready, 1)

            def copy_xt(w, par):
                wait(dve, tok_turned, w + 1)
                wait(dve, tok_proj, w - 1)
                dve.tensor_copy(xt[:, par, :, :], bank[par][0:FT, 0:3 * P].rearrange("p (c q) -> p c q", c=3)).then_inc(xt_ready, 1)

            def moments(n, pair, q, bn_done, ready):
                wait(dve, bn_done, pair_end(pair), apart=dve_passed)
                for k in range(2):
                    if some(2 * pair + k, TILES + 1):
                        p = rows(2 * pair + k)
                        last = dve.bn_aggr(mv[n][0:p, 2 * q + k, :], bst[n][0:p, 2 * q + k, :])
                last.then_inc(ready, 1)

            def tokens_step(s, q):
                if some(2 * s + 1):
                    copy_xt(2 * s + 1, 1)
                for k in range(2):
                    w = 2 * s + k - 4
                    if some(w, TILES + 1):
                        p = rows(w)
                        wait(dve, gamma_done, w + 1 if p == P else TILES, apart=dve_passed)
                        if p == B:
                            wait(dve, rstd2, s - 3)
                        dve.bn_stats(bst[1][0:p, 2 * q + k, :], h_tok[0:p, w, :]).then_inc(bn2_done, 1)
                if some(s - 2, 9):
                    moments(1, s - 2, q, bn2_done, stats2)
                for k in range(2):
                    w, slot = 2 * s + k - 2, 2 * (1 - q) + k
                    if some(w):
                        wait(dve, rstd1, s)
                        dve.tensor_scalar(h_tok[:, w, :], h_tok[:, w, :], mv[0][:, slot, 0:1], rs[0][:, slot:slot + 1],
                                          ALU.subtract, ALU.mult).then_inc(normed, 1)
                for k in range(2):
                    w = 2 * s + k
                    if some(w):
                        wait(dve, h_raw, w + 1, apart=dve_passed)
                        dve.bn_stats(bst[0][:, 2 * q + k, :], h_tok[:, w, :]).then_inc(bn1_done, 1)
                        if k == 0 and some(w + 2):
                            copy_xt(w + 2, 0)
                if some(s, 8):
                    moments(0, s, q, bn1_done, stats1)
                if isinstance(s, int) and s == 8:
                    setup_qkv()

            copy_xt(0, 0)
            all_steps(dve, tokens_step)
            dve.wait_ge(zt_written, TILES + 1)
            dve.tensor_copy(zt_b[:, :, :, NTOK], zt_b[:, :, :, NTOK - 1]).then_inc(zt_done, 1)

            ROTATE = [2 * i + 1 for i in range(8)] + [2 * i for i in range(8)]
            ROTATE = ROTATE + [HD + i for i in ROTATE]

            def rotate(bb, c):
                wait(dve, proj_ready, 4 * bb + c + 1)
                wait(dve, rot_done, 4 * (bb - 1) + c + 1, apart=dve_passed)
                dve.stream_shuffle(rot2[:, c, :], m_ps[:, 0:TT], ROTATE)
                dve.tensor_tensor(out=rot1[:, c, :], in0=m_ps[:, 0:TT], in1=cos[:, :], op=ALU.mult).then_inc(rot_in, 1)

            def maximum(bb, h):
                wait(dve, s_ready, HEADS * bb + h + 1)
                if h % 4 == 0:
                    wait(dve, mp_ready, 4 * bb + h // 4 - 1)
                ps = st_ps[0] if isinstance(bb, int) and bb == 0 and h < LEAD and h % 2 else s_ps
                dve.tensor_reduce(out=mx[:, (h // 4) % 2, :, h % 4],
                                  in_=ps[0:KT, 0:3 * TT].rearrange("p (q k) -> p q k", q=3),
                                  op=ALU.max, axis=AX.X).then_inc(s_read, 1)

            def normal(bb, g, stage):
                if stage == 0:
                    wait(dve, pv_done, PRE + 4 * bb + g + 1)
                    dve.transpose(ot[:, :], o_ps[:, 0:OC]).then_inc(o_read, 1)
                elif stage == 1:
                    wait(dve, o_read, PRE + 4 * bb + g + 1)
                    step.done(dve.reciprocal(rec[:, :], ot_b[:, :, HD]))
                elif stage == 2:
                    step.done(dve.tensor_tensor(out=oq_b[:, :, 0:HD], in0=ot_b[:, :, 0:HD],
                                                in1=rec[:, :].unsqueeze(2).to_broadcast([P, OC // 32, HD]),
                                                op=ALU.mult))
                else:
                    wait(dve, norm_done, PRE + 4 * bb + g)
                    dve.transpose(ob[:, :], oq[:, :]).then_inc(ob_ready, 1)

            def turn(b, par, kind):
                for j in range(HEADS):
                    g, stage = (j - 8) // 4, j % 4
                    now = kind != "first" and (g >= 0 or has_before(b))
                    bb = b if g >= 0 else b - 1
                    if now and stage == 0:
                        normal(bb, g % 4, 0)
                    if has_s_kind(kind, j):
                        maximum(*s_of(b, j))
                    if now and stage == 0:
                        normal(bb, g % 4, 1)
                    elif now and stage == 1:
                        normal(bb, g % 4, 2)
                    elif now and stage == 2:
                        normal(bb, g % 4, 3)
                    if kind == "loop" and j % 4 == 0:
                        rotate(b + 2, j // 4)

            step.done(dve.memset(oq[:, :], 0.0))
            dve.memset(o_ps[:, D:OC], 1.0).then_inc(o_cleared, 1)
            dve.wait_ge(small_in, 16 * SMALL_DMAS)
            dve.sem_inc(o_read, PRE)
            dve.sem_inc(norm_done, PRE)
            for bb in range(2):
                for i in range(6):
                    n = 4 * bb + i
                    if i < 4:
                        src = bank[FIRST_BANKS[bb][i]][:, 0:TT]
                        dve.wait_ge(proj_ready, n + 1)
                        wait(dve, rot_done, n - 3)
                        dve.stream_shuffle(rot2[:, i, :], src, ROTATE).then_inc(turned0, 1)
                        dve.tensor_tensor(out=rot1[:, i, :], in0=src, in1=cos[:, :], op=ALU.mult).then_inc(rot_in, 1)
                    if 1 <= i < 5:
                        dve.wait_ge(turned0, n)
                        dve.tensor_tensor(out=rot2[:, i - 1, :], in0=rot2[:, i - 1, :], in1=sin[:, :],
                                          op=ALU.mult).then_inc(sined0, 1)
                    if i >= 2:
                        dve.wait_ge(sined0, n - 1)
                        dve.wait_ge(rot_in, n - 1)
                        dve.tensor_tensor(out=rot1[:, i - 2, :], in0=rot1[:, i - 2, :], in1=rot2[:, i - 2, :],
                                          op=ALU.add).then_inc(x_ready, 1)
            dve.tensor_tensor(out=h_tok[:, 0:TILES, :], in0=h_tok[:, 0:TILES, :],
                              in1=bout[:, :].unsqueeze(1).to_broadcast([P, TILES, D]),
                              op=ALU.add).then_inc(bias_added, 1)
            dve.tensor_tensor(out=h_tok[0:B, 16, :], in0=h_tok[0:B, 16, :], in1=bout[0:B, :],
                              op=ALU.add).then_inc(bias_added, 1)
            dve.memset(qs[SPLIT:P, 1, :, :].bitcast(F32), 0.0).then_inc(qs_cleared, 1)
            setup_out()
            all_turns(dve, turn, step, 8)
            for g in (2, 3):
                for stage in range(4):
                    normal(B - 1, g, stage)

            def norms_step(s, q):
                for k in range(2):
                    w = 2 * s + k
                    if some(w, TILES + 1):
                        p = rows(w)
                        wait(dve, op_ready, w + 1)
                        dve.tensor_tensor(out=h_tok[0:p, w, :], in0=bank[k][0:p, 0:D], in1=h_tok[0:p, w, :],
                                          op=ALU.add).then_inc(h1_ready, 1)
                    w, slot = 2 * s + k - 4, 2 * q + k
                    if some(w, TILES + 1):
                        p = rows(w)
                        wait(dve, xn_out[k], 8 * (w - k))
                        dve.wait_ge(stats4, s - 1)
                        dve.scalar_tensor_tensor(out=xn[0:p, slot, :], in0=ut[0:p, slot, :], scalar=mv[1][0:p, slot, 0:1],
                                                 in1=gam_f[0:p, :], op0=ALU.subtract, op1=ALU.mult).then_inc(xg_done, 1)
                    w = 2 * s + k
                    if some(w, TILES + 1):
                        p = rows(w)
                        wait(dve, h1_ready, w + 1, apart=dve_passed)
                        dve.bn_stats(bst[0][0:p, 2 * q + k, :], h_tok[0:p, w, :]).then_inc(bn3_done, 1)
                    w, slot = 2 * s + k - 4, 2 * q + k
                    if some(w, TILES + 1):
                        p = rows(w)
                        wait(dve, xg_done, w + 1)
                        wait(dve, rstd4, s - 1)
                        dve.scalar_tensor_tensor(out=xn[0:p, slot, :], in0=xn[0:p, slot, :], scalar=rs[1][0:p, slot:slot + 1],
                                                 in1=bet_f[0:p, :], op0=ALU.mult, op1=ALU.add).then_inc(xn_ready, 1)
                if some(s, 9):
                    moments(0, s, q, bn3_done, stats3)
                for k in range(2):
                    w, slot = 2 * s + k - 2, 2 * (1 - q) + k
                    if some(w, TILES + 1):
                        p = rows(w)
                        wait(dve, u_ready, w + 1, apart=dve_passed)
                        dve.bn_stats(bst[1][0:p, slot, :], ut[0:p, slot, :]).then_inc(bn4_done, 1)
                if some(s - 1, 9):
                    moments(1, s - 1, 1 - q, bn4_done, stats4)
                for k in range(2):
                    w = 2 * s + k - 6
                    if some(w, TILES + 1):
                        p = rows(w)
                        wait(dve, lg_ready, w + 1)
                        dve.tensor_copy(lgt[0:p, w, :], bank[4 + k][0:p, 0:E]).then_inc(lg_read, 1)

            dve.sem_inc(lg_read, PRE)
            dve.wait_ge(bias_added, 2)
            all_steps(dve, norms_step)

            def b17(ap):
                return ap.unsqueeze(2).to_broadcast([P, 17, E])

            desc = tab[:, T_DESC:T_DESC + E].unsqueeze(1).to_broadcast([P, 17, E])
            dve.wait_ge(lg_read, PRE + TILES + 1)
            step.done(dve.tensor_reduce(out=col[0][:, :], in_=lgt[:, :, :], op=ALU.max, axis=AX.X))
            dve.tensor_tensor(out=tmp8[:, :, :], in0=lgt[:, :, :], in1=b17(col[0][:, :]), op=ALU.subtract).then_inc(ro_d, 1)
            dve.wait_ge(ex_ready, 1)
            step.done(dve.tensor_reduce(out=col[0][:, :], in_=prob[:, :, :], op=ALU.add, axis=AX.X))
            step.done(dve.reciprocal(col[1][:, :], col[0][:, :]))
            step.done(dve.tensor_tensor(out=prob[:, :, :], in0=prob[:, :, :], in1=b17(col[1][:, :]), op=ALU.mult))
            for k in range(2):
                step.done(dve.tensor_reduce(out=topw[:, k, :], in_=prob[:, :, :], op=ALU.max, axis=AX.X))
                step.done(dve.tensor_tensor(out=tmp8[:, :, :], in0=prob[:, :, :], in1=b17(topw[:, k, :]), op=ALU.is_equal))
                step.done(dve.tensor_tensor(out=tmp8[:, :, :], in0=tmp8[:, :, :], in1=desc, op=ALU.mult))
                step.done(dve.tensor_reduce(out=col[0][:, :], in_=tmp8[:, :, :], op=ALU.max, axis=AX.X))
                step.done(dve.tensor_tensor(out=sel[k][:, :, :], in0=desc, in1=b17(col[0][:, :]), op=ALU.is_equal))
                if k == 0:
                    step.done(dve.scalar_tensor_tensor(out=prob[:, :, :], in0=sel[0][:, :, :], scalar=-4.0,
                                                       in1=prob[:, :, :], op0=ALU.mult, op1=ALU.add))
            step.done(dve.tensor_tensor(out=tmp8[:, :, :], in0=sel[0][:, :, :], in1=sel[1][:, :, :], op=ALU.add))
            dve.tensor_tensor(out=mask[:, :, :], in0=tmp8[:, :, :], in1=b17(tab[:, T_VALID:T_VALID + 17]),
                              op=ALU.mult).then_inc(mask_ready, 1)
            tw = topw[:, :, :].rearrange("p k t -> p (k t)")
            step.done(dve.tensor_copy(wpart[:, 0, :], tw))
            step.done(dve.tensor_tensor(out=wres[:, :], in0=tw, in1=wpart[:, 0, :], op=ALU.subtract))
            step.done(dve.tensor_copy(wpart[:, 1, :], wres[:, :]))
            step.done(dve.tensor_tensor(out=wpart[:, 2, :], in0=wres[:, :], in1=wpart[:, 1, :], op=ALU.subtract))
            dve.wait_ge(rank_ready, 2)
            step.done(dve.tensor_copy(tot[:, :, :], bank[1][:, 0:17 * E].rearrange("p (t e) -> p e t", e=E)))
            step.done(dve.tensor_tensor_scan(cum[:, :, :].rearrange("p e t -> p (e t)"), tab[:, T_RESET:T_END],
                                             tot[:, :, :].rearrange("p e t -> p (e t)"), 0.0, ALU.mult, ALU.add))
            step.done(dve.tensor_tensor(out=tot[:, :, :], in0=cum[:, :, :], in1=tot[:, :, :], op=ALU.subtract))
            step.done(dve.tensor_tensor(out=big17[:, :, :], in0=cum[:, :, 16:17].to_broadcast([P, E, 17]),
                                        in1=tab[:, T_J128:T_J128 + 17].unsqueeze(1).to_broadcast([P, E, 17]), op=ALU.is_gt))
            step.done(dve.tensor_reduce(out=ntl[:, 0, :], in_=big17[:, :, :], op=ALU.add, axis=AX.X))
            step.done(dve.tensor_tensor_scan(ntl[:, 1, :], tab[:, T_VALID:T_VALID + E], ntl[:, 0, :], 0.0, ALU.mult, ALU.add))
            step.done(dve.tensor_tensor(out=ntl[:, 2, :], in0=ntl[:, 1, :], in1=ntl[:, 0, :], op=ALU.subtract))
            step.done(dve.tensor_scalar(ntl[:, 2, :], ntl[:, 2, :], float(P), None, ALU.mult))
            step.done(dve.tensor_tensor(out=posn[:, :, :], in0=bank[0][:, 0:17 * E].rearrange("p (t e) -> p t e", e=E),
                                        in1=tot[:, :, :].rearrange("p e t -> p t e"), op=ALU.add))
            step.done(dve.tensor_tensor(out=posn[:, :, :], in0=posn[:, :, :],
                                        in1=ntl[:, 2:3, :].to_broadcast([P, 17, E]), op=ALU.add))
            for k in range(2):
                step.done(dve.tensor_tensor(out=tmp8[:, :, :], in0=posn[:, :, :], in1=sel[k][:, :, :], op=ALU.mult))
                step.done(dve.tensor_reduce(out=col[2][:, :], in_=tmp8[:, :, :], op=ALU.add, axis=AX.X))
                step.done(dve.tensor_tensor(out=pos2[:, k, :], in0=col[2][:, :], in1=tab[:, T_INV:T_INV + 17], op=ALU.add))
            step.done(dve.tensor_copy(posi[:, :, :], pos2[:, :, :]))
            step.done(dve.tensor_scalar(poa[:, :, :], posi[:, :, :], 7, None, ALU.logical_shift_right))
            step.done(dve.tensor_scalar(pop[:, :, :], posi[:, :, :], P - 1, None, ALU.bitwise_and))
            step.done(dve.tensor_copy(poaf[:, :], poa[:, :, :].rearrange("p k t -> p (k t)")))
            step.done(dve.tensor_copy(popf[:, :], pop[:, :, :].rearrange("p k t -> p (k t)")))

            def b17n(ap, n):
                return ap.unsqueeze(2).to_broadcast([P, 17, n])

            dve.wait_ge(xn_out[0], 16 * 10)
            dve.wait_ge(xn_out[1], 16 * 9)
            halves = [slice(17 * k, 17 * k + 17) for k in range(2)]
            for half in halves:
                dve.tensor_tensor(out=vals[:, half, 2, :], in0=b17n(poaf[:, half], SLOTS),
                                  in1=tab[:, T_I40:T_I40 + SLOTS].unsqueeze(1).to_broadcast([P, 17, SLOTS]),
                                  op=ALU.is_equal).then_inc(wp_ready, 1)
            for k, half in enumerate(halves):
                dve.wait_ge(wp_ready, k + 1)
                for n, src in ((0, tab[:, T_IDHI:T_IDHI + 17]), (1, tab[:, T_IDLO:T_IDLO + 17])):
                    dve.tensor_tensor(out=vals[:, half, n, :], in0=vals[:, half, 2, :], in1=b17n(src, SLOTS), op=ALU.mult)
                for c0, c1 in OH_CUTS[2 * k:2 * k + 2]:
                    dve.tensor_tensor(out=ohp[:, c0:c1, :], in0=popf[:, c0:c1].unsqueeze(2).to_broadcast([P, c1 - c0, P]),
                                      in1=tab[:, T_I128:T_I128 + P].unsqueeze(1).to_broadcast([P, c1 - c0, P]),
                                      op=ALU.is_equal).then_inc(oh_ready, 1)
            step.done(dve.tensor_tensor(out=ecmp[:, :, :], in0=ntl[0:1, 1:2, :].to_broadcast([1, SLOTS, E]),
                                        in1=tab[0:1, T_I40:T_I40 + SLOTS].unsqueeze(2).to_broadcast([1, SLOTS, E]), op=ALU.is_le))
            step.done(dve.tensor_reduce(out=esum[:, :], in_=ecmp[:, :, :], op=ALU.add, axis=AX.X))
            step.done(dve.tensor_scalar(eid[:, :], esum[:, :], float(E - 1), None, ALU.min))
            dve.wait_ge(list_ready, 1)
            step.done(dve.tensor_copy(lst[:, 0:6, :], bank[2][:, 0:6 * SLOTS].rearrange("p (v s) -> p v s", v=6)))
            hi, lo, used, row = lst[:, 0, :], lst[:, 1, :], lst[:, 2, :], lst[:, 6, :]
            step.done(dve.scalar_tensor_tensor(out=row, in0=hi, scalar=float(GRID * GRID), in1=lo,
                                               op0=ALU.mult, op1=ALU.add))
            dve.tensor_copy(gid[:, :], row).then_inc(gid_ready, 1)
            step.done(dve.tensor_tensor(out=lwt[:, :], in0=lst[:, 3, :], in1=lst[:, 4, :], op=ALU.add))
            step.done(dve.tensor_tensor(out=lwt[:, :], in0=lwt[:, :], in1=lst[:, 5, :], op=ALU.add))
            step.done(dve.scalar_tensor_tensor(out=row, in0=row, scalar=1.0, in1=hi, op0=ALU.add, op1=ALU.add))
            step.done(dve.tensor_scalar(lst[:, 4, :], lo, float(GRID * GRID), -float(ROWS + 1), ALU.mult, ALU.add))
            step.done(dve.scalar_tensor_tensor(out=lst[:, 5, :], in0=hi, scalar=float(B), in1=lst[:, 4, :],
                                               op0=ALU.is_ge, op1=ALU.mult))
            step.done(dve.tensor_tensor(out=row, in0=row, in1=lst[:, 5, :], op=ALU.add))
            step.done(dve.tensor_scalar(used, used, -1.0, 1.0, ALU.mult, ALU.add))
            step.done(dve.scalar_tensor_tensor(out=row, in0=used, scalar=tab[:, T_DUMMY:T_DUMMY + 1],
                                               in1=row, op0=ALU.mult, op1=ALU.add))
            dve.tensor_copy(sid[:, :], row).then_inc(route_done, 1)

            def copy_w1(t, par):
                wait(dve, g1_ready, 2 * t - 2)
                e = dve.value_load(eid[0:1, bass.ds(t, 1)], min_val=0, max_val=E - 1)
                for k in range(KC):
                    dve.tensor_copy(w1c[:, par, k, :], w1_sb[:, e, k, :]).then_inc(w1_ready, 1)

            def scale_y(t, par):
                wait(dve, g2_ready, t + 1)
                wait(dve, y_added, 16 * (t - 1))
                dve.tensor_scalar(yb[:, par, :], bank[5 + par][:, 0:D], lwt[:, bass.ds(t, 1)], None, ALU.mult).then_inc(y_ready, 1)

            dve.wait_ge(route_done, 1)
            dve.wait_ge(w_early_in, 16 * len(EARLY))
            dve.wait_ge(w_late_in, 16 * (2 * E - len(EARLY)))
            copy_w1(0, 0)
            copy_w1(1, 1)
            tile_pairs(dve, 0, SLOTS - 2, lambda t, par: (copy_w1(t + 2, par), scale_y(t, par)))
            scale_y(SLOTS - 2, 0)
            scale_y(SLOTS - 1, 1)

        @block.tensor
        def _(pe):
            def mm(out_, lhs, rhs, start, stop):
                return pe.matmul(out_, lhs, rhs, start=start, stop=stop)

            def setup_qkv():
                pe.wait_ge(raw_in, 16 * RAW_DMAS)
                for n in range(3):
                    wait(pe, setup_read, n - 1)
                    for a in range(2):
                        for k in range(KC):
                            c0 = (2 * a + k) * P
                            last = pe.transpose(bank[6 + n % 2][:, c0:c0 + P], wq_raw[:, 2 * n + a, k * P:(k + 1) * P], eye[:, :])
                    last.then_inc(setup_ready, 1)

            def setup_out():
                pe.wait_ge(raw_ready, 3)
                for n in range(2):
                    for a in range(2):
                        for o in range(KC):
                            c0 = (2 * a + o) * P
                            last = pe.transpose(bank[n][:, c0:c0 + P],
                                                wo_raw[:, o, 2 * n + a, :, :].rearrange("p j i -> p (j i)"), eye[:, :])
                    last.then_inc(setup_ready, 1)
                pe.wait_ge(setup_read, 4)
                for k in range(KC):
                    last = pe.transpose(bank[0][:, k * E:(k + 1) * E], r_raw[:, k * P:(k + 1) * P], eye[0:E, 0:E])
                last.then_inc(setup_ready, 1)
                pe.wait_ge(setup_read, 6)

            def turn_x(w, par):
                wait(pe, xs_ready, w + 1)
                wait(pe, xt_ready, w - 1)
                for c in range(3):
                    last = pe.transpose(bank[par][0:FT, c * P:(c + 1) * P], xs[:, par, CUT[c]:CUT[c] + FT], eye[:, :])
                last.then_inc(tok_turned, 1)

            def project(w, par):
                wait(pe, xt_ready, w + 1)
                wait(pe, h_raw, w - 1)
                for c in range(3):
                    last = mm(bank[2 + par][:, 0:D], xt[:, par, c, :], wt[:, c, :], c == 0, c == 2)
                last.then_inc(tok_proj, 1)

            def turn_z(w, par, p=P):
                wait(pe, z_ready, w + 1)
                for k in range(KC):
                    last = pe.transpose(bank[4 + par][:, k * p:(k + 1) * p], zs[0:p, par, k * P:(k + 1) * P], eye[0:p, 0:p])
                last.then_inc(z_turned, 1)

            def tokens_step(s, q):
                for k in range(2):
                    w = 2 * s + k
                    if some(w + 1):
                        turn_x(w + 1, 1 - k)
                    if some(w):
                        project(w, k)
                    if some(w - 6, TILES + 1):
                        turn_z(w - 6, k, rows(w - 6))
                if isinstance(s, int) and s == 8:
                    setup_qkv()

            pe.wait_ge(tok_in, 16 * TOK_DMAS)
            turn_x(0, 0)
            all_steps(pe, tokens_step)

            def wide(ps, lhs, rhs):
                for t in range(3):
                    l = lhs(t)
                    if t == 1:
                        a = BANK - TT
                        mm(ps[0:KT, TT:BANK], l, rhs[:, 0:a], True, True)
                        mm(ps[0:KT, BANK:2 * TT], l, rhs[:, a:TT], True, True)
                    else:
                        last = mm(ps[0:KT, t * TT:(t + 1) * TT], l, rhs, True, True)
                return last

            def scores(bb, par, h):
                if h == 0:
                    wait(pe, stack_in, 16 * LOADS * (bb + 1))
                ahead = isinstance(bb, int) and bb == 0 and h < LEAD
                wait(pe, s_read, HEADS * bb + h - ahead)
                wide(st_ps[0] if ahead and h % 2 else s_ps, lambda t: qs[0:SPLIT, par, h, t * KT:(t + 1) * KT], ks[0:SPLIT, par, h, :]).then_inc(s_ready, 1)

            def scores_t(bb, par, h):
                if h % 4 == 0:
                    wait(pe, mrow_in[h // 4], 16 * MROWS * (bb + 1))
                wait(pe, exp_done, PRE + HEADS * bb + h - 1)
                wide(st_ps[h % 2], lambda t: ks[:, par, h, t * KT:(t + 1) * KT], qs[:, par, h, :]).then_inc(st_ready, 1)

            def weigh(bb, par, g, t):
                if t == 0:
                    wait(pe, exp_done, PRE + HEADS * bb + 4 * g + 4)
                    if g == 0:
                        wait(pe, v_written, 3 * (bb + 1))
                    wait(pe, o_read, PRE + 4 * bb + g)
                for j in range(4):
                    h = 4 * g + j
                    last = mm(o_ps[32 * j:32 * j + 32, 0:TT], vv[:, par, t, h, :],
                              pt[:, h % 8, t * TT:(t + 1) * TT], t == 0, t == 2)
                if t == 2:
                    last.then_inc(pv_done, 1)

            def misc(use, prev):
                _, what, bb, n_ = use
                s_, v_ = read_of(prev)
                wait(pe, s_, v_)
                if what == "p":
                    for k in range(KC):
                        last = mm(m_ps[:, 0:TT], wqkv_t[:, k, n_ * P:(n_ + 1) * P], zt_b[:, k, bb, :], k == 0, k == KC - 1)
                    last.then_inc(proj_ready, 1)
                elif what == "v":
                    wait(pe, zb_ready, bb + 1)
                    for k in range(KC):
                        last = mm(m_ps[0:KT, 0:D], zb[:, k, n_ * KT:(n_ + 1) * KT], wqkv_t[:, k, 2 * D:3 * D], k == 0, k == KC - 1)
                    last.then_inc(v_ready, 1)
                else:
                    wait(pe, mp_ready, 4 * bb + n_ + 1)
                    dst = m_ps[0:12, :].bitcast(BF16)
                    for t in range(3):
                        last = pe.transpose(dst[:, t * KT:(t + 1) * KT],
                                            mpt[:, n_ % 2, t, :, :].rearrange("p r h -> p (r h)"), eyeb[0:KT, 0:KT])
                    last.then_inc(mt_ready, 1)

            def turn(b, par, kind):
                uses = misc_uses(b, kind)
                prev = before(b, kind)
                for j in range(HEADS):
                    if has_s_kind(kind, j):
                        bb, h = s_of(b, j)
                        scores(bb, par if j < LEAD else 1 - par, h)
                    if kind != "first":
                        scores_t(b, par, j)
                        if j % 4 > 0 and j > 4:
                            weigh(b, par, j // 4 - 1, j % 4 - 1)
                        elif j % 4 > 0 and has_before(b):
                            weigh(b - 1, 1 - par, 3, j % 4 - 1)
                    for use in uses:
                        if use[0] == j:
                            misc(use, prev)
                            prev = use

            pe.wait_ge(zt_done, 1)
            pe.wait_ge(setup_read, 3)
            pe.wait_ge(o_cleared, 1)
            for bb in range(2):
                for c in range(4):
                    for k in range(KC):
                        last = mm(bank[FIRST_BANKS[bb][c]][:, 0:TT], wqkv_t[:, k, c * P:(c + 1) * P], zt_b[:, k, bb, :],
                                  k == 0, k == KC - 1)
                    last.then_inc(proj_ready, 1)
            prev = (0, "p", 1, 3)
            for t in range(3):
                use = (0, "v", 0, t)
                misc(use, prev)
                prev = use
            setup_out()
            pe.wait_ge(init_done, INIT)
            pe.wait_ge(qs_cleared, 2)
            pe.sem_inc(pv_done, PRE)
            all_turns(pe, turn)
            for t in range(3):
                weigh(B - 1, 1, 3, t)

            def out_project(w, k, slot, p):
                wait(pe, oa_ready, w + 1)
                wait(pe, h1_ready, w - 1)
                for g2 in range(4):
                    last = mm(bank[k][0:p, 0:D], oa[:, slot, g2, 0:p], wo_t[:, g2, :], g2 == 0, g2 == 3)
                last.then_inc(op_ready, 1)

            def turn_xn(w, par, slot, p):
                wait(pe, xn_ready, w + 1)
                for k in range(KC):
                    last = pe.transpose(bank[2 + par][:, k * p:(k + 1) * p], xn[0:p, slot, k * P:(k + 1) * P], eye[0:p, 0:p])
                last.then_inc(xn_turned, 1)

            def logits(w, par, p=P):
                wait(pe, xnt_ready, w + 1)
                wait(pe, lg_read, PRE + w - 1)
                for k in range(KC):
                    last = mm(bank[4 + par][0:p, 0:E], xnt[:, par, k, 0:p], r_t[:, k, :], k == 0, k == KC - 1)
                last.then_inc(lg_ready, 1)

            def norms_step(s, q):
                for k in range(2):
                    w = 2 * s + k
                    if some(w - 6, TILES + 1):
                        turn_xn(w - 6, k, 2 * (1 - q) + k, rows(w - 6))
                    if some(w, TILES + 1):
                        out_project(w, k, 2 * q + k, rows(w))
                for k in range(2):
                    if some(2 * s + k - 6, TILES + 1):
                        logits(2 * s + k - 6, k, rows(2 * s + k - 6))

            pe.wait_ge(norm_done, PRE + 4 * B)
            all_steps(pe, norms_step)

            pe.wait_ge(mask_ready, 1)
            flat = mask[:, :, :].rearrange("p t e -> p (t e)")
            mm(bank[0][:, 0:17 * E], trib[:, :], flat, True, True).then_inc(rank_ready, 1)
            mm(bank[1][:, 0:17 * E], onesb[:, :], flat, True, True).then_inc(rank_ready, 1)
            for c in range(34):
                for n, (c0, _) in enumerate(OH_CUTS):
                    if c == c0:
                        pe.wait_ge(oh_ready, n + 1)
                if c % 17 == 0:
                    pe.wait_ge(wv_ready, 3 * (c // 17 + 1))
                last = mm(bank[2][:, 0:6 * SLOTS], ohp[:, c, :], vals[:, c, :, :].rearrange("p v s -> p (v s)"), c == 0, c == 33)
            last.then_inc(list_ready, 1)

            def turn_g(t, par):
                wait(pe, xg_in[par], 8 * (t - par) + 16)
                wait(pe, xgt_ready, t)
                for k in range(KC):
                    last = pe.transpose(bank[4][:, k * P:(k + 1) * P], xg[:, par, k * P:(k + 1) * P], eye[:, :])
                last.then_inc(x_turned, 1)

            def gemm1(t, par):
                wait(pe, xgt_ready, t + 1)
                wait(pe, w1_ready, KC * (t + 1))
                for half in range(2):
                    wait(pe, silu_done, 2 * t - 3 + half)
                    for c in range(4):
                        for k in range(KC):
                            f0 = (half * 4 + c) * P
                            last = mm(bank[2 * par + half][:, c * P:(c + 1) * P], w1c[:, par, k, f0:f0 + P],
                                      xgt[:, par, k, :], k == 0, k == KC - 1)
                    last.then_inc(g1_ready, 1)

            def gemm2(t, par, e):
                wait(pe, y_ready, t - 1)
                for c in range(F // P):
                    if c % 4 == 0:
                        wait(pe, silu_done, 2 * t + c // 4 + 1)
                    last = mm(bank[5 + par][:, 0:D], ht[:, par, c, :], w2_sb[:, e, c, :], c == 0, c == F // P - 1)
                last.then_inc(g2_ready, 1)

            def expert(t):
                return pe.value_load(eid[0:1, bass.ds(t, 1)], min_val=0, max_val=E - 1)

            pe.wait_ge(route_done, 1)
            pe.wait_ge(w_early_in, 16 * len(EARLY))
            pe.wait_ge(w_late_in, 16 * (2 * E - len(EARLY)))
            turn_g(0, 0)
            gemm1(0, 0)
            turn_g(1, 1)

            def tile(t, par, more):
                e_before = expert(t - 1)
                gemm1(t, par)
                if more:
                    turn_g(t + 1, 1 - par)
                gemm2(t - 1, 1 - par, e_before)

            tile_pairs(pe, 1, SLOTS - 1, lambda t, par: tile(t, par, True))
            tile(SLOTS - 1, 1, False)
            gemm2(SLOTS - 1, 1, expert(SLOTS - 1))


def kernel(x, cls_tok, L0_tok_W, L0_tok_gamma, L0_attn_w_qkv, L0_attn_w_out, L0_attn_b_out, L0_ffn_gamma,
           L0_ffn_beta, L0_ffn_router_w, L0_ffn_W1, L0_ffn_W2):
    import concourse.bacc as _bacc
    from concourse.bass_utils import run_bass_kernel_spmd as _run

    data = dict(x=x, cls_tok=cls_tok, tok_w=L0_tok_W, tok_gamma=L0_tok_gamma, w_qkv=L0_attn_w_qkv,
                w_out=L0_attn_w_out, b_out=L0_attn_b_out, f_gamma=L0_ffn_gamma, f_beta=L0_ffn_beta,
                router_w=L0_ffn_router_w, w1=L0_ffn_W1, w2=L0_ffn_W2)
    data = {k: np.ascontiguousarray(v) for k, v in data.items()}
    data.update(zip(("cos_in", "sin_in", "eye_in", "tri_in", "tab_in"), shape_tables()))
    nc = _bacc.Bacc("TRN2", target_bir_lowering=False, num_devices=1)
    args = {k: nc.dram_tensor(k, v.shape, mybir.dt.from_np(v.dtype), kind="ExternalInput").ap() for k, v in data.items()}
    args["out"] = nc.dram_tensor("out", (ROWS + P, D), F32, kind="ExternalOutput").ap()
    vit_block(nc, **args)
    r = _run(nc, [data], core_ids=[0])
    return r.results[0]["out"][0:ROWS].reshape(B, NTOK, D)
```
